# Optimizing a Trainium2 kernel written in Bass

```python
import numpy as np
import jax
import jax.numpy as jnp

def _softmax(x, axis=-1):
    return jax.nn.softmax(x, axis=axis)

def _gelu(x):
    return jax.nn.gelu(x, approximate=True)

def _silu(x):
    return jax.nn.silu(x)

def _sigmoid(x):
    return jax.nn.sigmoid(x)

def _layernorm(x, axis=-1, eps=1e-05):
    m = jnp.mean(x, axis=axis, keepdims=True)
    v = jnp.var(x, axis=axis, keepdims=True)
    return (x - m) / jnp.sqrt(v + eps)

def _scatter_add(tgt, idx, src, axis=0):
    return tgt.at[idx].add(src)

def _segment_sum(src, seg, n):
    return jax.ops.segment_sum(src, seg, n)
kernel_name = 'mk_gnn_resnorm_d4_gnn_r64_a06242'

def setup_inputs(seed: int=0):
    np.random.seed(seed)
    _w = jnp.asarray

    def _rec_inputs():
        import jax
        import jax.numpy as jnp
        _gk = jax.random.key(seed)
        x = -0.0001006 + 1 * jax.random.normal(jax.random.fold_in(_gk, 1), (100000, 96), jnp.float32)
        src = jax.random.randint(jax.random.fold_in(_gk, 2), (25000,), 0, 100000, jnp.int32)
        dst = jax.random.randint(jax.random.fold_in(_gk, 3), (25000,), 0, 100000, jnp.int32)
        _o = jnp.argsort(dst, stable=True)
        src = src[_o]
        dst = dst[_o]
        return (x, src, dst)
    x, src, dst = _rec_inputs()

    def _L0_gnn_setup():
        import jax, jax.numpy as jnp
        import numpy as np
        N_NODES = 50000
        N_EDGES = 12500
        D_IN = 96
        D_OUT = 96
        K_HOPS = 4
        key = jax.random.key(seed)
        k1, k2, k3, k4, k5 = jax.random.split(key, 5)
        x = jax.random.normal(k1, (N_NODES, D_IN), dtype=jnp.float32)
        row = jax.random.randint(k2, (N_EDGES,), 0, N_NODES)
        col = jax.random.randint(k3, (N_EDGES,), 0, N_NODES)
        edge_index = jnp.stack([row, col], axis=0).astype(jnp.int64)
        bound = 1.0 / np.sqrt(K_HOPS * D_IN)
        weight = jax.random.uniform(k4, (K_HOPS, D_IN, D_OUT), dtype=jnp.float32, minval=-bound, maxval=bound)
        bias = jax.random.uniform(k5, (D_OUT,), dtype=jnp.float32, minval=-bound, maxval=bound)
        return {'x': x, 'edge_index': edge_index, 'weight': weight, 'bias': bias}
    _L0_gnn_all = _L0_gnn_setup()
    _L0_gnn_in = {k: v for k, v in _L0_gnn_all.items() if k in ('weight', 'bias')}
    del _L0_gnn_all

    def _L1_gnn_setup():
        import jax, jax.numpy as jnp
        import numpy as np
        N_NODES = 50000
        N_EDGES = 12500
        D = 96
        DEPTH = 2
        key = jax.random.key(seed)
        ks = jax.random.split(key, 8)
        scale = 1.0 / np.sqrt(D)
        x = jax.random.normal(ks[0], (N_NODES, D), dtype=jnp.float32)
        W0 = jax.random.normal(ks[1], (DEPTH, D, D), dtype=jnp.float32) * scale
        b0 = jnp.zeros((DEPTH, D), dtype=jnp.float32)
        W1 = jax.random.normal(ks[2], (DEPTH, D, D), dtype=jnp.float32) * scale
        b1 = jnp.zeros((DEPTH, D), dtype=jnp.float32)
        W2 = jax.random.normal(ks[3], (DEPTH, 2 * D, D), dtype=jnp.float32) * (1.0 / np.sqrt(2 * D))
        b2 = jnp.zeros((DEPTH, D), dtype=jnp.float32)
        edge_src = jax.random.randint(ks[4], (N_EDGES,), 0, N_NODES, dtype=jnp.int64 if jax.config.jax_enable_x64 else jnp.int32)
        edge_dst = jnp.sort(jax.random.randint(ks[5], (N_EDGES,), 0, N_NODES, dtype=jnp.int64 if jax.config.jax_enable_x64 else jnp.int32))
        return {'x': x, 'W0': W0, 'b0': b0, 'W1': W1, 'b1': b1, 'W2': W2, 'b2': b2, 'edge_src': edge_src, 'edge_dst': edge_dst}
    _L1_gnn_all = _L1_gnn_setup()
    _L1_gnn_in = {k: v for k, v in _L1_gnn_all.items() if k in ('W0', 'b0', 'W1', 'b1', 'W2', 'b2')}
    del _L1_gnn_all

    def _L2_gnn_setup():
        import jax, jax.numpy as jnp
        import numpy as np
        N_NODES = 50000
        N_EDGES = 12500
        D_IN = 96
        D_OUT = 96
        key = jax.random.key(seed)
        k1, k2, k3, k4 = jax.random.split(key, 4)
        x = jax.random.normal(k1, (N_NODES, D_IN), dtype=jnp.float32)
        edge_index = jax.random.randint(k2, (2, N_EDGES), 0, N_NODES, dtype=jnp.int64)
        W = jax.random.normal(k3, (D_IN, D_OUT), dtype=jnp.float32) * (1.0 / np.sqrt(D_IN))
        b = jax.random.normal(k4, (D_OUT,), dtype=jnp.float32) * 0.01
        return {'x': x, 'edge_index': edge_index, 'W': W, 'b': b}
    _L2_gnn_all = _L2_gnn_setup()
    _L2_gnn_in = {k: v for k, v in _L2_gnn_all.items() if k in ('W', 'b')}
    del _L2_gnn_all

    def _L3_gnn_setup():
        import jax, jax.numpy as jnp
        import numpy as np
        EPS = 1e-07
        BETA = 1.0
        key = jax.random.key(seed)
        k1, k2, k3, k4 = jax.random.split(key, 4)
        N, E, D_IN, D_OUT = (50000, 12500, 96, 96)
        feat = jax.random.normal(k1, (N, D_IN), dtype=jnp.float32)
        src = jax.random.randint(k2, (E,), 0, N, dtype=jnp.int32)
        dst = jax.random.randint(k3, (E,), 0, N, dtype=jnp.int32)
        W = jax.random.normal(k4, (D_IN, D_OUT), dtype=jnp.float32) / np.sqrt(D_IN)
        b = jnp.zeros((D_OUT,), dtype=jnp.float32)
        return {'feat': feat, 'src': src, 'dst': dst, 'W': W, 'b': b}
    _L3_gnn_all = _L3_gnn_setup()
    _L3_gnn_in = {k: v for k, v in _L3_gnn_all.items() if k in ('W', 'b')}
    del _L3_gnn_all
    return {'x': x, 'src': src, 'dst': dst, 'L0_gnn_weight': _L0_gnn_in['weight'], 'L0_gnn_bias': _L0_gnn_in['bias'], 'L1_gnn_W0': _L1_gnn_in['W0'], 'L1_gnn_b0': _L1_gnn_in['b0'], 'L1_gnn_W1': _L1_gnn_in['W1'], 'L1_gnn_b1': _L1_gnn_in['b1'], 'L1_gnn_W2': _L1_gnn_in['W2'], 'L1_gnn_b2': _L1_gnn_in['b2'], 'L2_gnn_W': _L2_gnn_in['W'], 'L2_gnn_b': _L2_gnn_in['b'], 'L3_gnn_W': _L3_gnn_in['W'], 'L3_gnn_b': _L3_gnn_in['b']}

def reference(x, src, dst, L0_gnn_weight, L0_gnn_bias, L1_gnn_W0, L1_gnn_b0, L1_gnn_W1, L1_gnn_b1, L1_gnn_W2, L1_gnn_b2, L2_gnn_W, L2_gnn_b, L3_gnn_W, L3_gnn_b):
    import jax
    import jax.numpy as jnp

    def _L0_gnn_ref(x, edge_index, weight, bias):
        import jax, jax.numpy as jnp
        import numpy as np
        N_NODES = 50000
        N_EDGES = 12500
        D_IN = 96
        D_OUT = 96
        K_HOPS = 4
        row, col = (edge_index[0], edge_index[1])
        n = x.shape[0]
        ew = jnp.ones((row.shape[0],), dtype=x.dtype)
        deg = jax.ops.segment_sum(ew, row, num_segments=n)
        dinv = jnp.where(deg > 0, jax.lax.rsqrt(jnp.maximum(deg, 1e-12)), 0.0)
        norm = -dinv[row] * ew * dinv[col]

        def prop(h):
            return jax.ops.segment_sum(norm[:, None] * h[col], row, num_segments=n)
        k_hops = weight.shape[0]
        tx0 = x
        out = tx0 @ weight[0]
        tx1 = prop(x)
        out = out + tx1 @ weight[1]
        for k in range(2, k_hops):
            tx2 = 2.0 * prop(tx1) - tx0
            out = out + tx2 @ weight[k]
            tx0, tx1 = (tx1, tx2)
        return out + bias

    def _L1_gnn_ref(x, W0, b0, W1, b1, W2, b2, edge_src, edge_dst):
        import jax, jax.numpy as jnp
        import numpy as np
        N_NODES = 50000
        N_EDGES = 12500
        D = 96
        DEPTH = 2
        n = x.shape[0]
        depth = W0.shape[0]
        for i in range(depth):
            h_self = x @ W1[i] + b1[i]
            h_nb = x @ W0[i] + b0[i]
            agg = jax.ops.segment_sum(h_nb[edge_src], edge_dst, num_segments=n)
            x = jnp.concatenate([h_self, agg], axis=-1) @ W2[i] + b2[i]
            x = x / jnp.std(x, axis=-1, ddof=1, keepdims=True)
        return x

    def _L2_gnn_ref(x, edge_index, W, b):
        import jax, jax.numpy as jnp
        import numpy as np
        N_NODES = 50000
        N_EDGES = 12500
        D_IN = 96
        D_OUT = 96
        num_nodes = x.shape[0]
        src, dst = (edge_index[0], edge_index[1])
        messages = x[src] @ W + b
        out = jax.ops.segment_sum(messages, dst, num_segments=num_nodes)
        deg = jax.ops.segment_sum(jnp.ones((dst.shape[0],), dtype=x.dtype), dst, num_segments=num_nodes)
        deg = jnp.clip(deg, 1.0, None)
        return out / deg[:, None]

    def _L3_gnn_ref(feat, src, dst, W, b):
        import jax, jax.numpy as jnp
        import numpy as np
        EPS = 1e-07
        BETA = 1.0
        N = feat.shape[0]
        m = jax.nn.relu(feat[src]) + EPS
        logits = BETA * m
        seg_max = jax.ops.segment_max(logits, dst, num_segments=N)
        ex = jnp.exp(logits - seg_max[dst])
        denom = jax.ops.segment_sum(ex, dst, num_segments=N)
        a = ex / denom[dst]
        msg = jax.ops.segment_sum(a * m, dst, num_segments=N)
        feats = feat + msg
        return feats @ W + b
    edge_index = jnp.stack([src, dst])
    x = _layernorm(x + _L0_gnn_ref(x, edge_index, L0_gnn_weight, L0_gnn_bias), axis=-1)
    x = _layernorm(x + _L1_gnn_ref(x, L1_gnn_W0, L1_gnn_b0, L1_gnn_W1, L1_gnn_b1, L1_gnn_W2, L1_gnn_b2, src, dst), axis=-1)
    x = _layernorm(x + _L2_gnn_ref(x, edge_index, L2_gnn_W, L2_gnn_b), axis=-1)
    x = _layernorm(x + _L3_gnn_ref(x, src, dst, L3_gnn_W, L3_gnn_b), axis=-1)
    return x

_drawn_inputs = setup_inputs


def setup_inputs(seed=0):
    import zlib

    import numpy as np

    out = dict(_drawn_inputs(seed))
    spreads = {'L1_gnn_b0': (0.0, 0.327),
     'L1_gnn_b1': (0.0, 0.1),
     'L1_gnn_b2': (0.0, 0.1),
     'L3_gnn_b': (0.0, 0.1)}
    factors = {'L2_gnn_b': 8.0}
    for name, (base, spread) in spreads.items():
        noise = np.random.default_rng([zlib.crc32(name.encode()), seed]).standard_normal(out[name].shape)
        drawn = base * np.exp(spread * noise) if base else spread * noise
        out[name] = jnp.asarray(drawn.astype(out[name].dtype))
    for name, factor in factors.items():
        out[name] = (out[name] * factor).astype(out[name].dtype)
    return out
```

```python
import numpy as np
import concourse.bass as bass
from concourse import mybir
from contextlib import ExitStack

F32 = mybir.dt.float32
I32 = mybir.dt.int32
ALU = mybir.AluOpType
ACT = mybir.ActivationFunctionType
AX = mybir.AxisListType

P = 128
N, D, E = 100000, 96, 25000
D1 = D + 1
SORT = 32768
SORT_BITS = 15
SORT_COLS = SORT // P
TILES = -(-E // P)
EP = TILES * P
W = 7
GROUPS = TILES // W
PAIRS = GROUPS // 2
GE = W * P
NONE_ROW = EP
FAR = float(1 << 20)
DP, DT = 125, 8
DROWS = DP * DT
CREDIT = 16
LN_EPS = 1e-5
MSG_EPS = 1e-7


class Steps:

    def __init__(self, sem, start, names, unit=1):
        self.sem, self.start, self.names, self.unit = sem, start, names, unit
        self.n = 0

    def at(self, i, name, back=0):
        k = self.start + (self.names.index(name) + 1 - back * len(self.names)) * self.unit
        return i * (len(self.names) * self.unit) + k

    def done(self, instruction, name):
        assert self.names[self.n % len(self.names)] == name, (name, self.names[self.n % len(self.names)])
        self.n += 1
        return instruction.then_inc(self.sem, self.unit)

    def end(self, rounds):
        return self.start + rounds * len(self.names) * self.unit


def weave(*programs):
    programs = list(programs)
    while programs:
        for p in list(programs):
            try:
                next(p)
            except StopIteration:
                programs.remove(p)


def gnn_program(nc, x, src, dst, cheb_w, cheb_b, sage_w0, sage_b0, sage_w1, sage_b1, sage_w2, sage_b2,
                mean_w, mean_b, soft_w, soft_b, out):
    ctx = ExitStack()
    with ctx:
        def sb(name, shape, dt=F32):
            return ctx.enter_context(nc.sbuf_tensor(name, shape, dt))

        def sem(name):
            return ctx.enter_context(nc.semaphore(name))

        def dram(name, shape):
            return nc.dram_tensor(name, shape, F32, kind="Internal").ap()

        x1_d = dram("x1_table", [N, D])
        sorted_d = dram("sorted_keys", [2, SORT + 2])
        cont_d = dram("segment_goes_on", [2, SORT])
        map_d = [dram(f"node_map{s}", [N, 2]) for s in range(2)]
        u_d = [dram(f"u_table{k}", [EP + 1, D]) for k in range(2)]
        sT_d = [dram(f"cheb_sums{k}", [D, EP]) for k in range(2)]
        agg_d = [dram(f"agg_table{k}", [EP + 1, D]) for k in range(3)]
        r_d = [dram(f"src_rows{k}", [GROUPS, P, W * D]) for k in range(3)]
        t_d = [dram(f"dst_rows{k}", [GROUPS, P, W * D]) for k in range(4)]

        ident = sb("ident", [P, P])
        zrow = sb("zrow", [1, D])
        neg = sb("neg", [1, 1])
        one = sb("one", [1, 1])
        eps = sb("eps", [P, 1])
        eps2 = sb("eps2", [P, 1])
        ones = sb("ones", [P, P])
        pos_i = sb("pos_i", [P, SORT_COLS], I32)
        chebw = sb("chebw", [D, 4, D])
        w1b1 = sb("w1b1", [D1, 2, D])
        w0b0 = sb("w0b0", [D1, 2, D])
        w2top = sb("w2top", [D, 2, D])
        w2bot = sb("w2bot", [D, 2, D])
        b2row = sb("b2row", [D1, 2, D])
        wT = sb("wT", [D, 4, D1])
        wt = sb("wt", [D1, 11, D])
        wmean = sb("wmean", [D1, 9])
        A0, B1, B2, B3, SELF1, NB1, MEANW, SOFTI, SOFTW, SELF0, NB0 = range(11)

        scat_i = sb("scat_i", [P, 2, SORT_COLS], I32)
        pay_i = sb("pay_i", [P, 2, SORT_COLS], I32)
        key_i = sb("key_i", [P, 2, SORT_COLS], I32)
        mapv = sb("mapv", [P, 2, SORT_COLS, 2])
        found = sb("found", [P, 2, TILES, 2])
        found_i = sb("found_i", [P, 2, TILES], I32)
        ndinv = sb("ndinv", [P, SORT_COLS])
        nrc = sb("nrc", [P, SORT_COLS])
        rcb = sb("rcb", [P, SORT_COLS])
        in_i = pay_i
        cnt_row = sb("cnt_row", [1, 2, SORT_COLS + 1])
        cnt_in = sb("cnt_in", [1, 4 * SORT_COLS])
        cnt_col = sb("cnt_col", [P, 4])

        DS = 4
        dX = [sb(f"dX{s}", [DP, DT * D]) for s in range(DS)]
        dXT = [sb(f"dXT{s}", [D1, DROWS]) for s in range(DS)]
        dSQ = [sb(f"dSQ{s}", [DP, DT * D]) for s in range(DS)]
        dH = [sb(f"dH{s}", [DP, DT * D]) for s in range(DS)]
        dst6 = [sb(f"dst6{s}", [DP, DT, 6]) for s in range(DS)]
        dsm = [sb(f"dsm{s}", [DP, 4, DT]) for s in range(DS)]

        def pair(name, shape, dt=F32):
            return [sb(f"{name}{b}", shape, dt) for b in range(2)]

        idx_a = pair("idx_a", [P, W], I32)
        idx_b = pair("idx_b", [P, W], I32)
        idx_s = pair("idx_s", [P, W], I32)
        mrow = pair("mrow", [P, W, 2])
        GB = pair("GB", [P, W, D])
        RB = pair("RB", [P, W, D1])
        TB = pair("TB", [P, W, D])
        TH = pair("TH", [P, W, D])
        RH = pair("RH", [P, W, D1])
        AR = pair("AR", [P, W, D])
        OR = pair("OR", [P, W, D])
        eH = [sb(f"eH{k}", [P, W, D]) for k in range(2)]
        eZ = [sb(f"eZ{k}", [P, W, D]) for k in range(2)]
        eSQ = [sb(f"eSQ{k}", [P, W, D]) for k in range(2)]
        est6 = [sb(f"est6{k}", [P, W, 6]) for k in range(2)]
        esm = [sb(f"esm{k}", [P, 4, W]) for k in range(2)]
        FL = pair("FL", [D1, GE])
        SC = pair("SC", [D1, GE])
        XT = [sb(f"XT{k}", [D1, GE]) for k in range(2)]
        MX = pair("MX", [P, GE + 1])
        DEN = pair("DEN", [P, GE])
        NUM = pair("NUM", [P, GE])
        MB = sb("MB", [P, GE])
        DEC = sb("DEC", [P, GE])
        EX = sb("EX", [P, GE])
        QQ = sb("QQ", [P, GE])
        MS = sb("MS", [P, GE])

        K = [DEN[0][:, 0:512], NUM[0][:, 0:512]]
        V = [DEN[1][:, 0:512], NUM[1][:, 0:512]]
        MASK = [MB[:, 0:512], DEC[:, 0:512]]
        DIF = EX[:, 0:512]
        KPREV, KNEXT, LOCAL, CPROD, CONT = QQ[:, 0:512], MS[:, 0:512], MX[0][:, 0:512], MX[1][:, 0:512], EX[:, 0:512]
        SIDX, CNT = MB[:, 0:512], DEC[:, 0:512]
        fill = TH[0][0:DP, :, :].rearrange("p w d -> p (w d)")[:, 0:320]

        PS = [ctx.enter_context(nc.psum_tensor(f"PS{k}", [P, 1024], F32)) for k in range(4)]

        def rows_of(ps, p, tiles):
            return ps[0:p, 0:tiles * P].rearrange("p (t c) -> p t c", c=P)[:, :, 0:D]

        loaded_w = sem("loaded_w")
        loaded_e = sem("loaded_e")
        pool_init = sem("pool_init")
        filled = sem("filled")
        prep_v = sem("prep_v")
        prep_pe = sem("prep_pe")
        sort_step = sem("sort_step")
        switch_ready = sem("switch_ready")
        switched = sem("switched")
        v_back = sem("v_back")
        keys_out = sem("keys_out")
        keys_in = sem("keys_in")
        post_pe = sem("post_pe")
        idx_ready = sem("idx_ready")
        map_out = sem("map_out")

        d1_ld = [Steps(sem(f"dense_loaded{s}"), 0, ["x"], 16) for s in range(DS)]
        d1_st = [Steps(sem(f"dense_stored{s}"), CREDIT, ["x1"], 16) for s in range(DS)]
        d1_pe = [Steps(sem(f"dense_pe{s}"), CREDIT, ["xT", "mm"]) for s in range(DS)]
        d1_act = [Steps(sem(f"dense_act{s}"), CREDIT, ["xT", "sq", "sd"]) for s in range(DS)]
        d1_v = [Steps(sem(f"dense_v{s}"), CREDIT, ["sum", "r", "x1"]) for s in range(DS)]
        D1N = N // DROWS // DS
        D2S = 2
        D2N = N // DROWS // D2S
        d2_ld = [Steps(d1_ld[s].sem, d1_ld[s].end(D1N), ["x1"], 16) for s in range(D2S)]
        d2_st = [Steps(d1_st[s].sem, d1_st[s].end(D1N), ["out"], 16) for s in range(D2S)]
        d2_pe = [Steps(d1_pe[s].sem, d1_pe[s].end(D1N), ["x1T", "mm0", "h1T", "mm1", "x3T", "mm3"]) for s in range(D2S)]
        d2_act = [Steps(d1_act[s].sem, d1_act[s].end(D1N), ["x1T", "sd1", "h1T", "sq2", "sd2", "sqz", "sdz", "x3T", "sqo", "sdo"]) for s in range(D2S)]
        d2_v = [Steps(d1_v[s].sem, d1_v[s].end(D1N),
                      ["bn", "dm", "dm2", "m2", "m2s", "r1", "h1", "sum2", "r2", "h2", "z",
                       "sumz", "rz", "x3", "sumo", "ro", "out"]) for s in range(D2S)]

        x_v = x.rearrange("(g p i) d -> g p (i d)", p=DP, i=DT)
        x1_v = x1_d.rearrange("(g p i) d -> g p (i d)", p=DP, i=DT)
        out_v = out.rearrange("(g p i) d -> g p (i d)", p=DP, i=DT)

        def group(view, g):
            v = view[bass.ds(g, 1)]
            return v.rearrange("g p f -> (g p) f")

        def by8(t):
            return t[:, :].rearrange("p (t d) -> p t d", d=D)

        def spread(scale, tiles, p=P):
            return scale.unsqueeze(2).to_broadcast([p, tiles, D])

        dma_sems = {k: [sem(f"{k}_dma{b}") for b in range(2)] for k in ("ga", "gb", "fl", "ld", "st", "sc")}
        step_sems = {k: sem(f"{k}_steps") for k in ("idx", "sidx", "rpe", "ract", "rv", "tpe", "tact", "tv")}
        pool_dmas = ("ga", "gb", "sc")
        reached = {k: 0 if k in pool_dmas else CREDIT for k in (*dma_sems, *step_sems)}

        class Round:
            def __init__(self, **lists):
                self.steps, self.dmas = {}, {}
                for k in step_sems:
                    self.steps[k] = Steps(step_sems[k], reached[k], lists.get(k, []))
                    reached[k] = self.steps[k].end(GROUPS)
                for k in dma_sems:
                    unit = 16 * (lists.get(k, 0))
                    self.dmas[k] = [Steps(q, reached[k], ["all"] if unit else [], unit) for q in dma_sems[k]]
                    reached[k] = self.dmas[k][0].end(PAIRS)
                self.idx, self.sidx, self.rpe, self.ract = (self.steps[k] for k in ("idx", "sidx", "rpe", "ract"))
                self.rv, self.tpe, self.tact, self.tv = (self.steps[k] for k in ("rv", "tpe", "tact", "tv"))
                self.ga, self.gb, self.sc = (self.dmas[k] for k in ("ga", "gb", "sc"))
                self.fl, self.ld, self.st = (self.dmas[k] for k in ("fl", "ld", "st"))

        map_put = [Round(idx=["a", "row"], sc=W) for side in range(2)]
        map_get = [Round(idx=["a"], ga=W), Round(idx=["a"], gb=W)]
        BN = ["bn", "dm", "dm2", "m2", "m2s", "r"]
        cheb = [
            Round(idx=["a"], ga=W, fl=1, st=2, rpe=["zT", "back"], rv=["scaled", "scan", "u"]),
            Round(idx=["a"], ga=W, fl=1, st=2, rpe=["zT", "back"], rv=["scan", "u"]),
            Round(idx=["a", "b"], sidx=["s"], ga=W, gb=W, fl=1, ld=2, sc=W, rpe=["zT", "mix", "xT", "self"],
                  ract=["xT", "sq", "sd"], rv=["scan", "y", "pre", "sum", "r", "x1"]),
        ]
        sage1 = Round(idx=["a", "b"], ga=W, gb=W, fl=1, st=4, rpe=["rT", "agg"], ract=["agg"], rv=["scan"],
                      tpe=["tT", "self"], tact=["tT", "sd"], tv=["h", *BN, "h1"])
        sage2 = Round(idx=["a"], ga=W, fl=1, ld=3, st=3, rpe=["rT", "self", "h1T", "agg"], ract=["rT", "sd", "agg"],
                      rv=["h", *BN, "h1", "scan"], tpe=["tT", "self"], tact=["tT", "sq", "sd", "sqz", "sdz"],
                      tv=["h", "sum", "r", "h2", "z", "sumz", "rz", "x2"])
        meanr = Round(idx=["a"], ga=W, fl=1, ld=3, st=3, rpe=["rT", "self", "x2T", "agg"], ract=["rT", "sq", "sd", "sqz", "sdz"],
                      rv=["h", "sum", "r", "h2", "z", "sumz", "rz", "x2", "scan", "agg"],
                      tact=["sqz", "sdz"], tv=["z", "sumz", "rz", "x3"])
        softr = Round(idx=["a"], sidx=["s"], ga=W, fl=1, ld=2, sc=W, rpe=["x3T"], ract=["sqz", "sdz", "dec", "ex"],
                      rv=["z", "sumz", "rz", "x3", "m", "carry", "max", "kept", "less", "off", "dec", "q",
                          "den", "num", "rec", "msg"],
                      tpe=["tT", "out"], tact=["tT", "sqo", "sdo"], tv=["sumo", "ro", "out"])

        x_v = x.rearrange("(g p i) d -> g p (i d)", p=DP, i=DT)
        x1_v = x1_d.rearrange("(g p i) d -> g p (i d)", p=DP, i=DT)
        out_v = out.rearrange("(g p i) d -> g p (i d)", p=DP, i=DT)

        def group(view, g):
            return view[bass.ds(g, 1)].rearrange("g p f -> (g p) f")

        def table_group(table, g):
            v = table[0:EP].rearrange("(g i p) d -> g p i d", p=P, i=W)
            return v[bass.ds(g, 1)].rearrange("g p i d -> (g p) i d")

        def by_tile(t):
            return t[:, :].rearrange("p (t d) -> p t d", d=D)

        def spread(scale, p, tiles):
            return scale.unsqueeze(2).to_broadcast([p, tiles, D])

        def on(eng, steps, i, name, back=0):
            eng.wait_ge(steps.sem, steps.at(i, name, back))

        def all_on(eng, steps, i, back=0):
            eng.wait_ge(steps.sem, steps.at(i, steps.names[-1], back))

        def finished(eng, r):
            for steps in r.steps.values():
                if steps.names:
                    eng.wait_ge(steps.sem, steps.end(GROUPS))
            for made in r.dmas.values():
                for q in made:
                    if q.names:
                        eng.wait_ge(q.sem, q.end(PAIRS))

        found_ready = sem("found_ready")
        MAP_Q = 160
        FILLS = 5 + 2 * (N // DP // MAP_Q) + 4
        SORTED = SORT_BITS * (SORT_BITS + 1) // 2 % 2
        POOL_INITS = 9
        WEIGHT_LOADS = 8 + 6
        post_v = sem("post_v")
        roots = sem("roots")
        held = sem("held")

        block = ctx.enter_context(nc.Block())

        @block.sync
        def _(sp):
            for q in (*dma_sems["fl"], *dma_sems["ld"], *dma_sems["st"], *(r.sem for r in d1_st)):
                sp.sem_inc(q, CREDIT)
            sp.wait_ge(pool_init, 2)
            full, rest = E // P, E % P
            for side, (k, v) in enumerate(((src, dst), (dst, src))):
                for t, a in ((key_i, k), (pay_i, v)):
                    rows = a[0:full * P].rearrange("(r p) -> r p", p=P)
                    sp.dma_start(t[:, side, 0:P], rows[0:P, :]).then_inc(loaded_e, 16)
                    sp.dma_start(t[0:full - P, side, P:2 * P], rows[P:full, :]).then_inc(loaded_e, 16)
                    sp.dma_start(t[full - P:full - P + 1, side, P:P + rest],
                                 a[full * P:E].rearrange("(o p) -> o p", o=1)).then_inc(loaded_e, 16)
            for t, a in ((chebw, cheb_w.rearrange("k i o -> i k o")),
                         (w1b1[0:D], sage_w1.rearrange("k i o -> i k o")),
                         (w0b0[0:D], sage_w0.rearrange("k i o -> i k o")),
                         (w2top, sage_w2[:, 0:D, :].rearrange("k i o -> i k o")),
                         (w2bot, sage_w2[:, D:2 * D, :].rearrange("k i o -> i k o"))):
                sp.dma_start(t[:], a).then_inc(loaded_w, 16)
            for t, a in ((w1b1, sage_b1), (w0b0, sage_b0), (b2row, sage_b2)):
                sp.dma_start(t[D:D1], a.rearrange("(o k) f -> o k f", o=1)).then_inc(loaded_w, 16)
            sp.wait_ge(pool_init, 3)
            for n, w, b in ((MEANW, mean_w, mean_b), (SOFTI, soft_w, soft_b), (SOFTW, soft_w, None), (A0, None, cheb_b)):
                if w is not None:
                    sp.dma_start(wt[0:D, n, :], w).then_inc(loaded_w, 16)
                if b is not None:
                    sp.dma_start(wt[D:D1, n, :], b.rearrange("(o f) -> o f", o=1)).then_inc(loaded_w, 16)
            sp.wait_ge(pool_init, 6)
            for table in (*u_d, *agg_d):
                sp.dma_start(table[NONE_ROW:NONE_ROW + 1, :], zrow[:]).then_inc(filled, 16)
            for m in map_d:
                mv = m.rearrange("(c p q) t -> c p (q t)", p=DP, q=MAP_Q)
                for c in range(mv.shape[0]):
                    sp.dma_start(mv[c], fill).then_inc(filled, 16)
            for side in range(2):
                for at in (0, SORT + 1):
                    sp.dma_start(sorted_d[side:side + 1, at:at + 1], neg[:]).then_inc(filled, 16)
            shifted = lambda side, o: sorted_d[side, o:o + SORT].rearrange("(h q p) -> q h p", h=2, p=P)
            sp.wait_ge(keys_out, 1)
            sp.wait_ge(filled, 16 * FILLS)
            for side in range(2):
                sp.dma_start(shifted(side, 1), K[SORTED][:, side * 256:side * 256 + 256]
                             .rearrange("q (h p) -> q h p", h=2)).then_inc(keys_in, 16)
            sp.wait_ge(keys_in, 32)
            for side in range(2):
                for o, t in ((0, KPREV), (2, KNEXT)):
                    sp.dma_start(t[:, side * 256:side * 256 + 256].rearrange("q (h p) -> q h p", h=2),
                                 shifted(side, o)).then_inc(keys_in, 16)
            sp.wait_ge(keys_out, 2)
            for side in range(2):
                sp.dma_start(cont_d[side].rearrange("(h q p) -> q h p", h=2, p=P),
                             CONT[:, side * 256:side * 256 + 256].rearrange("q (h p) -> q h p", h=2)).then_inc(keys_in, 16)
            sp.wait_ge(keys_in, 16 * 8)

            def d1_load(i, s):
                on(sp, d1_pe[s], i, "xT", back=1)
                sp.dma_start(dX[s][:], group(x_v, i * DS + s)).then_inc(d1_ld[s].sem, 16)

            def d1_store(i, s):
                on(sp, d1_v[s], i, "x1")
                sp.dma_start(group(x1_v, i * DS + s), dH[s][:]).then_inc(d1_st[s].sem, 16)

            for s in range(DS):
                sp.dma_start(dX[s][:], x_v[s]).then_inc(d1_ld[s].sem, 16)
            with sp.Fori(0, D1N - 1) as i:
                for s in range(DS):
                    d1_load(i + 1, s)
                for s in range(DS):
                    d1_store(i, s)
            for s in range(DS):
                d1_store(D1N - 1, s)

            def flags(r, side, g, b, reader, name, i):
                if i is not None:
                    on(sp, reader, g, name, back=2)
                sp.dma_start(FL[b][:], cont_d[side:side + 1, bass.ds(g * GE, GE)].to_broadcast([D1, GE])).then_inc(r.fl[b].sem, 16)

            def rounds(load, store):
                load(0, 0, None)
                load(1, 1, None)
                with sp.Fori(0, PAIRS - 1) as i:
                    for b in range(2):
                        store(i * 2 + b, b, i)
                        load(i * 2 + (b + 2), b, i)
                for b in range(2):
                    store(GROUPS - 2 + b, b, PAIRS - 1)

            for k, r in enumerate(cheb[:2]):
                def load(g, b, i, r=r):
                    flags(r, 0, g, b, r.rv, "scan", i)

                def store(g, b, i, r=r, k=k):
                    on(sp, r.rv, g, "scan")
                    sp.dma_start(sT_d[k][:, bass.ds(g * GE, GE)], SC[b][0:D, :]).then_inc(r.st[b].sem, 16)
                    on(sp, r.rv, g, "u")
                    sp.dma_start(table_group(u_d[k], g), OR[b][:]).then_inc(r.st[b].sem, 16)
                rounds(load, store)
                finished(sp, r)
            r = cheb[2]

            def load(g, b, i, r=r):
                flags(r, 0, g, b, r.rv, "scan", i)
                if i is not None:
                    on(sp, r.rpe, g, "mix", back=2)
                for k, t in enumerate((DEN, NUM)):
                    sp.dma_start(t[b][0:D, :], sT_d[k][:, bass.ds(g * GE, GE)]).then_inc(r.ld[b].sem, 16)
            rounds(load, lambda g, b, i: None)

            finished(sp, r)

            def d2_load(i, s):
                on(sp, d2_v[s], i, "z", back=1)
                sp.dma_start(dX[s][:], group(x1_v, i * D2S + s)).then_inc(d2_ld[s].sem, 16)

            def d2_store(i, s):
                on(sp, d2_v[s], i, "out")
                sp.dma_start(group(out_v, i * D2S + s), dX[s + 2][:]).then_inc(d2_st[s].sem, 16)

            for s in range(D2S):
                sp.dma_start(dX[s][:], x1_v[s]).then_inc(d2_ld[s].sem, 16)
            with sp.Fori(0, D2N - 1) as i:
                for s in range(D2S):
                    d2_load(i + 1, s)
                for s in range(D2S):
                    d2_store(i, s)
            for s in range(D2S):
                d2_store(D2N - 1, s)

            r = sage1

            def load(g, b, i, r=r):
                flags(r, 1, g, b, r.rv, "scan", i)

            def store(g, b, i, r=r):
                sp.wait_ge(r.ga[b].sem, r.ga[b].at(i, "all"))
                sp.dma_start(group(r_d[0], g), RB[b][:, :, 0:D]).then_inc(r.st[b].sem, 16)
                sp.wait_ge(r.gb[b].sem, r.gb[b].at(i, "all"))
                sp.dma_start(group(t_d[0], g), TB[b][:]).then_inc(r.st[b].sem, 16)
                on(sp, r.ract, g, "agg")
                sp.dma_start(table_group(agg_d[0], g), AR[b][:]).then_inc(r.st[b].sem, 16)
                on(sp, r.tv, g, "h1")
                sp.dma_start(group(t_d[1], g), TH[b][:]).then_inc(r.st[b].sem, 16)
            rounds(load, store)

            finished(sp, sage1)
            r = sage2

            def load(g, b, i, r=r):
                flags(r, 1, g, b, r.rv, "scan", i)
                if i is not None:
                    on(sp, r.rpe, g, "rT", back=2)
                sp.dma_start(RB[b][:, :, 0:D], group(r_d[0], g)).then_inc(r.ld[b].sem, 16)
                if i is not None:
                    on(sp, r.tv, g, "z", back=2)
                sp.dma_start(TB[b][:], group(t_d[0], g)).then_inc(r.ld[b].sem, 16)
                if i is not None:
                    on(sp, r.tpe, g, "tT", back=2)
                sp.dma_start(TH[b][:], group(t_d[1], g)).then_inc(r.ld[b].sem, 16)

            def store(g, b, i, r=r):
                on(sp, r.rv, g, "h1")
                sp.dma_start(group(r_d[1], g), RH[b][:, :, 0:D]).then_inc(r.st[b].sem, 16)
                on(sp, r.ract, g, "agg")
                sp.dma_start(table_group(agg_d[1], g), AR[b][:]).then_inc(r.st[b].sem, 16)
                on(sp, r.tv, g, "x2")
                sp.dma_start(group(t_d[2], g), OR[b][:]).then_inc(r.st[b].sem, 16)
            rounds(load, store)

            finished(sp, sage2)
            r = meanr

            def load(g, b, i, r=r):
                flags(r, 1, g, b, r.rv, "scan", i)
                if i is not None:
                    on(sp, r.rv, g, "z", back=2)
                sp.dma_start(RB[b][:, :, 0:D], group(r_d[0], g)).then_inc(r.ld[b].sem, 16)
                if i is not None:
                    on(sp, r.rpe, g, "x2T", back=2)
                    sp.wait_ge(r.st[b].sem, r.st[b].at(i, "all"))
                sp.dma_start(RH[b][:, :, 0:D], group(r_d[1], g)).then_inc(r.ld[b].sem, 16)
                if i is not None:
                    on(sp, r.tv, g, "z", back=2)
                sp.dma_start(TB[b][:], group(t_d[2], g)).then_inc(r.ld[b].sem, 16)

            def store(g, b, i, r=r):
                on(sp, r.rv, g, "x2")
                sp.dma_start(group(r_d[2], g), RH[b][:, :, 0:D]).then_inc(r.st[b].sem, 16)
                on(sp, r.rv, g, "agg")
                sp.dma_start(table_group(agg_d[2], g), AR[b][:]).then_inc(r.st[b].sem, 16)
                on(sp, r.tv, g, "x3")
                sp.dma_start(group(t_d[3], g), OR[b][:]).then_inc(r.st[b].sem, 16)
            rounds(load, store)

            finished(sp, meanr)
            r = softr

            def load(g, b, i, r=r):
                flags(r, 1, g, b, r.rv, "num", i)
                if i is not None:
                    on(sp, r.rv, g, "z", back=2)
                sp.dma_start(RB[b][:, :, 0:D], group(r_d[2], g)).then_inc(r.ld[b].sem, 16)
                if i is not None:
                    on(sp, r.tpe, g, "tT", back=2)
                sp.dma_start(TB[b][:], group(t_d[3], g)).then_inc(r.ld[b].sem, 16)
            rounds(load, lambda g, b, i: None)
            for b in range(2):
                sp.wait_ge(r.sc[b].sem, r.sc[b].end(PAIRS))

        @block.gpsimd
        def _(gp):
            gp.sem_inc(step_sems["idx"], CREDIT)
            gp.sem_inc(step_sems["sidx"], CREDIT)
            gp.memset(key_i[:], N).then_inc(pool_init, 1)
            gp.memset(pay_i[:], 0).then_inc(pool_init, 1)
            gp.memset(wt[:], 0.0).then_inc(pool_init, 1)
            gp.memset(zrow[:], 0.0)
            gp.memset(neg[:], -1.0).then_inc(pool_init, 1)
            fv = fill.rearrange("p (q t) -> p q t", t=2)
            gp.memset(fv[:, :, 0], float(NONE_ROW)).then_inc(pool_init, 1)
            gp.memset(fv[:, :, 1], 0.0).then_inc(pool_init, 1)
            gp.memset(ident[:], 0.0).then_inc(pool_init, 1)
            gp.iota(pos_i[:], pattern=[[P, SORT_COLS]], base=0, channel_multiplier=1).then_inc(pool_init, 1)
            gp.wait_ge(pool_init, 8)
            gp.affine_select(out=ident[:], in_=ident[:], compare_op=ALU.not_equal, fill=1.0, base=0,
                             pattern=[[-1, P]], channel_multiplier=1).then_inc(pool_init, 1)

            last_node = gp.to_reg(N - 1)

            def hold(*conditions):
                for steps, i, name, back in conditions:
                    on(gp, steps, i, name, back)
                gp.sem_inc(held, 1)

            def cols(t, side, g):
                return t[:, side, bass.ds(g * W, W)]

            def copy_idx(steps, name, to, columns, dmas, i, b, first=False):
                if not first:
                    on(gp, dmas[b], i, "all", back=1)
                steps.done(gp.tensor_copy(to[b][:], columns), name)

            gp.wait_ge(idx_ready, 1)
            gp.wait_ge(filled, 16 * FILLS)

            def put_map(r, side, i, first=False):
                for b in range(2):
                    g = i * 2 + b
                    copy_idx(r.idx, "a", idx_a, cols(scat_i, side, g), r.sc, i, b, first)
                    r.idx.done(gp.tensor_copy(mrow[b][:], mapv[:, side, bass.ds(g * W, W), :]), "row")
                    hold((r.idx, g, "row", 0))
                    for w in range(W):
                        gp.indirect_dma_start(
                            out=map_d[side], out_offset=bass.IndirectOffsetOnAxis(ap=idx_a[b][:, w:w + 1], axis=0),
                            in_=mrow[b][:, w, :], in_offset=None, bounds_check=last_node, oob_is_err=False,
                        ).then_inc(r.sc[b].sem, 16)

            put_map(map_put[0], 0, 0, first=True)
            for side, r in enumerate(map_put):
                with gp.Fori(1 - side, PAIRS) as i:
                    put_map(r, side, i)
            finished(gp, map_put[1])
            for side, r in enumerate(map_get):
                dmas = (r.ga, r.gb)[side]

                def fetch(i, b, side=side, r=r, dmas=dmas):
                    g = i * 2 + b
                    r.idx.done(gp.tensor_copy(idx_a[b][:], cols(pay_i, side, g)), "a")
                    hold((r.idx, g, "a", 0))
                    for w in range(W):
                        gp.indirect_dma_start(
                            out=mrow[b][:, w, :], out_offset=None, in_=map_d[side],
                            in_offset=bass.IndirectOffsetOnAxis(ap=idx_a[b][:, w:w + 1], axis=0),
                        ).then_inc(dmas[b].sem, 16)

                def keep(i, b, side=side, dmas=dmas):
                    on(gp, dmas[b], i, "all")
                    gp.tensor_copy(found[:, side, bass.ds((i * 2 + b) * W, W), :], mrow[b][:]).then_inc(map_out, 1)

                for b in range(2):
                    if side:
                        gp.wait_ge(map_out, GROUPS)
                    fetch(0, b)
                with gp.Fori(0, PAIRS - 1) as i:
                    for b in range(2):
                        keep(i, b)
                        gp.wait_ge(map_out, i * 2 + (b + 1 + side * GROUPS))
                        fetch(i + 1, b)
                for b in range(2):
                    keep(PAIRS - 1, b)

            def gather(r, key, b, to, table, idx):
                for w in range(W):
                    gp.indirect_dma_start(out=to[b][:, w, 0:D], out_offset=None, in_=table,
                                          in_offset=bass.IndirectOffsetOnAxis(ap=idx[b][:, w:w + 1], axis=0),
                                          ).then_inc(r.dmas[key][b].sem, 16)

            def scatter(r, b, table, rows, idx):
                for w in range(W):
                    gp.indirect_dma_start(out=table, out_offset=bass.IndirectOffsetOnAxis(ap=idx[b][:, w:w + 1], axis=0),
                                          in_=rows[b][:, w, :], in_offset=None, bounds_check=last_node, oob_is_err=False,
                                          ).then_inc(r.sc[b].sem, 16)

            found_rows = lambda side, g: found_i[:, side, bass.ds(g * W, W)]

            gp.wait_ge(found_ready, 1)
            for k, r in enumerate(cheb[:2]):
                with gp.Fori(0, PAIRS) as i:
                    for b in range(2):
                        g = i * 2 + b
                        copy_idx(r.idx, "a", idx_a, cols(pay_i, 0, g) if k == 0 else found_rows(0, g), r.ga, i, b)
                        hold((r.rpe, g, "zT", 2), (r.idx, g, "a", 0))
                        gather(r, "ga", b, GB, x if k == 0 else u_d[k - 1], idx_a)
                finished(gp, r)
            for s in range(DS):
                gp.wait_ge(d1_st[s].sem, d1_st[s].end(D1N))
            r = cheb[2]

            def fetch3(i, b):
                g = i * 2 + b
                copy_idx(r.idx, "a", idx_a, found_rows(0, g), r.ga, i, b)
                copy_idx(r.idx, "b", idx_b, cols(key_i, 0, g), r.gb, i, b)
                hold((r.rpe, g, "zT", 2), (r.idx, g, "b", 0))
                gather(r, "ga", b, GB, u_d[1], idx_a)
                hold((r.rpe, g, "xT", 2))
                gather(r, "gb", b, RB, x, idx_b)

            def put(r, i, b, side, steps, name, table):
                g = i * 2 + b
                copy_idx(r.sidx, "s", idx_s, cols(scat_i, side, g), r.sc, i, b)
                hold((steps, g, name, 0), (r.sidx, g, "s", 0))
                scatter(r, b, table, OR, idx_s)

            def lagging(fetch, put_):
                fetch(0, 0)
                fetch(0, 1)
                put_(0, 0)
                with gp.Fori(1, PAIRS) as i:
                    fetch(i, 0)
                    put_(i - 1, 1)
                    fetch(i, 1)
                    put_(i, 0)
                put_(PAIRS - 1, 1)
            lagging(fetch3, lambda i, b: put(r, i, b, 0, r.rv, "x1", x1_d))
            finished(gp, r)

            r = sage1
            with gp.Fori(0, PAIRS) as i:
                for b in range(2):
                    g = i * 2 + b
                    copy_idx(r.idx, "a", idx_a, cols(pay_i, 1, g), r.ga, i, b)
                    copy_idx(r.idx, "b", idx_b, cols(key_i, 1, g), r.gb, i, b)
                    hold((r.rpe, g, "rT", 2), (r.st[b], i, "all", 1), (r.idx, g, "b", 0))
                    gather(r, "ga", b, RB, x1_d, idx_a)
                    hold((r.tpe, g, "tT", 2))
                    gather(r, "gb", b, TB, x1_d, idx_b)
            finished(gp, r)
            for r, table in ((sage2, agg_d[0]), (meanr, agg_d[1])):
                with gp.Fori(0, PAIRS) as i:
                    for b in range(2):
                        g = i * 2 + b
                        copy_idx(r.idx, "a", idx_a, found_rows(1, g), r.ga, i, b)
                        hold((r.rv, g, "h", 2), (r.idx, g, "a", 0))
                        gather(r, "ga", b, GB, table, idx_a)
                finished(gp, r)
            r = softr
            for s in range(D2S):
                gp.wait_ge(d2_st[s].sem, d2_st[s].end(D2N))

            def fetch4(i, b):
                g = i * 2 + b
                copy_idx(r.idx, "a", idx_a, found_rows(1, g), r.ga, i, b)
                hold((r.rv, g, "z", 2), (r.idx, g, "a", 0))
                gather(r, "ga", b, GB, agg_d[2], idx_a)
            lagging(fetch4, lambda i, b: put(r, i, b, 1, r.tv, "out", out))

        def sort_plan():
            for k in range(1, SORT_BITS + 1):
                if k <= 6:
                    yield ("flip", k - 1 if k > 1 else None, k)
                else:
                    if k == 7:
                        yield ("flip", 6, None)
                    yield ("switch",)
                    yield ("flip", k - 8 if k > 7 else None, k - 7 if k < SORT_BITS else None)
                    for j in range(k - 8, -1, -1):
                        yield ("step", 1 << j)
                    yield ("switch",)
                for j in range(min(k, 7) - 1, -1, -1):
                    yield ("step", 1 << j)

        def scratch_rows(t):
            return t[:, :, :].rearrange("p t d -> p (t d)")

        @block.tensor
        def _(pe):
            for s in range(DS):
                pe.sem_inc(d1_pe[s].sem, CREDIT)
            pe.sem_inc(step_sems["rpe"], CREDIT)
            pe.sem_inc(step_sems["tpe"], CREDIT)
            pe.wait_ge(pool_init, POOL_INITS)
            pe.wait_ge(loaded_w, 16 * WEIGHT_LOADS)
            for q, t in enumerate((w1b1[:, 0], w1b1[:, 1], w0b0[:, 0], w0b0[:, 1])):
                last = pe.transpose(PS[0][0:D, q * P:q * P + D1], t, ident[0:D1, 0:D1])
            last.then_inc(prep_pe, 1)
            pe.wait_ge(prep_v, 1)
            for q, t in enumerate((w2top[:, 0], w2top[:, 1], w2bot[:, 0], w2bot[:, 1])):
                last = pe.matmul(PS[1][0:D1, q * P:q * P + D], wT[:, q, :], t, start=True, stop=True)
            last.then_inc(prep_pe, 1)
            pe.wait_ge(prep_v, 2)
            cur = n = 0
            for op in sort_plan():
                if op[0] == "step":
                    cur ^= 1
                if op[0] != "switch":
                    continue
                n += 1
                pe.wait_ge(switch_ready, n)
                for ps, t in ((PS[0], K[cur]), (PS[1], V[cur])):
                    for q in range(4):
                        last = pe.transpose(ps[:, q * P:(q + 1) * P], t[:, q * P:(q + 1) * P], ident[:])
                    last.then_inc(switched, 1)
                cur ^= 1
            pe.wait_ge(post_v, 1)
            for k, t in enumerate((LOCAL, CPROD)):
                for q in range(4):
                    last = pe.matmul(PS[2][0:1, (4 * k + q) * P:(4 * k + q + 1) * P], t[:, q * P + P - 1:q * P + P],
                                     ident[:], start=True, stop=True)
            last.then_inc(post_pe, 1)
            pe.wait_ge(post_v, 2)
            for q in range(4):
                last = pe.matmul(PS[3][:, q:q + 1], cnt_row[0:1, q // 2, (q % 2) * P:(q % 2 + 1) * P], one[:],
                                 start=True, stop=True)
            last.then_inc(post_pe, 1)
            pe.wait_ge(post_v, 3)
            for k, t in enumerate((SIDX, V[SORTED], K[SORTED], CNT)):
                for q in range(4):
                    last = pe.transpose(PS[k // 2][:, (k % 2) * 512 + q * P:(k % 2) * 512 + (q + 1) * P],
                                        t[:, q * P:(q + 1) * P], ident[:])
            last.then_inc(post_pe, 1)
            pe.wait_ge(idx_ready, 1)

            def transposed(ps, t, tiles=W, p=P, width=D):
                for i in range(tiles):
                    last = pe.transpose(ps[0:width, i * P:i * P + p], t(i), ident[0:p, 0:p])
                return last

            def times(ps, parts, tiles=W, p=P):
                for i in range(tiles):
                    for k, (t, w) in enumerate(parts):
                        last = pe.matmul(ps[0:p, i * P:i * P + D], t(i), w, start=k == 0, stop=k == len(parts) - 1)
                return last

            dense = lambda t: lambda i: t[:, i * D:(i + 1) * D]
            dense_T = lambda t: lambda i: t[:, i * DP:(i + 1) * DP]
            tile = lambda t, width=D: lambda i: t[:, i, 0:width]
            tile_T = lambda t, rows=D1: lambda i: t[0:rows, i * P:(i + 1) * P]
            w97 = lambda n: wt[:, n, :]
            w96 = lambda n: wt[0:D, n, :]

            def d1(i, s):
                on(pe, d1_ld[s], i, "x")
                on(pe, d1_v[s], i, "x1", back=1)
                d1_pe[s].done(transposed(PS[s], dense(dX[s]), DT, DP), "xT")
                yield
                on(pe, d1_act[s], i, "xT")
                d1_pe[s].done(times(PS[s], [(dense_T(dXT[s]), w97(A0))], DT, DP), "mm")

            with pe.Fori(0, D1N) as i:
                weave(*(d1(i, s) for s in range(DS)))
            for s in range(DS):
                pe.wait_ge(d1_v[s].sem, d1_v[s].end(D1N))

            for k, r in enumerate(cheb):
                def chain(g, b, i, k=k, r=r):
                    if k == 0:
                        on(pe, r.rv, g, "scaled")
                    else:
                        on(pe, r.ga[b], i, "all")
                    on(pe, r.rv, g, r.rv.names[-1], back=1)
                    r.rpe.done(transposed(PS[b], tile(GB[b])), "zT")
                    on(pe, r.rv, g, "scan")
                    if k < 2:
                        r.rpe.done(transposed_back(PS[2 + b], SC[b]), "back")
                        return
                    on(pe, r.ld[b], i, "all")
                    r.rpe.done(times(PS[2 + b], [(tile_T(DEN[b], D), w96(B1)), (tile_T(NUM[b], D), w96(B2)),
                                                 (tile_T(SC[b], D), w96(B3))]), "mix")
                    on(pe, r.gb[b], i, "all")
                    r.rpe.done(transposed(PS[b], tile(RB[b])), "xT")
                    on(pe, r.ract, g, "xT")
                    on(pe, r.rv, g, "y")
                    r.rpe.done(times(PS[2 + b], [(tile_T(XT[0]), w97(A0))]), "self")

                def transposed_back(ps, t):
                    for i in range(W):
                        last = pe.transpose(ps[:, i * P:i * P + D], t[0:D, i * P:(i + 1) * P], ident[0:D, 0:D])
                    return last

                with pe.Fori(0, PAIRS) as i:
                    for b in range(2):
                        chain(i * 2 + b, b, i)
                finished(pe, r)

            def d2(i, s):
                ps, v, a = PS[2 + s], d2_v[s], d2_act[s]
                on(pe, d2_ld[s], i, "x1")
                on(pe, v, i, "out", back=1)
                d2_pe[s].done(transposed(ps, dense(dX[s]), DT, DP), "x1T")
                yield
                on(pe, a, i, "x1T")
                d2_pe[s].done(times(ps, [(dense_T(dXT[s]), w97(SELF0))], DT, DP), "mm0")
                yield
                on(pe, v, i, "h1")
                d2_pe[s].done(transposed(ps, dense(dH[s]), DT, DP), "h1T")
                yield
                on(pe, a, i, "h1T")
                d2_pe[s].done(times(ps, [(dense_T(dXT[s]), w97(SELF1))], DT, DP), "mm1")
                yield
                on(pe, v, i, "x3")
                d2_pe[s].done(transposed(ps, dense(dH[s]), DT, DP), "x3T")
                yield
                on(pe, a, i, "x3T")
                d2_pe[s].done(times(ps, [(dense_T(dXT[s]), w97(SOFTI))], DT, DP), "mm3")

            with pe.Fori(0, D2N) as i:
                weave(*(d2(i, s) for s in range(D2S)))

            def src1(r, g, b, i):
                on(pe, r.ga[b], i, "all")
                on(pe, r.ract, g, "agg", back=1)
                r.rpe.done(transposed(PS[0], tile(RB[b], D1), width=D1), "rT")
                yield
                on(pe, r.rv, g, "scan")
                r.rpe.done(times(PS[0], [(tile_T(SC[b]), w97(NB0))]), "agg")

            def dst1(r, g, b, i):
                on(pe, r.gb[b], i, "all")
                on(pe, r.tv, g, r.tv.names[-1], back=1)
                r.tpe.done(transposed(PS[1], tile(TB[b])), "tT")
                yield
                on(pe, r.tact, g, "tT")
                r.tpe.done(times(PS[1], [(tile_T(XT[1]), w97(SELF0))]), "self")

            def src2(r, g, b, i):
                on(pe, r.ld[b], i, "all")
                on(pe, r.ract, g, "agg", back=1)
                r.rpe.done(transposed(PS[0], tile(RB[b])), "rT")
                yield
                on(pe, r.ract, g, "rT")
                r.rpe.done(times(PS[0], [(tile_T(XT[0]), w97(SELF0))]), "self")
                yield
                on(pe, r.rv, g, "h1")
                r.rpe.done(transposed(PS[0], tile(RH[b], D1), width=D1), "h1T")
                yield
                on(pe, r.rv, g, "scan")
                r.rpe.done(times(PS[0], [(tile_T(SC[b]), w97(NB1))]), "agg")

            def dst2(r, g, b, i):
                on(pe, r.ld[b], i, "all")
                on(pe, r.tv, g, "h2", back=1)
                r.tpe.done(transposed(PS[1], tile(TH[b])), "tT")
                yield
                on(pe, r.tact, g, "tT")
                r.tpe.done(times(PS[1], [(tile_T(XT[1]), w97(SELF1))]), "self")

            def src3(r, g, b, i):
                on(pe, r.ld[b], i, "all")
                on(pe, r.rv, g, "agg", back=1)
                r.rpe.done(transposed(PS[0], tile(RH[b])), "rT")
                yield
                on(pe, r.ract, g, "rT")
                r.rpe.done(times(PS[0], [(tile_T(XT[0]), w97(SELF1))]), "self")
                yield
                on(pe, r.rv, g, "x2")
                r.rpe.done(transposed(PS[0], tile(RH[b], D1), width=D1), "x2T")
                yield
                on(pe, r.rv, g, "scan")
                r.rpe.done(times(PS[0], [(tile_T(SC[b]), w97(MEANW))]), "agg")

            def src4(r, g, b, i):
                on(pe, r.rv, g, "x3")
                on(pe, r.rv, g, "m", back=1)
                r.rpe.done(transposed(PS[0], tile(eH[0])), "x3T")
                yield

            def dst4(r, g, b, i):
                on(pe, r.ld[b], i, "all")
                on(pe, r.tv, g, "out", back=1)
                r.tpe.done(transposed(PS[1], tile(TB[b])), "tT")
                yield
                on(pe, r.tact, g, "tT")
                on(pe, r.rv, g, "msg")
                r.tpe.done(times(PS[1], [(tile_T(XT[1]), w97(SOFTI)), (tile_T(MS, D), w96(SOFTW))]), "out")

            for r, streams in ((sage1, (src1, dst1)), (sage2, (src2, dst2)), (meanr, (src3,)), (softr, (src4, dst4))):
                with pe.Fori(0, PAIRS) as i:
                    for b in range(2):
                        weave(*(stream(r, i * 2 + b, b, i) for stream in streams))
                finished(pe, r)

        @block.scalar
        def _(act):
            for s in range(DS):
                act.sem_inc(d1_act[s].sem, CREDIT)
            act.sem_inc(step_sems["ract"], CREDIT)
            act.sem_inc(step_sems["tact"], CREDIT)
            cur = n = 0
            for op in sort_plan():
                if op[0] == "step":
                    cur ^= 1
                if op[0] != "switch":
                    continue
                n += 1
                cur ^= 1
                act.wait_ge(switched, 2 * n)
                act.copy(V[cur], PS[1][:, 0:512]).then_inc(v_back, 1)

            act.wait_ge(post_v, 4)
            act.activation(MX[1][:, 0:512], PS[1][:, 512:1024], ACT.Sqrt).then_inc(roots, 1)

            LN = float(D) ** -0.5
            STD = float(D - 1) ** -0.5

            def from_T(out, ps):
                return act.copy(out[0:D, :].rearrange("f (t c) -> f t c", c=DP),
                                ps[0:D, :].rearrange("f (t c) -> f t c", c=P)[:, :, 0:DP])

            def square(out, in_, scale):
                return act.activation(out, in_, ACT.Square, scale=scale)

            def deviation(m, p, scale=1.0, bias=0.0):
                return act.activation(m[:, 3, :], m[:, 0, :], ACT.Sqrt, scale=scale, bias=bias)

            eps_ = eps[:, :]
            act.wait_ge(idx_ready, 1)

            def d1(i, s):
                on(act, d1_pe[s], i, "xT")
                on(act, d1_pe[s], i, "mm", back=1)
                d1_act[s].done(from_T(dXT[s], PS[s]), "xT")
                yield
                on(act, d1_pe[s], i, "mm")
                on(act, d1_v[s], i, "sum", back=1)
                d1_act[s].done(square(by_tile(dSQ[s]), rows_of(PS[s], DP, DT), LN), "sq")
                yield
                on(act, d1_v[s], i, "sum")
                on(act, d1_v[s], i, "r", back=1)
                d1_act[s].done(deviation(dsm[s], DP, 1.0, eps[0:DP, :]), "sd")

            with act.Fori(0, D1N) as i:
                weave(*(d1(i, s) for s in range(DS)))
            finished(act, cheb[1])

            r = cheb[2]
            with act.Fori(0, PAIRS) as i:
                for b in range(2):
                    g = i * 2 + b
                    on(act, r.rpe, g, "xT")
                    on(act, r.rpe, g, "self", back=1)
                    r.ract.done(act.copy(XT[0][0:D, :], PS[b][0:D, 0:GE]), "xT")
                    on(act, r.rv, g, "pre")
                    on(act, r.rv, g, "sum", back=1)
                    r.ract.done(square(eSQ[0][:], eH[0][:], LN), "sq")
                    on(act, r.rv, g, "sum")
                    r.ract.done(deviation(esm[0], P, 1.0, eps_), "sd")
            finished(act, r)

            def d2(i, s):
                ps, pe_, v = PS[2 + s], d2_pe[s], d2_v[s]
                Z = dH[s + 2]
                on(act, pe_, i, "x1T")
                d2_act[s].done(from_T(dXT[s], ps), "x1T")
                yield
                on(act, v, i, "m2s")
                d2_act[s].done(act.activation(dsm[s][:, 3, :], dsm[s][:, 2, :], ACT.Sqrt, scale=1.0 / (D - 1)), "sd1")
                yield
                on(act, pe_, i, "h1T")
                d2_act[s].done(from_T(dXT[s], ps), "h1T")
                yield
                on(act, pe_, i, "mm1")
                on(act, v, i, "sumo", back=1)
                d2_act[s].done(square(by_tile(dSQ[s]), rows_of(ps, DP, DT), STD), "sq2")
                yield
                on(act, v, i, "sum2")
                d2_act[s].done(deviation(dsm[s], DP), "sd2")
                yield
                on(act, v, i, "z")
                d2_act[s].done(square(dSQ[s][:], Z[:], LN), "sqz")
                yield
                on(act, v, i, "sumz")
                d2_act[s].done(deviation(dsm[s], DP, 1.0 + LN_EPS, eps2[0:DP, :]), "sdz")
                yield
                on(act, pe_, i, "x3T")
                d2_act[s].done(from_T(dXT[s], ps), "x3T")
                yield
                on(act, pe_, i, "mm3")
                d2_act[s].done(square(by_tile(dSQ[s]), rows_of(ps, DP, DT), LN), "sqo")
                yield
                on(act, v, i, "sumo")
                d2_act[s].done(deviation(dsm[s], DP, 1.0, eps[0:DP, :]), "sdo")

            with act.Fori(0, D2N) as i:
                weave(*(d2(i, s) for s in range(D2S)))

            def src1(r, g, b, i):
                on(act, r.rpe, g, "agg")
                on(act, r.st[b], i, "all", back=1)
                on(act, r.tv, g, "h", back=2)
                r.ract.done(act.copy(AR[b][:], rows_of(PS[0], P, W)), "agg")
                yield

            def dst_T(r, g, last):
                on(act, r.tpe, g, "tT")
                on(act, r.tpe, g, last, back=1)
                r.tact.done(act.copy(XT[1][0:D, :], PS[1][0:D, 0:GE]), "tT")

            def plain_std(m):
                return act.activation(m[:, 3, :], m[:, 2, :], ACT.Sqrt, scale=1.0 / (D - 1))

            def dst1(r, g, b, i):
                dst_T(r, g, "self")
                yield
                on(act, r.tv, g, "m2s")
                r.tact.done(plain_std(esm[1]), "sd")
                yield

            def src2(r, g, b, i):
                on(act, r.rpe, g, "rT")
                r.ract.done(act.copy(XT[0][0:D, :], PS[0][0:D, 0:GE]), "rT")
                yield
                on(act, r.rv, g, "m2s")
                r.ract.done(plain_std(esm[0]), "sd")
                yield
                on(act, r.rpe, g, "agg")
                on(act, r.st[b], i, "all", back=1)
                on(act, r.tv, g, "h", back=2)
                r.ract.done(act.copy(AR[b][:], rows_of(PS[0], P, W)), "agg")
                yield

            def dst2(r, g, b, i):
                dst_T(r, g, "self")
                yield
                yield
                on(act, r.tv, g, "h")
                on(act, r.tv, g, "sumz", back=1)
                r.tact.done(square(eSQ[1][:], eH[1][:], STD), "sq")
                on(act, r.tv, g, "sum")
                r.tact.done(deviation(esm[1], P), "sd")
                yield
                on(act, r.tv, g, "z")
                r.tact.done(square(eSQ[1][:], eZ[1][:], LN), "sqz")
                on(act, r.tv, g, "sumz")
                r.tact.done(deviation(esm[1], P, 1.0, eps_), "sdz")
                yield

            def src3(r, g, b, i):
                on(act, r.rpe, g, "rT")
                r.ract.done(act.copy(XT[0][0:D, :], PS[0][0:D, 0:GE]), "rT")
                yield
                on(act, r.rv, g, "h")
                on(act, r.rv, g, "sumz", back=1)
                r.ract.done(square(eSQ[0][:], eH[0][:], STD), "sq")
                on(act, r.rv, g, "sum")
                r.ract.done(deviation(esm[0], P), "sd")
                yield
                on(act, r.rv, g, "z")
                r.ract.done(square(eSQ[0][:], eZ[0][:], LN), "sqz")
                on(act, r.rv, g, "sumz")
                r.ract.done(deviation(esm[0], P, 1.0, eps_), "sdz")
                yield

            def dst3(r, g, b, i):
                yield
                yield
                yield
                on(act, r.tv, g, "z")
                on(act, r.tv, g, "sumz", back=1)
                r.tact.done(square(eSQ[1][:], eZ[1][:], LN), "sqz")
                on(act, r.tv, g, "sumz")
                r.tact.done(deviation(esm[1], P, 1.0, eps_), "sdz")

            def src4(r, g, b, i):
                on(act, r.rv, g, "z")
                on(act, r.rv, g, "sumz", back=1)
                r.ract.done(square(eSQ[0][:], eZ[0][:], LN), "sqz")
                on(act, r.rv, g, "sumz")
                r.ract.done(deviation(esm[0], P, 1.0, eps_), "sdz")
                yield
                on(act, r.rv, g, "less")
                r.ract.done(act.activation(DEC[0:D, :], DEC[0:D, :], ACT.Exp), "dec")
                yield
                on(act, r.rv, g, "off")
                r.ract.done(act.activation(EX[0:D, :], EX[0:D, :], ACT.Exp), "ex")
                yield

            def dst4(r, g, b, i):
                dst_T(r, g, "out")
                yield
                yield
                yield
                on(act, r.tpe, g, "out")
                on(act, r.tv, g, "sumo", back=1)
                r.tact.done(square(eSQ[1][:], rows_of(PS[1], P, W), LN), "sqo")
                on(act, r.tv, g, "sumo")
                r.tact.done(deviation(esm[1], P, 1.0, eps_), "sdo")

            for r, streams in ((sage1, (src1, dst1)), (sage2, (src2, dst2)), (meanr, (src3, dst3)), (softr, (src4, dst4))):
                with act.Fori(0, PAIRS) as i:
                    for b in range(2):
                        weave(*(stream(r, i * 2 + b, b, i) for stream in streams))
                finished(act, r)

        @block.vector
        def _(dve):
            for s in range(DS):
                dve.sem_inc(d1_v[s].sem, CREDIT)
            dve.sem_inc(step_sems["rv"], CREDIT)
            dve.sem_inc(step_sems["tv"], CREDIT)
            count = [0]

            def do(instruction):
                count[0] += 1
                instruction.then_inc(sort_step, 1)
                return count[0]

            def need(*numbers):
                dve.wait_ge(sort_step, max(numbers))

            for t, value in ((ones[:], 1.0), (one[:], 1.0), (cnt_row[:], 0.0), (eps[:], LN_EPS), (eps2[:], LN_EPS * LN_EPS),
                             *((t[D:D1, :], 1.0) for t in (*dXT, *XT)),
                             *((t[:, :, D:D1], 1.0) for t in (*RB, *RH))):
                do(dve.memset(t, value))
            dve.wait_ge(pool_init, POOL_INITS)
            dve.wait_ge(loaded_w, 16 * WEIGHT_LOADS)
            dve.wait_ge(prep_pe, 1)
            a = do(dve.tensor_copy(wT[:], PS[0][0:D, 0:512].rearrange("p (q c) -> p q c", c=P)[:, :, 0:D1]))
            need(a)
            dve.sem_inc(prep_v, 1)
            dve.wait_ge(prep_pe, 2)
            q4 = lambda q: PS[1][0:D1, q * P:q * P + D]
            for q, w in ((0, SELF0), (1, SELF1), (2, NB0), (3, NB1)):
                a = do(dve.tensor_copy(wt[:, w, :], q4(q)))
            need(a)
            for q, w in ((0, SELF0), (1, SELF1)):
                a = do(dve.tensor_tensor(wt[D:D1, w, :], wt[D:D1, w, :], b2row[D:D1, q, :], ALU.add))
            dve.sem_inc(prep_v, 1)
            idn = ident[0:D, 0:D]
            c = lambda k: chebw[:, k, :]
            a = do(dve.tensor_tensor(wt[0:D, A0, :], c(0), c(2), ALU.subtract))
            do(dve.scalar_tensor_tensor(wt[0:D, B1, :], c(3), -3.0, c(1), ALU.mult, ALU.add))
            do(dve.tensor_scalar(wt[0:D, B2, :], c(2), 2.0, None, ALU.mult))
            do(dve.tensor_scalar(wt[0:D, B3, :], c(3), 4.0, None, ALU.mult))
            do(dve.tensor_copy(wt[0:D, SOFTI, :], wt[0:D, SOFTW, :]))
            need(count[0])
            do(dve.tensor_tensor(wt[0:D, A0, :], wt[0:D, A0, :], idn, ALU.add))
            a = do(dve.tensor_tensor(wt[0:D, SOFTI, :], wt[0:D, SOFTI, :], idn, ALU.add))
            need(a)
            a = do(dve.tensor_reduce(wmean[:], wt[:, 0:9, :], AX.X, ALU.add))
            need(a)
            a = do(dve.tensor_scalar(wmean[:], wmean[:], -1.0 / D, None, ALU.mult))
            need(a)
            a = do(dve.tensor_tensor(wt[:, 0:9, :], wt[:, 0:9, :], spread(wmean[:], D1, 9), ALU.add))
            need(a)
            dve.wait_ge(loaded_e, 16 * 12)
            k_in = do(dve.tensor_copy(K[0], key_i[:].rearrange("p s c -> p (s c)")))
            v_in = do(dve.tensor_copy(V[0], pay_i[:].rearrange("p s c -> p (s c)")))

            cur = n = 0
            k_ok, v_ok = k_in, v_in

            def blocks(t, half, part):
                return t.rearrange("p (s two d) -> p s two d", two=2, d=half)[:, :, part, :]

            for op in sort_plan():
                if op[0] == "flip":
                    back, on_ = op[1], op[2]
                    if back is None and on_ is None:
                        continue
                    if back is not None and on_ is not None:
                        quarter = 1 << back
                        t = K[cur].rearrange("p (s four d) -> p s four d", four=4, d=quarter)[:, :, 1:3, :]
                    else:
                        t = blocks(K[cur], 1 << (on_ if back is None else back), 1)
                    need(k_ok)
                    k_ok = do(dve.tensor_scalar(t, t, -1.0, None, ALU.mult))
                elif op[0] == "switch":
                    n += 1
                    need(max(k_ok, v_ok))
                    dve.sem_inc(switch_ready, 1)
                    cur ^= 1
                    dve.wait_ge(switched, 2 * n - 1)
                    k_ok = do(dve.tensor_copy(K[cur], PS[0][:, 0:512]))
                    dve.wait_ge(v_back, n)
                    v_ok = k_ok
                else:
                    d = op[1]
                    ka, kb, va, vb = (blocks(t, d, part) for t in (K[cur], V[cur]) for part in (0, 1))
                    new = cur ^ 1
                    nka, nkb, nva, nvb = (blocks(t, d, part) for t in (K[new], V[new]) for part in (0, 1))
                    mask = MASK[cur][:, 0:256].rearrange("p (s d) -> p s d", d=d)
                    dif = DIF[:, 0:256].rearrange("p (s d) -> p s d", d=d)
                    need(k_ok)
                    do(dve.tensor_tensor(nka, ka, kb, ALU.min))
                    m = do(dve.tensor_tensor(mask, ka, kb, ALU.is_gt))
                    need(v_ok)
                    f = do(dve.tensor_tensor(dif, vb, va, ALU.subtract))
                    k_ok = do(dve.tensor_tensor(nkb, ka, kb, ALU.max))
                    need(m, f)
                    f = do(dve.tensor_tensor(dif, dif, mask, ALU.mult))
                    need(f)
                    do(dve.tensor_tensor(nva, va, dif, ALU.add))
                    v_ok = do(dve.tensor_tensor(nvb, vb, dif, ALU.subtract))
                    cur = new
            assert cur == SORTED
            KS = K[cur]
            need(v_ok, k_ok)
            dve.sem_inc(keys_out, 1)

            dve.wait_ge(keys_in, 16 * 6)
            a = do(dve.tensor_tensor(CONT, KS, KPREV, ALU.is_equal))
            f = do(dve.tensor_tensor(KNEXT, KS, KNEXT, ALU.is_equal))
            need(f)
            dve.sem_inc(keys_out, 1)
            do(dve.scalar_tensor_tensor(SIDX, KNEXT, FAR, KS, ALU.mult, ALU.add))
            for q in range(4):
                part = slice(q * P, (q + 1) * P)
                do(dve.tensor_tensor_scan(LOCAL[:, part], CONT[:, part], ones[:], 0.0, ALU.mult, ALU.add))
                a = do(dve.tensor_tensor_scan(CPROD[:, part], CONT[:, part], ones[:], 1.0, ALU.mult, ALU.mult))
            need(a)
            dve.sem_inc(post_v, 1)
            dve.wait_ge(post_pe, 1)
            a = do(dve.tensor_copy(cnt_in[:], PS[2][0:1, :]))
            need(a)
            for side in range(2):
                row = slice(side * SORT_COLS, (side + 1) * SORT_COLS)
                goes_on = slice((side + 2) * SORT_COLS, (side + 3) * SORT_COLS)
                a = do(dve.tensor_tensor_scan(cnt_row[0:1, side, 1:SORT_COLS + 1], cnt_in[:, goes_on], cnt_in[:, row],
                                              0.0, ALU.mult, ALU.add))
            need(a)
            dve.sem_inc(post_v, 1)
            dve.wait_ge(post_pe, 2)
            a = do(dve.tensor_copy(cnt_col[:], PS[3][:, 0:4]))
            need(a)
            for q in range(4):
                part = slice(q * P, (q + 1) * P)
                a = do(dve.scalar_tensor_tensor(CNT[:, part], CPROD[:, part], cnt_col[:, q:q + 1], LOCAL[:, part],
                                                ALU.mult, ALU.add))
            need(a)
            dve.sem_inc(post_v, 1)
            dve.wait_ge(post_pe, 3)
            flat = lambda t: t[:].rearrange("p s c -> p (s c)")
            do(dve.tensor_copy(flat(scat_i), PS[0][:, 0:512]))
            do(dve.tensor_copy(flat(pay_i), PS[0][:, 512:1024]))
            do(dve.tensor_scalar(flat(key_i), PS[1][:, 0:512], float(N - 1), None, ALU.min))
            for side in range(2):
                do(dve.tensor_copy(mapv[:, side, :, 0], pos_i[:]))
            b_ = do(dve.reciprocal(nrc[:], PS[1][:, 512:768]))
            do(dve.tensor_scalar(rcb[:], PS[1][:, 768:1024], 1.0, None, ALU.max))
            need(count[0])
            dve.sem_inc(post_v, 1)
            dve.wait_ge(roots, 1)
            a = do(dve.reciprocal(mapv[:, :, :, 1], MX[1][:, 0:512].rearrange("p (s c) -> p s c", s=2)))
            need(a)
            do(dve.tensor_scalar(ndinv[:], mapv[:, 0, :, 1], -1.0, None, ALU.mult))
            do(dve.tensor_scalar(nrc[:], nrc[:], -1.0, None, ALU.mult))
            a = do(dve.reciprocal(rcb[:], rcb[:]))
            for t in (SC[1], DEN[1], NUM[1]):
                a = do(dve.memset(t[:, GE - 1:GE], 0.0))
            for t in MX:
                a = do(dve.memset(t[:, GE:GE + 1], 0.0))
            need(a)
            dve.sem_inc(idx_ready, 1)

            def means(out, sq):
                return dve.tensor_reduce(out, sq, AX.X, ALU.add)

            def d1(i, s):
                v, m = d1_v[s], dsm[s]
                on(dve, d1_act[s], i, "sq")
                v.done(means(m[:, 0, :], by_tile(dSQ[s])), "sum")
                yield
                on(dve, d1_act[s], i, "sd")
                v.done(dve.reciprocal(m[:, 1, :], m[:, 3, :]), "r")
                on(dve, v, i, "r")
                on(dve, d1_st[s], i, "x1", back=1)
                v.done(dve.tensor_tensor(by_tile(dH[s]), rows_of(PS[s], DP, DT), spread(m[:, 1, :], DP, DT), ALU.mult), "x1")

            with dve.Fori(0, D1N) as i:
                weave(*(d1(i, s) for s in range(DS)))

            dve.wait_ge(map_out, 2 * GROUPS)
            a = do(dve.tensor_copy(found_i[:], found[:, :, :, 0]))
            need(a)
            dve.sem_inc(found_ready, 1)

            def cols(t, g):
                return t[:, bass.ds(g * W, W)]

            def scan(out, flags_, values, before, op1=ALU.add):
                return dve.tensor_tensor_scan(out, flags_, values, before, ALU.mult, op1)

            def sums(r, g, b, i, rows, source):
                on(dve, r.fl[b], i, "all")
                on(dve, r.rv, g, "scan", back=1)
                r.rv.done(scan(SC[b][0:rows, :], FL[b][0:rows, :], source[0:rows, 0:GE], SC[b ^ 1][0:rows, GE - 1:GE]), "scan")

            for k, r in enumerate(cheb):
                with dve.Fori(0, PAIRS) as i:
                    for b in range(2):
                        g = i * 2 + b
                        if k == 0:
                            on(dve, r.ga[b], i, "all")
                            r.rv.done(dve.tensor_tensor(GB[b][:], GB[b][:], spread(found[:, 0, bass.ds(g * W, W), 1], P, W),
                                                        ALU.mult), "scaled")
                        on(dve, r.rpe, g, "zT")
                        if k < 2:
                            on(dve, r.st[b], i, "all", back=1)
                            sums(r, g, b, i, D, PS[b])
                            on(dve, r.rpe, g, "back")
                            r.rv.done(dve.tensor_tensor(OR[b][:], rows_of(PS[2 + b], P, W), spread(cols(nrc, g), P, W),
                                                        ALU.mult), "u")
                            continue
                        on(dve, r.rpe, g, "mix", back=2)
                        sums(r, g, b, i, D, PS[b])
                        on(dve, r.rpe, g, "mix")
                        r.rv.done(dve.tensor_tensor(eH[1][:], rows_of(PS[2 + b], P, W), spread(cols(ndinv, g), P, W), ALU.mult), "y")
                        on(dve, r.rpe, g, "self")
                        on(dve, r.rv, g, "y")
                        r.rv.done(dve.tensor_tensor(eH[0][:], eH[1][:], rows_of(PS[2 + b], P, W), ALU.add), "pre")
                        on(dve, r.ract, g, "sq")
                        r.rv.done(means(esm[0][:, 0, :], eSQ[0][:]), "sum")
                        on(dve, r.ract, g, "sd")
                        r.rv.done(dve.reciprocal(esm[0][:, 1, :], esm[0][:, 3, :]), "r")
                        on(dve, r.rv, g, "r")
                        on(dve, r.sc[b], i, "all", back=1)
                        r.rv.done(dve.tensor_tensor(OR[b][:], eH[0][:], spread(esm[0][:, 1, :], P, W), ALU.mult), "x1")
                finished(dve, r)

            def about_mean(v, i, rows, six, m, tiles):
                for t in range(tiles):
                    ins = dve.bn_stats(six[:, t, :], rows[:, t, :])
                v.done(ins, "bn")
                on(dve, v, i, "bn")
                v.done(dve.tensor_tensor(m[:, 0, :], six[:, :, 1], six[:, :, 4], ALU.subtract), "dm")
                on(dve, v, i, "dm")
                v.done(dve.scalar_tensor_tensor(m[:, 1, :], m[:, 0, :], D / 4.0, m[:, 0, :], ALU.mult, ALU.mult), "dm2")
                v.done(dve.tensor_tensor(m[:, 2, :], six[:, :, 2], six[:, :, 5], ALU.add), "m2")
                on(dve, v, i, "m2")
                v.done(dve.tensor_tensor(m[:, 2, :], m[:, 1, :], m[:, 2, :], ALU.add), "m2s")

            def inverse(m):
                return dve.reciprocal(m[:, 1, :], m[:, 3, :])

            def scale_by(out, rows, m, p, tiles):
                return dve.tensor_tensor(out, rows, spread(m[:, 1, :], p, tiles), ALU.mult)

            def d2(i, s):
                v, a_, m, ps = d2_v[s], d2_act[s], dsm[s], PS[2 + s]
                rows = rows_of(ps, DP, DT)
                H, Z, X, OUT, SQ = (by_tile(t) for t in (dH[s], dH[s + 2], dX[s], dX[s + 2], dSQ[s]))
                on(dve, d2_pe[s], i, "mm0")
                about_mean(v, i, rows, dst6[s], m, DT)
                yield
                on(dve, a_, i, "sd1")
                v.done(inverse(m), "r1")
                on(dve, v, i, "r1")
                v.done(scale_by(H, rows, m, DP, DT), "h1")
                yield
                on(dve, a_, i, "sq2")
                v.done(means(m[:, 0, :], SQ), "sum2")
                yield
                on(dve, a_, i, "sd2")
                v.done(inverse(m), "r2")
                on(dve, v, i, "r2")
                v.done(scale_by(Z, rows, m, DP, DT), "h2")
                on(dve, v, i, "h2")
                v.done(dve.tensor_tensor(Z, Z, X, ALU.add), "z")
                yield
                on(dve, a_, i, "sqz")
                v.done(means(m[:, 0, :], SQ), "sumz")
                yield
                on(dve, a_, i, "sdz")
                v.done(inverse(m), "rz")
                on(dve, v, i, "rz")
                v.done(scale_by(H, Z, m, DP, DT), "x3")
                yield
                on(dve, a_, i, "sqo")
                v.done(means(m[:, 0, :], SQ), "sumo")
                yield
                on(dve, a_, i, "sdo")
                v.done(inverse(m), "ro")
                on(dve, v, i, "ro")
                on(dve, d2_st[s], i, "out", back=1)
                v.done(scale_by(OUT, rows, m, DP, DT), "out")

            with dve.Fori(0, D2N) as i:
                weave(*(d2(i, s) for s in range(D2S)))

            def src1(r, g, b, i):
                on(dve, r.rpe, g, "rT")
                on(dve, r.rpe, g, "agg", back=2)
                sums(r, g, b, i, D1, PS[0])
                yield

            def dst1(r, g, b, i):
                yield
                on(dve, r.tpe, g, "self")
                on(dve, r.ract, g, "agg")
                r.tv.done(dve.tensor_tensor(eH[1][:], rows_of(PS[1], P, W), AR[b][:], ALU.add), "h")
                on(dve, r.tv, g, "h")
                about_mean(r.tv, g, eH[1], est6[1], esm[1], W)
                on(dve, r.tact, g, "sd")
                r.tv.done(inverse(esm[1]), "r")
                on(dve, r.tv, g, "r")
                on(dve, r.st[b], i, "all", back=1)
                r.tv.done(scale_by(TH[b][:], eH[1][:], esm[1], P, W), "h1")

            def src2(r, g, b, i):
                on(dve, r.rpe, g, "self")
                on(dve, r.ga[b], i, "all")
                r.rv.done(dve.tensor_tensor(eH[0][:], rows_of(PS[0], P, W), GB[b][:], ALU.add), "h")
                on(dve, r.rv, g, "h")
                about_mean(r.rv, g, eH[0], est6[0], esm[0], W)
                on(dve, r.ract, g, "sd")
                r.rv.done(inverse(esm[0]), "r")
                on(dve, r.rv, g, "r")
                on(dve, r.st[b], i, "all", back=1)
                on(dve, r.rpe, g, "h1T", back=2)
                r.rv.done(scale_by(RH[b][:, :, 0:D], eH[0][:], esm[0], P, W), "h1")
                yield
                on(dve, r.rpe, g, "h1T")
                on(dve, r.rpe, g, "agg", back=2)
                sums(r, g, b, i, D1, PS[0])
                yield

            def residual(v, acts, g, H, X, e):
                m = esm[e]
                on(dve, acts, g, "sq")
                v.done(means(m[:, 0, :], eSQ[e][:]), "sum")
                on(dve, acts, g, "sd")
                v.done(inverse(m), "r")
                on(dve, v, g, "r")
                v.done(scale_by(eZ[e][:], H, m, P, W), "h2")
                on(dve, v, g, "h2")
                v.done(dve.tensor_tensor(eZ[e][:], eZ[e][:], X, ALU.add), "z")

            def normed(v, acts, g, out, name, e, before):
                m = esm[e]
                on(dve, acts, g, "sqz")
                v.done(means(m[:, 0, :], eSQ[e][:]), "sumz")
                on(dve, acts, g, "sdz")
                v.done(inverse(m), "rz")
                on(dve, v, g, "rz")
                before()
                v.done(scale_by(out, eZ[e][:], m, P, W), name)

            def dst2(r, g, b, i):
                yield
                yield
                on(dve, r.tpe, g, "self")
                on(dve, r.ract, g, "agg")
                r.tv.done(dve.tensor_tensor(eH[1][:], rows_of(PS[1], P, W), AR[b][:], ALU.add), "h")
                yield
                residual(r.tv, r.tact, g, eH[1][:], TB[b][:], 1)
                yield
                normed(r.tv, r.tact, g, OR[b][:], "x2", 1, lambda: on(dve, r.st[b], i, "all", back=1))

            def src3(r, g, b, i):
                on(dve, r.rpe, g, "self")
                on(dve, r.ga[b], i, "all")
                r.rv.done(dve.tensor_tensor(eH[0][:], rows_of(PS[0], P, W), GB[b][:], ALU.add), "h")
                yield
                residual(r.rv, r.ract, g, eH[0][:], RB[b][:, :, 0:D], 0)
                yield
                normed(r.rv, r.ract, g, RH[b][:, :, 0:D], "x2", 0, lambda: None)
                yield
                on(dve, r.rpe, g, "x2T")
                on(dve, r.rpe, g, "agg", back=2)
                sums(r, g, b, i, D1, PS[0])
                yield
                on(dve, r.rpe, g, "agg")
                on(dve, r.st[b], i, "all", back=1)
                on(dve, r.tv, g, "z", back=2)
                r.rv.done(dve.tensor_tensor(AR[b][:], rows_of(PS[0], P, W), spread(cols(rcb, g), P, W), ALU.mult), "agg")
                yield

            def dst3(r, g, b, i):
                for _ in range(5):
                    yield
                on(dve, r.ld[b], i, "all")
                on(dve, r.rv, g, "agg")
                r.tv.done(dve.tensor_tensor(eZ[1][:], TB[b][:], AR[b][:], ALU.add), "z")
                yield
                normed(r.tv, r.tact, g, OR[b][:], "x3", 1, lambda: on(dve, r.st[b], i, "all", back=1))

            def src4(r, g, b, i):
                f = lambda t: t[0:D, 0:GE]
                v = r.rv
                on(dve, r.ga[b], i, "all")
                on(dve, r.ld[b], i, "all")
                v.done(dve.tensor_tensor(eZ[0][:], RB[b][:, :, 0:D], GB[b][:], ALU.add), "z")
                normed(v, r.ract, g, eH[0][:], "x3", 0, lambda: None)
                yield
                on(dve, r.rpe, g, "x3T")
                v.done(dve.tensor_scalar(f(MB), PS[0][0:D, 0:GE], 0.0, MSG_EPS, ALU.max, ALU.add), "m")
                v.done(dve.tensor_copy(MX[b][0:D, 0:1], MX[b ^ 1][0:D, GE:GE + 1]), "carry")
                on(dve, r.fl[b], i, "all")
                on(dve, v, g, "carry")
                v.done(scan(MX[b][0:D, 1:GE + 1], FL[b][0:D, :], f(MB), MX[b][0:D, 0:1], ALU.max), "max")
                on(dve, v, g, "max")
                v.done(dve.tensor_tensor(f(DEC), FL[b][0:D, :], MX[b][0:D, 0:GE], ALU.mult), "kept")
                on(dve, v, g, "kept")
                v.done(dve.tensor_tensor(f(DEC), f(DEC), MX[b][0:D, 1:GE + 1], ALU.subtract), "less")
                v.done(dve.tensor_tensor(f(EX), f(MB), MX[b][0:D, 1:GE + 1], ALU.subtract), "off")
                on(dve, r.ract, g, "dec")
                v.done(dve.tensor_tensor(f(DEC), f(DEC), FL[b][0:D, :], ALU.mult), "dec")
                on(dve, r.ract, g, "ex")
                v.done(dve.tensor_tensor(f(QQ), f(EX), f(MB), ALU.mult), "q")
                on(dve, v, g, "dec")
                v.done(scan(f(DEN[b]), f(DEC), f(EX), DEN[b ^ 1][0:D, GE - 1:GE]), "den")
                on(dve, v, g, "q")
                v.done(scan(f(NUM[b]), f(DEC), f(QQ), NUM[b ^ 1][0:D, GE - 1:GE]), "num")
                on(dve, v, g, "den")
                on(dve, r.tpe, g, "out", back=1)
                v.done(dve.reciprocal(f(MS), f(DEN[b])), "rec")
                on(dve, v, g, "rec")
                v.done(dve.tensor_tensor(f(MS), f(MS), f(NUM[b]), ALU.mult), "msg")
                yield

            def dst4(r, g, b, i):
                v, m = r.tv, esm[1]
                yield
                yield
                on(dve, r.tact, g, "sqo")
                v.done(means(m[:, 0, :], eSQ[1][:]), "sumo")
                on(dve, r.tact, g, "sdo")
                v.done(inverse(m), "ro")
                on(dve, v, g, "ro")
                on(dve, r.sc[b], i, "all", back=1)
                v.done(dve.tensor_tensor(OR[b][:], rows_of(PS[1], P, W), spread(m[:, 1, :], P, W), ALU.mult), "out")

            for r, streams in ((sage1, (src1, dst1)), (sage2, (src2, dst2)), (meanr, (src3, dst3)), (softr, (src4, dst4))):
                with dve.Fori(0, PAIRS) as i:
                    for b in range(2):
                        weave(*(stream(r, i * 2 + b, b, i) for stream in streams))
                finished(dve, r)
                if r is meanr:
                    for t in (DEN[1], NUM[1]):
                        a = do(dve.memset(t[0:D, GE - 1:GE], 0.0))
                    need(a)


_INS = ["x", "src", "dst", "L0_gnn_weight", "L0_gnn_bias", "L1_gnn_W0", "L1_gnn_b0", "L1_gnn_W1", "L1_gnn_b1",
        "L1_gnn_W2", "L1_gnn_b2", "L2_gnn_W", "L2_gnn_b", "L3_gnn_W", "L3_gnn_b"]


def kernel(**inputs):
    import concourse.bacc as _bacc
    from concourse.bass_utils import run_bass_kernel_spmd as _run

    nc = _bacc.Bacc("TRN2", target_bir_lowering=False, num_devices=1)
    arrays, args = {}, []
    for name in _INS:
        a = np.ascontiguousarray(inputs[name])
        arrays[f"in_{name}"] = a
        args.append(nc.dram_tensor(f"in_{name}", a.shape, mybir.dt.from_np(a.dtype), kind="ExternalInput").ap())
    args.append(nc.dram_tensor("out_x", (N, D), F32, kind="ExternalOutput").ap())
    gnn_program(nc, *args)
    r = _run(nc, [arrays], core_ids=[0])
    return r.results[0]["out_x"]
```

```python
import numpy as np
import concourse.bass as bass
from concourse import mybir
from contextlib import ExitStack

F32 = mybir.dt.float32
I32 = mybir.dt.int32
ALU = mybir.AluOpType
ACT = mybir.ActivationFunctionType
AX = mybir.AxisListType

P = 128
N, D, E = 100000, 96, 25000
D1 = D + 1
SORT = 32768
SORT_BITS = 15
SORT_COLS = SORT // P
TILES = -(-E // P)
EP = TILES * P
W = 7
GROUPS = TILES // W
PAIRS = GROUPS // 2
GE = W * P
NONE_ROW = EP
FAR = float(1 << 20)
DP, DT = 125, 8
DROWS = DP * DT
CREDIT = 16
LN_EPS = 1e-5
MSG_EPS = 1e-7


class Steps:

    def __init__(self, sem, start, names, unit=1):
        self.sem, self.start, self.names, self.unit = sem, start, names, unit
        self.n = 0

    def at(self, i, name, back=0):
        k = self.start + (self.names.index(name) + 1 - back * len(self.names)) * self.unit
        return i * (len(self.names) * self.unit) + k

    def done(self, instruction, name):
        assert self.names[self.n % len(self.names)] == name, (name, self.names[self.n % len(self.names)])
        self.n += 1
        return instruction.then_inc(self.sem, self.unit)

    def end(self, rounds):
        return self.start + rounds * len(self.names) * self.unit


def weave(*programs):
    due = [(p, 0) for p in programs if p]
    slot = 0
    while due:
        later = []
        for p, at in due:
            while at is not None and at <= slot:
                try:
                    at = next(p)
                    at = slot + 1 if at is None else at
                except StopIteration:
                    at = None
            if at is not None:
                later.append((p, at))
        due = later
        slot += 1




def gnn_program(nc, x, src, dst, cheb_w, cheb_b, sage_w0, sage_b0, sage_w1, sage_b1, sage_w2, sage_b2,
                mean_w, mean_b, soft_w, soft_b, out):
    ctx = ExitStack()
    with ctx:
        def sb(name, shape, dt=F32):
            return ctx.enter_context(nc.sbuf_tensor(name, shape, dt))

        def sem(name):
            return ctx.enter_context(nc.semaphore(name))

        def dram(name, shape):
            return nc.dram_tensor(name, shape, F32, kind="Internal").ap()

        x1_d = dram("x1_table", [N, D])
        sorted_d = dram("sorted_keys", [2, SORT + 2])
        cont_d = dram("segment_goes_on", [2, SORT])
        map_d = [dram(f"node_map{s}", [N, 2]) for s in range(2)]
        u_d = [dram(f"u_table{k}", [EP + 1, D]) for k in range(2)]
        sT_d = [dram(f"cheb_sums{k}", [D, EP]) for k in range(2)]
        agg_d = [dram(f"agg_table{k}", [EP + 1, D]) for k in range(3)]
        r_d = [dram(f"src_rows{k}", [GROUPS, P, W * D]) for k in range(3)]
        t_d = [dram(f"dst_rows{k}", [GROUPS, P, W * D]) for k in range(4)]

        ident = sb("ident", [P, P])
        zrow = sb("zrow", [1, D])
        neg = sb("neg", [1, 1])
        one = sb("one", [1, 1])
        eps = sb("eps", [P, 1])
        eps2 = sb("eps2", [P, 1])
        ones = sb("ones", [P, P])
        pos_i = sb("pos_i", [P, SORT_COLS], I32)
        chebw = sb("chebw", [D, 4, D])
        w1b1 = sb("w1b1", [D1, 2, D])
        w0b0 = sb("w0b0", [D1, 2, D])
        w2top = sb("w2top", [D, 2, D])
        w2bot = sb("w2bot", [D, 2, D])
        b2row = sb("b2row", [D1, 2, D])
        wT = sb("wT", [D, 4, D1])
        wt = sb("wt", [D1, 11, D])
        wmean = sb("wmean", [D1, 9])
        A0, B1, B2, B3, SELF1, NB1, MEANW, SOFTI, SOFTW, SELF0, NB0 = range(11)

        scat_i = sb("scat_i", [P, 2, SORT_COLS], I32)
        pay_i = sb("pay_i", [P, 2, SORT_COLS], I32)
        key_i = sb("key_i", [P, 2, SORT_COLS], I32)
        mapv = sb("mapv", [P, 2, SORT_COLS, 2])
        found = sb("found", [P, 2, TILES, 2])
        found_i = sb("found_i", [P, 2, TILES], I32)
        ndinv = sb("ndinv", [P, SORT_COLS])
        nrc = sb("nrc", [P, SORT_COLS])
        rcb = sb("rcb", [P, SORT_COLS])
        in_i = pay_i
        cnt_row = sb("cnt_row", [1, 2, SORT_COLS + 1])
        cnt_in = sb("cnt_in", [1, 4 * SORT_COLS])
        cnt_col = sb("cnt_col", [P, 4])

        DS = 4
        dX = [sb(f"dX{s}", [DP, DT * D]) for s in range(DS)]
        dXT = [sb(f"dXT{s}", [D1, DROWS]) for s in range(DS)]
        dst6 = [sb(f"dst6{s}", [DP, DT, 6]) for s in range(DS)]
        dsm = [sb(f"dsm{s}", [DP, 4, DT]) for s in range(DS)]

        def pair(name, shape, dt=F32):
            return [sb(f"{name}{b}", shape, dt) for b in range(2)]

        idx_a = pair("idx_a", [P, W], I32)
        idx_b = pair("idx_b", [P, W], I32)
        idx_s = pair("idx_s", [P, W], I32)
        idx_o = pair("idx_o", [P, W], I32)
        mrow = pair("mrow", [P, W, 2])
        GB = pair("GB", [P, W, D])
        RB = pair("RB", [P, W, D1])
        TB = pair("TB", [P, W, D])
        TH = pair("TH", [P, W, D])
        RH = pair("RH", [P, W, D1])
        AR = pair("AR", [P, W, D])
        OR = pair("OR", [P, W, D])
        eH = pair("eH", [P, W, D])
        eZ = pair("eZ", [P, W, D])
        est6 = [sb(f"est6{k}", [P, W, 6]) for k in range(4)]
        esm = [sb(f"esm{k}", [P, 4, W]) for k in range(4)]
        FL = pair("FL", [D1, GE])
        SC = pair("SC", [D1, GE])
        XT = [sb(f"XT{k}", [D1, GE]) for k in range(3)]
        MX = pair("MX", [P, GE + 1])
        DEN = pair("DEN", [P, GE])
        NUM = pair("NUM", [P, GE])
        MB = sb("MB", [P, GE])
        DEC = sb("DEC", [P, GE])
        EX = sb("EX", [P, GE])
        QQ = sb("QQ", [P, GE])
        MS = pair("MS", [P, GE])

        K = [DEN[0][:, 0:512], NUM[0][:, 0:512]]
        V = [DEN[1][:, 0:512], NUM[1][:, 0:512]]
        MASK = [MB[:, 0:512], DEC[:, 0:512]]
        DIF = EX[:, 0:512]
        KPREV, KNEXT, LOCAL, CPROD, CONT = QQ[:, 0:512], MS[0][:, 0:512], MX[0][:, 0:512], MX[1][:, 0:512], EX[:, 0:512]
        SIDX, CNT = MB[:, 0:512], DEC[:, 0:512]
        dA, dB, dC = ([*(sb(f"{name}{s}", [DP, DT * D]) for s in range(2)), *(t[0:DP, 0:DT * D] for t in held_)]
                      for name, held_ in (("dA", (MB, DEC)), ("dB", (EX, QQ)), ("dC", MX)))
        as_rows = lambda t: t[:, 0:W * D].rearrange("p (w d) -> p w d", d=D)
        eSQ = [sb("eSQ0", [P, W, D])[:], sb("eSQ1", [P, W, D])[:], as_rows(EX)]
        eQ = as_rows(QQ)
        fill = TH[0][0:DP, :, :].rearrange("p w d -> p (w d)")[:, 0:320]

        PS = [ctx.enter_context(nc.psum_tensor(f"PS{k}", [P, 1024], F32)) for k in range(4)]

        def rows_of(ps, p, tiles):
            return ps[0:p, 0:tiles * P].rearrange("p (t c) -> p t c", c=P)[:, :, 0:D]

        loaded_w = sem("loaded_w")
        loaded_e = sem("loaded_e")
        pool_init = sem("pool_init")
        filled = sem("filled")
        prep_v = sem("prep_v")
        prep_pe = sem("prep_pe")
        sort_step = sem("sort_step")
        switch_ready = sem("switch_ready")
        switched = sem("switched")
        v_back = sem("v_back")
        keys_out = sem("keys_out")
        keys_in = sem("keys_in")
        post_pe = sem("post_pe")
        idx_ready = sem("idx_ready")
        map_out = sem("map_out")

        d_ld = [Steps(sem(f"dense_loaded{s}"), 0, ["x"], 16) for s in range(DS)]
        d_sx = [Steps(sem(f"dense_x1_stored{s}"), CREDIT, ["x1"], 16) for s in range(DS)]
        d_so = [Steps(sem(f"dense_out_stored{s}"), CREDIT, ["out"], 16) for s in range(DS)]
        d_pe = [Steps(sem(f"dense_pe{s}"), CREDIT, ["xT", "mm", "x1T", "mm0", "h1T", "mm1", "x3T", "mm3"])
                for s in range(DS)]
        d_act = [Steps(sem(f"dense_act{s}"), CREDIT,
                       ["xT", "sq", "sd", "x1T", "sd1", "h1T", "sq2", "sd2", "sqz", "sdz", "x3T", "sqo", "sdo"])
                 for s in range(DS)]
        d_v = [Steps(sem(f"dense_v{s}"), CREDIT,
                     ["sum", "r", "x1", "bn", "dm", "m2", "dm2", "m2s", "r1", "h1", "sum2", "r2", "h2", "z",
                      "sumz", "rz", "x3", "sumo", "ro", "out"]) for s in range(DS)]
        BESIDE = 12
        ROUNDS4 = (N // DROWS - 3 * BESIDE) // DS
        assert ROUNDS4 * DS + BESIDE * 3 == N // DROWS
        ROUNDS_OF = [ROUNDS4 + (BESIDE if s < 3 else 0) for s in range(DS)]
        SLOTS = 31
        START4, START3 = (0, 19, 15, 3), (0, 16, 26)

        def dense_group(j, s, beside):
            return j * 3 + (s + ROUNDS4 * DS) if beside else j * DS + s

        def part(steps, low, high, shift):
            for at, action in steps:
                if low <= at < high:
                    yield at + shift
                    action()

        def dense_round(program, j, start, others=(), old=True, new=True):
            def stream(s, first):
                if old:
                    yield from part(program(j - 1, s), SLOTS - first, SLOTS, first - SLOTS)
                if new:
                    yield from part(program(j, s), 0, SLOTS - first, first)
            weave(*(stream(s, first) for s, first in enumerate(start)), *others)

        def dense_rounds(eng, program, begin, count, start, others=lambda i: ()):
            dense_round(program, begin, start, others(0), old=False)
            with eng.Fori(1, count) as i:
                dense_round(program, i + begin, start, others(i))
            dense_round(program, begin + count, start, new=False)

        dma_sems = {k: [sem(f"{k}_dma{b}") for b in range(2)] for k in ("ga", "gb", "sc", "so", "fl", "ld", "lr", "lt", "st", "su")}
        step_sems = {k: sem(f"{k}_steps") for k in ("idx", "sidx", "oidx", *(f"{e}{n}" for e in ("pe", "act", "v") for n in range(4)))}
        pool_dmas = ("ga", "gb", "sc", "so")
        reached = {k: 0 if k in pool_dmas else CREDIT for k in (*dma_sems, *step_sems)}

        class Round:
            def __init__(self, **lists):
                self.steps, self.dmas = {}, {}
                for k in step_sems:
                    self.steps[k] = Steps(step_sems[k], reached[k], lists.get(k, []))
                    reached[k] = self.steps[k].end(GROUPS)
                for k in dma_sems:
                    unit = 16 * (lists.get(k, 0))
                    self.dmas[k] = [Steps(q, reached[k], ["all"] if unit else [], unit) for q in dma_sems[k]]
                    reached[k] = self.dmas[k][0].end(PAIRS)
                self.idx, self.sidx, self.oidx = (self.steps[k] for k in ("idx", "sidx", "oidx"))
                self.pe, self.act, self.v = ([self.steps[f"{e}{n}"] for n in range(4)] for e in ("pe", "act", "v"))
                self.ga, self.gb, self.sc, self.so = (self.dmas[k] for k in pool_dmas)
                self.fl, self.ld, self.lr, self.lt, self.st, self.su = (
                    self.dmas[k] for k in ("fl", "ld", "lr", "lt", "st", "su"))

        map_put = [Round(idx=["a", "row"], sc=W), Round(idx=["a", "row"], so=W)]
        map_get = [Round(idx=["a"], ga=W), Round(idx=["a"], gb=W)]
        BN = ["bn", "dm", "m2", "dm2", "m2s", "r"]
        cheb = [
            Round(idx=["a"], ga=W, fl=1, st=2, pe0=["zT"], v2=["scaled"], v0=["scan"], pe1=["back"], v1=["u"]),
            Round(idx=["a"], ga=W, fl=1, st=2, pe0=["zT"], v0=["scan"], pe1=["back"], v1=["u"]),
            Round(idx=["a", "b"], sidx=["s"], oidx=["s"], ga=W, gb=W, fl=1, ld=2, sc=W, so=W,
                  pe0=["zT", "mix"], v0=["scan", "y"],
                  pe1=["xT", "self"], act1=["xT", "sq", "sd"], v1=["pre", "sum", "r", "x1"],
                  pe2=["x1T", "self", "h1T", "self1"], act2=["x1T", "sd1", "h1T", "sq", "sd"],
                  v2=[*BN, "h1", "sum", "r2", "h2", "z"],
                  pe3=["x3T", "out"], act3=["sqz", "sdz", "x3T", "sqo", "sdo"],
                  v3=["sumz", "rz", "x3", "sumo", "ro", "out"]),
        ]
        sage1 = Round(idx=["a", "b"], ga=W, gb=W, fl=1, st=3, su=1,
                      pe0=["rT", "agg"], act0=["agg"], v0=["scan"],
                      pe1=["tT", "self"], act1=["tT"], v1=["h"],
                      act2=["sd"], v2=[*BN, "h1"])
        sage2 = Round(idx=["a"], ga=W, fl=1, ld=1, lt=2, st=2, su=1,
                      pe0=["rT", "self"], act0=["rT"], v0=["h"],
                      pe1=["h1T", "agg"], act1=["sd", "agg"], v1=[*BN, "h1", "scan"],
                      pe2=["tT", "self"], act2=["tT", "sq", "sd"], v2=["h", "sum", "r", "h2", "z"],
                      act3=["sqz", "sdz"], v3=["sumz", "rz", "x2"])
        meanr = Round(idx=["a"], ga=W, fl=1, ld=1, lr=1, lt=1, st=2, su=1,
                      pe0=["rT", "self"], act0=["rT"], v0=["h"],
                      act1=["sq", "sd"], v1=["sum", "r", "h2", "z"],
                      pe2=["x2T", "agg"], act2=["sqz", "sdz"], v2=["sumz", "rz", "x2", "scan", "agg"],
                      act3=["sqz", "sdz"], v3=["z", "sumz", "rz", "x3"])
        softr = Round(idx=["a"], sidx=["s"], ga=W, fl=1, ld=1, lt=1, sc=W,
                      pe0=["x3T"], act0=["sqz", "sdz"], v0=["z", "sumz", "rz", "x3"],
                      act1=["dec", "ex"], v1=["m", "carry", "max", "kept", "less", "off", "dec", "q",
                                              "den", "num", "rec", "msg"],
                      pe2=["tT", "out"], act2=["tT", "sqo", "sdo"], v2=["sumo", "ro", "out"])

        def staged(eng, *stages):
            most = max(lag for _, lag in stages)
            lead = (most + 1) // 2

            def step(i, t, live):
                weave(*(program(i * 2 + (t - lag), (t - lag) % 2, i + (t - lag) // 2)
                        for program, lag in stages if live(lag)))

            for t in range(2 * lead):
                step(0, t, lambda lag: lag <= t)
            with eng.Fori(lead, PAIRS) as i:
                for t in range(2):
                    step(i, t, lambda lag: True)
            for t in range(most):
                step(PAIRS, t, lambda lag: lag > t)

        x_v = x.rearrange("(g p i) d -> g p (i d)", p=DP, i=DT)
        x1_v = x1_d.rearrange("(g p i) d -> g p (i d)", p=DP, i=DT)
        out_v = out.rearrange("(g p i) d -> g p (i d)", p=DP, i=DT)

        def group(view, g):
            return view[bass.ds(g, 1)].rearrange("g p f -> (g p) f")

        def table_group(table, g):
            v = table[0:EP].rearrange("(g i p) d -> g p i d", p=P, i=W)
            return v[bass.ds(g, 1)].rearrange("g p i d -> (g p) i d")

        def by_tile(t):
            return t[:, :].rearrange("p (t d) -> p t d", d=D)

        def spread(scale, p, tiles):
            return scale.unsqueeze(2).to_broadcast([p, tiles, D])

        def on(eng, steps, i, name, back=0):
            eng.wait_ge(steps.sem, steps.at(i, name, back))

        def credit(eng, kind, streams):
            for n in range(4):
                eng.sem_inc(step_sems[f"{kind}{n}"], CREDIT)
            for steps in streams:
                eng.sem_inc(steps.sem, CREDIT)

        def beside(i, *steps):
            for at, stage, b in steps:
                yield at
                stage(i * 2 + b, b, i)

        def first_round(eng, program, *steps):
            dense_rounds(eng, program, ROUNDS4, BESIDE, START3, lambda i: [beside(i, *steps)])
            with eng.Fori(BESIDE, PAIRS) as i:
                weave(beside(i, *steps))

        def finished(eng, r):
            for steps in r.steps.values():
                if steps.names:
                    eng.wait_ge(steps.sem, steps.end(GROUPS))
            for made in r.dmas.values():
                for q in made:
                    if q.names:
                        eng.wait_ge(q.sem, q.end(PAIRS))

        found_ready = sem("found_ready")
        MAP_Q = 160
        FILLS = 5 + 2 * (N // DP // MAP_Q) + 4
        SORTED = SORT_BITS * (SORT_BITS + 1) // 2 % 2
        POOL_INITS = 9
        WEIGHT_LOADS = 8 + 6
        post_v = sem("post_v")
        roots = sem("roots")
        held = sem("held")

        block = ctx.enter_context(nc.Block())

        @block.sync
        def _(sp):
            for q in (*(q for k in ("fl", "ld", "lr", "lt", "st", "su") for q in dma_sems[k]),
                      *(steps.sem for steps in (*d_sx, *d_so))):
                sp.sem_inc(q, CREDIT)
            sp.wait_ge(pool_init, 2)
            full, rest = E // P, E % P
            for side, (k, v) in enumerate(((src, dst), (dst, src))):
                for t, a in ((key_i, k), (pay_i, v)):
                    rows = a[0:full * P].rearrange("(r p) -> r p", p=P)
                    sp.dma_start(t[:, side, 0:P], rows[0:P, :]).then_inc(loaded_e, 16)
                    sp.dma_start(t[0:full - P, side, P:2 * P], rows[P:full, :]).then_inc(loaded_e, 16)
                    sp.dma_start(t[full - P:full - P + 1, side, P:P + rest],
                                 a[full * P:E].rearrange("(o p) -> o p", o=1)).then_inc(loaded_e, 16)
            for t, a in ((chebw, cheb_w.rearrange("k i o -> i k o")),
                         (w1b1[0:D], sage_w1.rearrange("k i o -> i k o")),
                         (w0b0[0:D], sage_w0.rearrange("k i o -> i k o")),
                         (w2top, sage_w2[:, 0:D, :].rearrange("k i o -> i k o")),
                         (w2bot, sage_w2[:, D:2 * D, :].rearrange("k i o -> i k o"))):
                sp.dma_start(t[:], a).then_inc(loaded_w, 16)
            for t, a in ((w1b1, sage_b1), (w0b0, sage_b0), (b2row, sage_b2)):
                sp.dma_start(t[D:D1], a.rearrange("(o k) f -> o k f", o=1)).then_inc(loaded_w, 16)
            sp.wait_ge(pool_init, 3)
            for n, w, b in ((MEANW, mean_w, mean_b), (SOFTI, soft_w, soft_b), (SOFTW, soft_w, None), (A0, None, cheb_b)):
                if w is not None:
                    sp.dma_start(wt[0:D, n, :], w).then_inc(loaded_w, 16)
                if b is not None:
                    sp.dma_start(wt[D:D1, n, :], b.rearrange("(o f) -> o f", o=1)).then_inc(loaded_w, 16)
            sp.wait_ge(pool_init, 6)
            for table in (*u_d, *agg_d):
                sp.dma_start(table[NONE_ROW:NONE_ROW + 1, :], zrow[:]).then_inc(filled, 16)
            for m in map_d:
                mv = m.rearrange("(c p q) t -> c p (q t)", p=DP, q=MAP_Q)
                for c in range(mv.shape[0]):
                    sp.dma_start(mv[c], fill).then_inc(filled, 16)
            for side in range(2):
                for at in (0, SORT + 1):
                    sp.dma_start(sorted_d[side:side + 1, at:at + 1], neg[:]).then_inc(filled, 16)
            shifted = lambda side, o: sorted_d[side, o:o + SORT].rearrange("(h q p) -> q h p", h=2, p=P)
            sp.wait_ge(keys_out, 1)
            sp.wait_ge(filled, 16 * FILLS)
            for side in range(2):
                sp.dma_start(shifted(side, 1), K[SORTED][:, side * 256:side * 256 + 256]
                             .rearrange("q (h p) -> q h p", h=2)).then_inc(keys_in, 16)
            sp.wait_ge(keys_in, 32)
            for side in range(2):
                for o, t in ((0, KPREV), (2, KNEXT)):
                    sp.dma_start(t[:, side * 256:side * 256 + 256].rearrange("q (h p) -> q h p", h=2),
                                 shifted(side, o)).then_inc(keys_in, 16)
            sp.wait_ge(keys_out, 2)
            for side in range(2):
                sp.dma_start(cont_d[side].rearrange("(h q p) -> q h p", h=2, p=P),
                             CONT[:, side * 256:side * 256 + 256].rearrange("q (h p) -> q h p", h=2)).then_inc(keys_in, 16)
            sp.wait_ge(keys_in, 16 * 8)

            def load_rows(j, g, s):
                on(sp, d_pe[s], j, "xT", back=1)
                sp.dma_start(dX[s][:], group(x_v, g)).then_inc(d_ld[s].sem, 16)

            def dense_io(base, beside, more):
                def program(j, s):
                    g = dense_group(j - base, s, beside)

                    def store(step, steps, view):
                        on(sp, d_v[s], j, step)
                        sp.dma_start(group(view, g), dA[s][:, :]).then_inc(steps.sem, 16)

                    load = lambda: load_rows(j + 1, dense_group(j + (1 - base), s, beside), s)
                    return [*([(1, load)] if more else []), (7, lambda: store("x1", d_sx[s], x1_v)),
                            (30, lambda: store("out", d_so[s], out_v))]
                return program

            for s in range(DS):
                load_rows(0, dense_group(0, s, False), s)
            def flags(r, side, stage, name):
                def load(g, b, i):
                    on(sp, r.v[stage], g, name, back=2)
                    sp.dma_start(FL[b][:], cont_d[side:side + 1, bass.ds(g * GE, GE)].to_broadcast([D1, GE])
                                 ).then_inc(r.fl[b].sem, 16)
                    yield
                return load

            def dense_rounds_io(begin, count, start, beside, others=lambda i: ()):
                program, last = dense_io(begin, beside, True), dense_io(begin, beside, False)
                dense_round(program, begin, start, others(0), old=False)
                with sp.Fori(1, count - 1) as i:
                    dense_round(program, i + begin, start, others(i))
                dense_round(last, begin + count - 1, start, others(count - 1))
                dense_round(last, begin + count, start, new=False)

            dense_rounds_io(0, ROUNDS4, START4, False)
            for s in range(3):
                load_rows(ROUNDS4, dense_group(0, s, True), s)

            for k, r in enumerate(cheb[:2]):
                def store_sums(g, b, i, r=r, k=k):
                    on(sp, r.v[0], g, "scan")
                    sp.dma_start(sT_d[k][:, bass.ds(g * GE, GE)], SC[b][0:D, :]).then_inc(r.st[b].sem, 16)

                def store_table(g, b, i, r=r, k=k):
                    on(sp, r.v[1], g, "u")
                    sp.dma_start(table_group(u_d[k], g), OR[b][:]).then_inc(r.st[b].sem, 16)

                def next_flags(g, b, i, r=r):
                    weave(flags(r, 0, 0, "scan")(g + 2, b, i))

                if k:
                    staged(sp, (flags(r, 0, 0, "scan"), 0), (store_sums, 2), (store_table, 2))
                else:
                    for b in range(2):
                        next_flags(b - 2, b, 0)
                    steps = [(5, store_sums, 0), (6, next_flags, 0), (9, store_table, 0),
                             (20, store_sums, 1), (21, next_flags, 1), (24, store_table, 1)]
                    dense_rounds_io(ROUNDS4, BESIDE, START3, True, lambda i: [beside(i, *steps)])
                    with sp.Fori(BESIDE, PAIRS - 1) as i:
                        weave(beside(i, *steps))
                    weave(beside(PAIRS - 1, *(step for step in steps if step[1] is not next_flags)))
                finished(sp, r)
            r = cheb[2]

            def load(g, b, i, r=r):
                on(sp, r.pe[0], g, "mix", back=2)
                for k, t in enumerate((DEN, NUM)):
                    sp.dma_start(t[b][0:D, :], sT_d[k][:, bass.ds(g * GE, GE)]).then_inc(r.ld[b].sem, 16)
                yield
            staged(sp, (flags(r, 0, 0, "scan"), 0), (load, 0))
            finished(sp, r)

            r = sage1

            def store_r(g, b, i, r=r):
                on(sp, r.ga[b], i, "all")
                sp.dma_start(group(r_d[0], g), RB[b][:, :, 0:D]).then_inc(r.st[b].sem, 16)
                yield
                on(sp, r.gb[b], i, "all")
                sp.dma_start(group(t_d[0], g), TB[b][:]).then_inc(r.st[b].sem, 16)
                yield
                on(sp, r.act[0], g, "agg")
                sp.dma_start(table_group(agg_d[0], g), AR[b][:]).then_inc(r.st[b].sem, 16)
                yield
                on(sp, r.v[2], g, "h1")
                sp.dma_start(group(t_d[1], g), TH[b][:]).then_inc(r.su[b].sem, 16)
            staged(sp, (flags(r, 1, 0, "scan"), 0), (store_r, 2))

            finished(sp, sage1)
            r = sage2

            def load(g, b, i, r=r):
                on(sp, r.pe[0], g, "rT", back=2)
                sp.dma_start(RB[b][:, :, 0:D], group(r_d[0], g)).then_inc(r.ld[b].sem, 16)
                yield

            def load_t(g, b, i, r=r):
                on(sp, r.v[2], g, "z", back=2)
                sp.dma_start(TB[b][:], group(t_d[0], g)).then_inc(r.lt[b].sem, 16)
                sp.dma_start(TH[b][:], group(t_d[1], g)).then_inc(r.lt[b].sem, 16)
                yield

            def store(g, b, i, r=r):
                on(sp, r.v[1], g, "h1")
                sp.dma_start(group(r_d[1], g), RH[b][:, :, 0:D]).then_inc(r.st[b].sem, 16)
                on(sp, r.act[1], g, "agg")
                sp.dma_start(table_group(agg_d[1], g), AR[b][:]).then_inc(r.st[b].sem, 16)
                yield

            def store_t(g, b, i, r=r):
                on(sp, r.v[3], g, "x2")
                sp.dma_start(group(t_d[2], g), OR[b][:]).then_inc(r.su[b].sem, 16)
                yield
            staged(sp, (load, 0), (flags(r, 1, 1, "scan"), 1), (load_t, 2), (store, 3), (store_t, 5))

            finished(sp, sage2)
            r = meanr

            def load(g, b, i, r=r):
                on(sp, r.pe[0], g, "rT", back=2)
                sp.dma_start(TH[b][:], group(r_d[1], g)).then_inc(r.ld[b].sem, 16)
                yield

            def load_r(g, b, i, r=r):
                on(sp, r.v[1], g, "z", back=2)
                sp.dma_start(RB[b][:, :, 0:D], group(r_d[0], g)).then_inc(r.lr[b].sem, 16)
                yield

            def load_t(g, b, i, r=r):
                on(sp, r.v[3], g, "z", back=2)
                sp.dma_start(TB[b][:], group(t_d[2], g)).then_inc(r.lt[b].sem, 16)
                yield

            def store(g, b, i, r=r):
                on(sp, r.v[2], g, "x2")
                sp.dma_start(group(r_d[2], g), RH[b][:, :, 0:D]).then_inc(r.st[b].sem, 16)
                on(sp, r.v[2], g, "agg")
                sp.dma_start(table_group(agg_d[2], g), AR[b][:]).then_inc(r.st[b].sem, 16)
                yield

            def store_t(g, b, i, r=r):
                on(sp, r.v[3], g, "x3")
                sp.dma_start(group(t_d[3], g), OR[b][:]).then_inc(r.su[b].sem, 16)
                yield
            staged(sp, (load, 0), (load_r, 1), (flags(r, 1, 2, "scan"), 2), (load_t, 3), (store, 4), (store_t, 5))

            finished(sp, meanr)
            r = softr

            def load(g, b, i, r=r):
                on(sp, r.v[0], g, "z", back=2)
                sp.dma_start(RB[b][:, :, 0:D], group(r_d[2], g)).then_inc(r.ld[b].sem, 16)
                yield

            def load_t(g, b, i, r=r):
                on(sp, r.pe[2], g, "tT", back=2)
                sp.dma_start(TB[b][:], group(t_d[3], g)).then_inc(r.lt[b].sem, 16)
                yield
            staged(sp, (load, 0), (flags(r, 1, 1, "dec"), 1), (load_t, 2))
            for b in range(2):
                sp.wait_ge(r.sc[b].sem, r.sc[b].end(PAIRS))

        @block.gpsimd
        def _(gp):
            gp.sem_inc(step_sems["idx"], CREDIT)
            gp.sem_inc(step_sems["sidx"], CREDIT)
            gp.sem_inc(step_sems["oidx"], CREDIT)
            gp.memset(key_i[:], N).then_inc(pool_init, 1)
            gp.memset(pay_i[:], 0).then_inc(pool_init, 1)
            gp.memset(wt[:], 0.0).then_inc(pool_init, 1)
            gp.memset(zrow[:], 0.0)
            gp.memset(neg[:], -1.0).then_inc(pool_init, 1)
            fv = fill.rearrange("p (q t) -> p q t", t=2)
            gp.memset(fv[:, :, 0], float(NONE_ROW)).then_inc(pool_init, 1)
            gp.memset(fv[:, :, 1], 0.0).then_inc(pool_init, 1)
            gp.memset(ident[:], 0.0).then_inc(pool_init, 1)
            gp.iota(pos_i[:], pattern=[[P, SORT_COLS]], base=0, channel_multiplier=1).then_inc(pool_init, 1)
            gp.wait_ge(pool_init, 8)
            gp.affine_select(out=ident[:], in_=ident[:], compare_op=ALU.not_equal, fill=1.0, base=0,
                             pattern=[[-1, P]], channel_multiplier=1).then_inc(pool_init, 1)

            last_node = gp.to_reg(N - 1)

            def hold(*conditions):
                for steps, i, name, back in conditions:
                    on(gp, steps, i, name, back)
                gp.sem_inc(held, 1)

            def cols(t, side, g):
                return t[:, side, bass.ds(g * W, W)]

            def copy_idx(steps, name, to, columns, dmas, i, b, first=False):
                if not first:
                    on(gp, dmas[b], i, "all", back=1)
                steps.done(gp.tensor_copy(to[b][:], columns), name)

            gp.wait_ge(idx_ready, 1)
            gp.wait_ge(filled, 16 * FILLS)

            def put_map(side, i, first=False):
                r = map_put[side]
                dmas = (r.sc, r.so)[side]
                for b in range(2):
                    g = i * 2 + b
                    copy_idx(r.idx, "a", idx_a, cols(scat_i, side, g), dmas, i, b, first)
                    r.idx.done(gp.tensor_copy(mrow[b][:], mapv[:, side, bass.ds(g * W, W), :]), "row")
                    hold((r.idx, g, "row", 0))
                    for w in range(W):
                        gp.indirect_dma_start(
                            out=map_d[side], out_offset=bass.IndirectOffsetOnAxis(ap=idx_a[b][:, w:w + 1], axis=0),
                            in_=mrow[b][:, w, :], in_offset=None, bounds_check=last_node, oob_is_err=False,
                        ).then_inc(dmas[b].sem, 16)

            for side in range(2):
                if side:
                    finished(gp, map_put[0])
                put_map(side, 0, first=True)
                with gp.Fori(1, PAIRS) as i:
                    put_map(side, i)
            finished(gp, map_put[1])
            for side, r in enumerate(map_get):
                dmas = (r.ga, r.gb)[side]

                def fetch(i, b, side=side, r=r, dmas=dmas):
                    g = i * 2 + b
                    r.idx.done(gp.tensor_copy(idx_a[b][:], cols(pay_i, side, g)), "a")
                    hold((r.idx, g, "a", 0))
                    for w in range(W):
                        gp.indirect_dma_start(
                            out=mrow[b][:, w, :], out_offset=None, in_=map_d[side],
                            in_offset=bass.IndirectOffsetOnAxis(ap=idx_a[b][:, w:w + 1], axis=0),
                        ).then_inc(dmas[b].sem, 16)

                def keep(i, b, side=side, dmas=dmas):
                    on(gp, dmas[b], i, "all")
                    gp.tensor_copy(found[:, side, bass.ds((i * 2 + b) * W, W), :], mrow[b][:]).then_inc(map_out, 1)

                for b in range(2):
                    if side:
                        gp.wait_ge(map_out, GROUPS)
                    fetch(0, b)
                with gp.Fori(0, PAIRS - 1) as i:
                    for b in range(2):
                        keep(i, b)
                        gp.wait_ge(map_out, i * 2 + (b + 1 + side * GROUPS))
                        fetch(i + 1, b)
                for b in range(2):
                    keep(PAIRS - 1, b)

            def gather(r, key, b, to, table, idx):
                for w in range(W):
                    gp.indirect_dma_start(out=to[b][:, w, 0:D], out_offset=None, in_=table,
                                          in_offset=bass.IndirectOffsetOnAxis(ap=idx[b][:, w:w + 1], axis=0),
                                          ).then_inc(r.dmas[key][b].sem, 16)

            def scatter(dmas, b, table, rows, idx):
                for w in range(W):
                    gp.indirect_dma_start(out=table, out_offset=bass.IndirectOffsetOnAxis(ap=idx[b][:, w:w + 1], axis=0),
                                          in_=rows[b][:, w, :], in_offset=None, bounds_check=last_node, oob_is_err=False,
                                          ).then_inc(dmas[b].sem, 16)

            found_rows = lambda side, g: found_i[:, side, bass.ds(g * W, W)]

            for k, r in enumerate(cheb[:2]):
                if k:
                    gp.wait_ge(found_ready, 1)
                with gp.Fori(0, PAIRS) as i:
                    for b in range(2):
                        g = i * 2 + b
                        copy_idx(r.idx, "a", idx_a, found_rows(0, g) if k else cols(pay_i, 0, g), r.ga, i, b)
                        hold((r.pe[0], g, "zT", 2), (r.idx, g, "a", 0))
                        gather(r, "ga", b, GB, u_d[k - 1] if k else x, idx_a)
                finished(gp, r)
            for s in range(DS):
                gp.wait_ge(d_sx[s].sem, d_sx[s].end(ROUNDS_OF[s]))
                gp.wait_ge(d_so[s].sem, d_so[s].end(ROUNDS_OF[s]))
            r = cheb[2]

            def fetch(g, b, i, r=r):
                copy_idx(r.idx, "a", idx_a, found_rows(0, g), r.ga, i, b)
                copy_idx(r.idx, "b", idx_b, cols(key_i, 0, g), r.gb, i, b)
                hold((r.pe[0], g, "zT", 2), (r.idx, g, "b", 0))
                gather(r, "ga", b, GB, u_d[1], idx_a)
                hold((r.pe[1], g, "xT", 2))
                gather(r, "gb", b, RB, x, idx_b)
                yield

            def put_x1(g, b, i, r=r):
                copy_idx(r.sidx, "s", idx_s, cols(scat_i, 0, g), r.sc, i, b)
                hold((r.v[1], g, "x1", 0), (r.sidx, g, "s", 0))
                scatter(r.sc, b, x1_d, OR, idx_s)
                yield

            def put_out(g, b, i, r=r, first=False):
                copy_idx(r.oidx, "s", idx_o, cols(scat_i, 0, g), r.so, i, b, first)
                hold((r.v[3], g, "out", 0), (r.oidx, g, "s", 0))
                scatter(r.so, b, out, AR, idx_o)
                yield
            staged(gp, (fetch, 0), (put_x1, 3), (put_out, 5))
            finished(gp, r)

            r = sage1
            with gp.Fori(0, PAIRS) as i:
                for b in range(2):
                    g = i * 2 + b
                    copy_idx(r.idx, "a", idx_a, cols(pay_i, 1, g), r.ga, i, b)
                    copy_idx(r.idx, "b", idx_b, cols(key_i, 1, g), r.gb, i, b)
                    hold((r.pe[0], g, "rT", 2), (r.st[b], i, "all", 1), (r.idx, g, "b", 0))
                    gather(r, "ga", b, RB, x1_d, idx_a)
                    hold((r.pe[1], g, "tT", 2))
                    gather(r, "gb", b, TB, x1_d, idx_b)
            finished(gp, r)
            for r, table in ((sage2, agg_d[0]), (meanr, agg_d[1])):
                with gp.Fori(0, PAIRS) as i:
                    for b in range(2):
                        g = i * 2 + b
                        copy_idx(r.idx, "a", idx_a, found_rows(1, g), r.ga, i, b)
                        hold((r.v[0], g, "h", 2), (r.idx, g, "a", 0))
                        gather(r, "ga", b, GB, table, idx_a)
                finished(gp, r)
            r = softr

            def fetch(g, b, i, r=r):
                copy_idx(r.idx, "a", idx_a, found_rows(1, g), r.ga, i, b)
                hold((r.v[0], g, "z", 2), (r.idx, g, "a", 0))
                gather(r, "ga", b, GB, agg_d[2], idx_a)
                yield

            def put_out(g, b, i, r=r):
                copy_idx(r.sidx, "s", idx_s, cols(scat_i, 1, g), r.sc, i, b)
                hold((r.v[2], g, "out", 0), (r.sidx, g, "s", 0))
                scatter(r.sc, b, out, OR, idx_s)
                yield
            staged(gp, (fetch, 0), (put_out, 4))

        def sort_plan():
            for k in range(1, SORT_BITS + 1):
                if k <= 6:
                    yield ("flip", k - 1 if k > 1 else None, k)
                else:
                    if k == 7:
                        yield ("flip", 6, None)
                    yield ("switch",)
                    yield ("flip", k - 8 if k > 7 else None, k - 7 if k < SORT_BITS else None)
                    for j in range(k - 8, -1, -1):
                        yield ("step", 1 << j)
                    yield ("switch",)
                for j in range(min(k, 7) - 1, -1, -1):
                    yield ("step", 1 << j)

        @block.tensor
        def _(pe):
            credit(pe, "pe", d_pe)
            pe.wait_ge(pool_init, POOL_INITS)
            pe.wait_ge(loaded_w, 16 * WEIGHT_LOADS)
            for q, t in enumerate((w1b1[:, 0], w1b1[:, 1], w0b0[:, 0], w0b0[:, 1])):
                last = pe.transpose(PS[0][0:D, q * P:q * P + D1], t, ident[0:D1, 0:D1])
            last.then_inc(prep_pe, 1)
            pe.wait_ge(prep_v, 1)
            for q, t in enumerate((w2top[:, 0], w2top[:, 1], w2bot[:, 0], w2bot[:, 1])):
                last = pe.matmul(PS[1][0:D1, q * P:q * P + D], wT[:, q, :], t, start=True, stop=True)
            last.then_inc(prep_pe, 1)
            pe.wait_ge(prep_v, 2)
            cur = n = 0
            for op in sort_plan():
                if op[0] == "step":
                    cur ^= 1
                if op[0] != "switch":
                    continue
                n += 1
                pe.wait_ge(switch_ready, n)
                for ps, t in ((PS[0], K[cur]), (PS[1], V[cur])):
                    for q in range(4):
                        last = pe.transpose(ps[:, q * P:(q + 1) * P], t[:, q * P:(q + 1) * P], ident[:])
                    last.then_inc(switched, 1)
                cur ^= 1
            pe.wait_ge(post_v, 1)
            for k, t in enumerate((LOCAL, CPROD)):
                for q in range(4):
                    last = pe.matmul(PS[2][0:1, (4 * k + q) * P:(4 * k + q + 1) * P], t[:, q * P + P - 1:q * P + P],
                                     ident[:], start=True, stop=True)
            last.then_inc(post_pe, 1)
            pe.wait_ge(post_v, 2)
            for q in range(4):
                last = pe.matmul(PS[3][:, q:q + 1], cnt_row[0:1, q // 2, (q % 2) * P:(q % 2 + 1) * P], one[:],
                                 start=True, stop=True)
            last.then_inc(post_pe, 1)
            pe.wait_ge(post_v, 3)
            for k, t in enumerate((SIDX, V[SORTED], K[SORTED], CNT)):
                for q in range(4):
                    last = pe.transpose(PS[k // 2][:, (k % 2) * 512 + q * P:(k % 2) * 512 + (q + 1) * P],
                                        t[:, q * P:(q + 1) * P], ident[:])
            last.then_inc(post_pe, 1)
            pe.wait_ge(idx_ready, 1)

            def transposed(ps, t, tiles=W, p=P, width=D):
                for i in range(tiles):
                    last = pe.transpose(ps[0:width, i * P:i * P + p], t(i), ident[0:p, 0:p])
                return last

            def times(ps, parts, tiles=W, p=P):
                for i in range(tiles):
                    for k, (t, w) in enumerate(parts):
                        last = pe.matmul(ps[0:p, i * P:i * P + D], t(i), w, start=k == 0, stop=k == len(parts) - 1)
                return last

            columns = lambda t: lambda i: t[:, i * D:(i + 1) * D]
            columns_T = lambda t: lambda i: t[:, i * DP:(i + 1) * DP]
            tile = lambda t, width=D: lambda i: t[:, i, 0:width]
            tile_T = lambda t, rows=D1: lambda i: t[0:rows, i * P:(i + 1) * P]
            w97 = lambda n: wt[:, n, :]
            w96 = lambda n: wt[0:D, n, :]

            def dense(j, s):
                ps, v, a = PS[(s + 1) % DS], d_v[s], d_act[s]

                def turned(rows, name):
                    d_pe[s].done(transposed(ps, columns(rows[s]), DT, DP), name)

                def x_turned():
                    on(pe, d_ld[s], j, "x")
                    on(pe, v, j, "out", back=1)
                    turned(dX, "xT")

                def made(step, rows, name):
                    on(pe, v, j, step)
                    turned(rows, name)

                def product(turned_name, w, name):
                    on(pe, a, j, turned_name)
                    d_pe[s].done(times(ps, [(columns_T(dXT[s]), w97(w))], DT, DP), name)

                return [(0, x_turned), (2, lambda: product("xT", A0, "mm")),
                        (7, lambda: made("x1", dA, "x1T")), (9, lambda: product("x1T", SELF0, "mm0")),
                        (13, lambda: made("h1", dC, "h1T")), (15, lambda: product("h1T", SELF1, "mm1")),
                        (24, lambda: made("x3", dC, "x3T")), (26, lambda: product("x3T", SOFTI, "mm3"))]

            dense_rounds(pe, dense, 0, ROUNDS4, START4)

            for k, r in enumerate(cheb[:2]):
                def sums(g, b, i, k=k, r=r):
                    if k == 0:
                        on(pe, r.v[2], g, "scaled")
                    else:
                        on(pe, r.ga[b], i, "all")
                    on(pe, r.v[1], g, "u", back=2 if k else 1)
                    r.pe[0].done(transposed(PS[b if k else 0], tile(GB[b])), "zT")

                def back(g, b, i, k=k, r=r):
                    on(pe, r.v[0], g, "scan")
                    for t in range(W):
                        last = pe.transpose(PS[b if k else 0][:, t * P:t * P + D], SC[b][0:D, t * P:(t + 1) * P], ident[0:D, 0:D])
                    r.pe[1].done(last, "back")

                if k:
                    staged(pe, (sums, 0), (back, 1))
                else:
                    first_round(pe, dense, (2, sums, 0), (6, back, 0), (17, sums, 1), (21, back, 1))
                finished(pe, r)
            r = cheb[2]

            def mix(g, b, i, r=r):
                on(pe, r.ga[b], i, "all")
                on(pe, r.v[0], g, "y", back=1)
                r.pe[0].done(transposed(PS[0], tile(GB[b])), "zT")
                yield
                on(pe, r.v[0], g, "scan")
                on(pe, r.ld[b], i, "all")
                r.pe[0].done(times(PS[0], [(tile_T(DEN[b], D), w96(B1)), (tile_T(NUM[b], D), w96(B2)),
                                           (tile_T(SC[b], D), w96(B3))]), "mix")
                yield

            def own(g, b, i, r=r):
                on(pe, r.gb[b], i, "all")
                on(pe, r.v[1], g, "pre", back=1)
                r.pe[1].done(transposed(PS[1], tile(RB[b])), "xT")
                yield
                on(pe, r.act[1], g, "xT")
                r.pe[1].done(times(PS[1], [(tile_T(XT[0]), w97(A0))]), "self")
                yield

            def depths(g, b, i, r=r):
                on(pe, r.v[1], g, "x1")
                on(pe, r.v[2], g, "h2", back=1)
                r.pe[2].done(transposed(PS[2], tile(OR[b])), "x1T")
                yield
                on(pe, r.act[2], g, "x1T")
                r.pe[2].done(times(PS[2], [(tile_T(XT[1]), w97(SELF0))]), "self")
                yield 3
                on(pe, r.v[2], g, "h1")
                r.pe[2].done(transposed(PS[2], tile(eH[1])), "h1T")
                yield
                on(pe, r.act[2], g, "h1T")
                r.pe[2].done(times(PS[2], [(tile_T(XT[1]), w97(SELF1))]), "self1")
                yield

            def last(g, b, i, r=r):
                yield 2
                on(pe, r.v[3], g, "x3")
                on(pe, r.v[3], g, "out", back=1)
                r.pe[3].done(transposed(PS[3], tile(eQ)), "x3T")
                yield
                on(pe, r.act[3], g, "x3T")
                r.pe[3].done(times(PS[3], [(tile_T(XT[2]), w97(SOFTI))]), "out")
                yield
            staged(pe, (mix, 0), (own, 1), (depths, 2), (last, 3))
            finished(pe, r)

            r = sage1

            def src_rows(g, b, i, r=r):
                on(pe, r.ga[b], i, "all")
                on(pe, r.act[0], g, "agg", back=2)
                r.pe[0].done(transposed(PS[b], tile(RB[b], D1), width=D1), "rT")
                yield
                on(pe, r.v[0], g, "scan")
                r.pe[0].done(times(PS[b], [(tile_T(SC[b]), w97(NB0))]), "agg")
                yield

            def dst_rows(g, b, i, r=r):
                on(pe, r.gb[b], i, "all")
                on(pe, r.v[1], g, "h", back=2)
                r.pe[1].done(transposed(PS[2 + b], tile(TB[b])), "tT")
                yield
                on(pe, r.act[1], g, "tT")
                r.pe[1].done(times(PS[2 + b], [(tile_T(XT[1]), w97(SELF0))]), "self")
                yield
            staged(pe, (src_rows, 0), (dst_rows, 0))
            finished(pe, r)

            r = sage2

            def src_self(g, b, i, r=r):
                on(pe, r.ld[b], i, "all")
                on(pe, r.v[0], g, "h", back=1)
                r.pe[0].done(transposed(PS[0], tile(RB[b])), "rT")
                yield
                on(pe, r.act[0], g, "rT")
                r.pe[0].done(times(PS[0], [(tile_T(XT[0]), w97(SELF0))]), "self")
                yield

            def src_agg(g, b, i, r=r):
                yield 2
                on(pe, r.v[1], g, "h1")
                on(pe, r.act[1], g, "agg", back=1)
                r.pe[1].done(transposed(PS[1], tile(RH[b], D1), width=D1), "h1T")
                yield
                on(pe, r.v[1], g, "scan")
                r.pe[1].done(times(PS[1], [(tile_T(SC[b]), w97(NB1))]), "agg")
                yield

            def dst_self(g, b, i, r=r):
                on(pe, r.lt[b], i, "all")
                on(pe, r.v[2], g, "h", back=1)
                r.pe[2].done(transposed(PS[2], tile(TH[b])), "tT")
                yield
                on(pe, r.act[2], g, "tT")
                r.pe[2].done(times(PS[2], [(tile_T(XT[1]), w97(SELF1))]), "self")
                yield
            staged(pe, (src_self, 0), (src_agg, 1), (dst_self, 2))
            finished(pe, r)

            r = meanr

            def src_self(g, b, i, r=r):
                on(pe, r.ld[b], i, "all")
                on(pe, r.v[0], g, "h", back=1)
                r.pe[0].done(transposed(PS[0], tile(TH[b])), "rT")
                yield
                on(pe, r.act[0], g, "rT")
                r.pe[0].done(times(PS[0], [(tile_T(XT[0]), w97(SELF1))]), "self")
                yield

            def src_agg(g, b, i, r=r):
                yield 2
                on(pe, r.v[2], g, "x2")
                on(pe, r.v[2], g, "agg", back=1)
                r.pe[2].done(transposed(PS[1], tile(RH[b], D1), width=D1), "x2T")
                yield
                on(pe, r.v[2], g, "scan")
                r.pe[2].done(times(PS[1], [(tile_T(SC[b]), w97(MEANW))]), "agg")
                yield
            staged(pe, (src_self, 0), (src_agg, 2))
            finished(pe, r)

            r = softr

            def src_T(g, b, i, r=r):
                yield 3
                on(pe, r.v[0], g, "x3")
                on(pe, r.v[1], g, "m", back=2)
                r.pe[0].done(transposed(PS[b], tile(eH[b])), "x3T")
                yield

            def dst_out(g, b, i, r=r):
                on(pe, r.lt[b], i, "all")
                on(pe, r.v[2], g, "out", back=1)
                r.pe[2].done(transposed(PS[2], tile(TB[b])), "tT")
                yield
                on(pe, r.act[2], g, "tT")
                on(pe, r.v[1], g, "msg")
                r.pe[2].done(times(PS[2], [(tile_T(XT[1]), w97(SOFTI)), (tile_T(MS[b], D), w96(SOFTW))]), "out")
                yield
            staged(pe, (src_T, 0), (dst_out, 2))

        @block.scalar
        def _(act):
            credit(act, "act", d_act)
            cur = n = 0
            for op in sort_plan():
                if op[0] == "step":
                    cur ^= 1
                if op[0] != "switch":
                    continue
                n += 1
                cur ^= 1
                act.wait_ge(switched, 2 * n)
                act.copy(V[cur], PS[1][:, 0:512]).then_inc(v_back, 1)

            act.wait_ge(post_v, 4)
            act.activation(MX[1][:, 0:512], PS[1][:, 512:1024], ACT.Sqrt).then_inc(roots, 1)

            LN = float(D) ** -0.5
            STD = float(D - 1) ** -0.5

            def from_T(out, ps):
                return act.copy(out[0:D, :].rearrange("f (t c) -> f t c", c=DP),
                                ps[0:D, :].rearrange("f (t c) -> f t c", c=P)[:, :, 0:DP])

            def square(out, in_, scale):
                return act.activation(out, in_, ACT.Square, scale=scale)

            def deviation(m, p, scale=1.0, bias=0.0):
                return act.activation(m[:, 3, :], m[:, 0, :], ACT.Sqrt, scale=scale, bias=bias)

            eps_ = eps[:, :]
            act.wait_ge(idx_ready, 1)

            def plain_std(m):
                return act.activation(m[:, 3, :], m[:, 2, :], ACT.Sqrt, scale=1.0 / (D - 1))

            def dense(j, s):
                ps, pe_, v, m, a = PS[(s + 1) % DS], d_pe[s], d_v[s], dsm[s], d_act[s]
                rows = rows_of(ps, DP, DT)

                def turned(name):
                    on(act, pe_, j, name)
                    a.done(from_T(dXT[s], ps), name)

                def squares(after, step, out, rows, scale, name):
                    on(act, after, j, step)
                    a.done(square(out, rows, scale), name)

                def root(step, name, make):
                    on(act, v, j, step)
                    a.done(make(), name)

                B, e = by_tile(dB[s]), eps[0:DP, :]
                return [(1, lambda: turned("xT")), (3, lambda: squares(pe_, "mm", B, rows, LN, "sq")),
                        (5, lambda: root("sum", "sd", lambda: deviation(m, DP, 1.0, e))),
                        (8, lambda: turned("x1T")), (11, lambda: root("m2s", "sd1", lambda: plain_std(m))),
                        (14, lambda: turned("h1T")), (16, lambda: squares(pe_, "mm1", B, rows, STD, "sq2")),
                        (18, lambda: root("sum2", "sd2", lambda: deviation(m, DP))),
                        (20, lambda: squares(v, "z", dC[s][:, :], dB[s][:, :], LN, "sqz")),
                        (22, lambda: root("sumz", "sdz", lambda: deviation(m, DP, 1.0 + LN_EPS, eps2[0:DP, :]))),
                        (25, lambda: turned("x3T")), (27, lambda: squares(pe_, "mm3", B, rows, LN, "sqo")),
                        (29, lambda: root("sumo", "sdo", lambda: deviation(m, DP, 1.0, e)))]

            dense_rounds(act, dense, 0, ROUNDS4, START4)
            dense_rounds(act, dense, ROUNDS4, BESIDE, START3)
            finished(act, cheb[1])

            r = cheb[2]

            def own(g, b, i, r=r):
                on(act, r.pe[1], g, "xT")
                on(act, r.pe[1], g, "self", back=1)
                r.act[1].done(act.copy(XT[0][0:D, :], PS[1][0:D, 0:GE]), "xT")
                yield 2
                on(act, r.v[1], g, "pre")
                on(act, r.v[1], g, "sum", back=1)
                r.act[1].done(square(eSQ[0], eH[0][:], LN), "sq")
                yield
                on(act, r.v[1], g, "sum")
                r.act[1].done(deviation(esm[1], P, 1.0, eps_), "sd")
                yield

            def depths(g, b, i, r=r):
                on(act, r.pe[2], g, "x1T")
                on(act, r.pe[2], g, "self1", back=1)
                r.act[2].done(act.copy(XT[1][0:D, :], PS[2][0:D, 0:GE]), "x1T")
                yield 2
                on(act, r.v[2], g, "m2s")
                r.act[2].done(plain_std(esm[2]), "sd1")
                yield
                on(act, r.pe[2], g, "h1T")
                r.act[2].done(act.copy(XT[1][0:D, :], PS[2][0:D, 0:GE]), "h1T")
                yield
                on(act, r.pe[2], g, "self1")
                on(act, r.v[2], g, "sum", back=1)
                r.act[2].done(square(eSQ[1], rows_of(PS[2], P, W), STD), "sq")
                yield
                on(act, r.v[2], g, "sum")
                r.act[2].done(deviation(esm[2], P), "sd")
                yield

            def last(g, b, i, r=r):
                on(act, r.v[2], g, "z")
                on(act, r.v[3], g, "sumo", back=1)
                r.act[3].done(square(eSQ[2], eZ[b][:], LN), "sqz")
                yield
                on(act, r.v[3], g, "sumz")
                r.act[3].done(deviation(esm[3], P, 1.0 + LN_EPS, eps2[:, :]), "sdz")
                yield
                on(act, r.pe[3], g, "x3T")
                on(act, r.pe[3], g, "out", back=1)
                r.act[3].done(act.copy(XT[2][0:D, :], PS[3][0:D, 0:GE]), "x3T")
                yield
                on(act, r.pe[3], g, "out")
                r.act[3].done(square(eSQ[2], rows_of(PS[3], P, W), LN), "sqo")
                yield
                on(act, r.v[3], g, "sumo")
                r.act[3].done(deviation(esm[3], P, 1.0, eps_), "sdo")
                yield
            staged(act, (own, 1), (depths, 2), (last, 3))
            finished(act, r)

            r = sage1

            def src_rows(g, b, i, r=r):
                yield 1
                on(act, r.pe[0], g, "agg")
                on(act, r.st[b], i, "all", back=1)
                on(act, r.v[1], g, "h", back=2)
                r.act[0].done(act.copy(AR[b][:], rows_of(PS[b], P, W)), "agg")
                yield

            def dst_rows(g, b, i, r=r):
                on(act, r.pe[1], g, "tT")
                on(act, r.pe[1], g, "self", back=1)
                r.act[1].done(act.copy(XT[1][0:D, :], PS[2 + b][0:D, 0:GE]), "tT")
                yield

            def dst_h1(g, b, i, r=r):
                yield 1
                on(act, r.v[2], g, "m2s")
                r.act[2].done(plain_std(esm[2]), "sd")
                yield
            staged(act, (dst_rows, 0), (dst_h1, 1), (src_rows, 0))
            finished(act, r)

            r = sage2

            def src_self(g, b, i, r=r):
                on(act, r.pe[0], g, "rT")
                on(act, r.pe[0], g, "self", back=1)
                r.act[0].done(act.copy(XT[0][0:D, :], PS[0][0:D, 0:GE]), "rT")
                yield

            def src_agg(g, b, i, r=r):
                yield 1
                on(act, r.v[1], g, "m2s")
                r.act[1].done(plain_std(esm[1]), "sd")
                yield 3
                on(act, r.pe[1], g, "agg")
                on(act, r.st[b], i, "all", back=1)
                on(act, r.v[2], g, "h", back=2)
                r.act[1].done(act.copy(AR[b][:], rows_of(PS[1], P, W)), "agg")
                yield

            def dst_self(g, b, i, r=r):
                on(act, r.pe[2], g, "tT")
                on(act, r.pe[2], g, "self", back=1)
                r.act[2].done(act.copy(XT[1][0:D, :], PS[2][0:D, 0:GE]), "tT")
                yield 2
                on(act, r.v[2], g, "h")
                on(act, r.v[2], g, "sum", back=1)
                r.act[2].done(square(eSQ[0], eQ, STD), "sq")
                yield
                on(act, r.v[2], g, "sum")
                r.act[2].done(deviation(esm[2], P), "sd")
                yield

            def normed(r, stage, Z, sq, before=0):
                def program(g, b, i):
                    yield before
                    on(act, r.v[stage], g, "z") if "z" in r.v[stage].names else on(act, r.v[stage - 1], g, "z")
                    on(act, r.v[stage], g, "sumz", back=1)
                    r.act[stage].done(square(sq, Z(b), LN), "sqz")
                    yield
                    on(act, r.v[stage], g, "sumz")
                    r.act[stage].done(deviation(esm[stage], P, 1.0, eps_), "sdz")
                    yield
                return program
            staged(act, (src_self, 0), (src_agg, 1), (dst_self, 2), (normed(r, 3, lambda b: eZ[b][:], eSQ[1]), 3))
            finished(act, r)

            r = meanr

            def src_z(g, b, i, r=r):
                on(act, r.v[0], g, "h")
                on(act, r.v[1], g, "sum", back=1)
                r.act[1].done(square(eSQ[0], eH[b][:], STD), "sq")
                yield
                on(act, r.v[1], g, "sum")
                r.act[1].done(deviation(esm[1], P), "sd")
                yield
            staged(act, (normed(r, 2, lambda b: eZ[b][:], eSQ[1]), 2), (src_z, 1),
                   (normed(r, 3, lambda b: eQ, eSQ[2], 1), 3), (lambda g, b, i: src_self(g, b, i, r=meanr), 0))
            finished(act, r)

            r = softr

            def weights(g, b, i, r=r):
                yield 1
                on(act, r.v[1], g, "less")
                r.act[1].done(act.activation(DEC[0:D, :], DEC[0:D, :], ACT.Exp), "dec")
                on(act, r.v[1], g, "off")
                r.act[1].done(act.activation(EX[0:D, :], EX[0:D, :], ACT.Exp), "ex")
                yield

            def dst_out(g, b, i, r=r):
                on(act, r.pe[2], g, "tT")
                on(act, r.pe[2], g, "out", back=1)
                r.act[2].done(act.copy(XT[1][0:D, :], PS[2][0:D, 0:GE]), "tT")
                yield
                on(act, r.pe[2], g, "out")
                on(act, r.v[2], g, "sumo", back=1)
                r.act[2].done(square(eSQ[1], rows_of(PS[2], P, W), LN), "sqo")
                yield
                on(act, r.v[2], g, "sumo")
                r.act[2].done(deviation(esm[2], P, 1.0, eps_), "sdo")
                yield
            staged(act, (normed(r, 0, lambda b: eZ[b][:], eSQ[0], 1), 0), (weights, 1), (dst_out, 2))

        @block.vector
        def _(dve):
            credit(dve, "v", d_v)
            count = [0]

            def do(instruction):
                count[0] += 1
                instruction.then_inc(sort_step, 1)
                return count[0]

            def need(*numbers):
                dve.wait_ge(sort_step, max(numbers))

            for t, value in ((ones[:], 1.0), (one[:], 1.0), (cnt_row[:], 0.0), (eps[:], LN_EPS), (eps2[:], LN_EPS * LN_EPS),
                             *((t[D:D1, :], 1.0) for t in (*dXT, *XT)),
                             *((t[:, :, D:D1], 1.0) for t in (*RB, *RH))):
                do(dve.memset(t, value))
            dve.wait_ge(pool_init, POOL_INITS)
            dve.wait_ge(loaded_w, 16 * WEIGHT_LOADS)
            dve.wait_ge(prep_pe, 1)
            a = do(dve.tensor_copy(wT[:], PS[0][0:D, 0:512].rearrange("p (q c) -> p q c", c=P)[:, :, 0:D1]))
            need(a)
            dve.sem_inc(prep_v, 1)
            dve.wait_ge(prep_pe, 2)
            q4 = lambda q: PS[1][0:D1, q * P:q * P + D]
            for q, w in ((0, SELF0), (1, SELF1), (2, NB0), (3, NB1)):
                a = do(dve.tensor_copy(wt[:, w, :], q4(q)))
            need(a)
            for q, w in ((0, SELF0), (1, SELF1)):
                a = do(dve.tensor_tensor(wt[D:D1, w, :], wt[D:D1, w, :], b2row[D:D1, q, :], ALU.add))
            dve.sem_inc(prep_v, 1)
            idn = ident[0:D, 0:D]
            c = lambda k: chebw[:, k, :]
            a = do(dve.tensor_tensor(wt[0:D, A0, :], c(0), c(2), ALU.subtract))
            do(dve.scalar_tensor_tensor(wt[0:D, B1, :], c(3), -3.0, c(1), ALU.mult, ALU.add))
            do(dve.tensor_scalar(wt[0:D, B2, :], c(2), 2.0, None, ALU.mult))
            do(dve.tensor_scalar(wt[0:D, B3, :], c(3), 4.0, None, ALU.mult))
            do(dve.tensor_copy(wt[0:D, SOFTI, :], wt[0:D, SOFTW, :]))
            need(count[0])
            do(dve.tensor_tensor(wt[0:D, A0, :], wt[0:D, A0, :], idn, ALU.add))
            a = do(dve.tensor_tensor(wt[0:D, SOFTI, :], wt[0:D, SOFTI, :], idn, ALU.add))
            need(a)
            a = do(dve.tensor_reduce(wmean[:], wt[:, 0:9, :], AX.X, ALU.add))
            need(a)
            a = do(dve.tensor_scalar(wmean[:], wmean[:], -1.0 / D, None, ALU.mult))
            need(a)
            a = do(dve.tensor_tensor(wt[:, 0:9, :], wt[:, 0:9, :], spread(wmean[:], D1, 9), ALU.add))
            need(a)
            dve.wait_ge(loaded_e, 16 * 12)
            k_in = do(dve.tensor_copy(K[0], key_i[:].rearrange("p s c -> p (s c)")))
            v_in = do(dve.tensor_copy(V[0], pay_i[:].rearrange("p s c -> p (s c)")))

            cur = n = 0
            k_ok, v_ok = k_in, v_in

            def blocks(t, half, part):
                return t.rearrange("p (s two d) -> p s two d", two=2, d=half)[:, :, part, :]

            for op in sort_plan():
                if op[0] == "flip":
                    back, on_ = op[1], op[2]
                    if back is None and on_ is None:
                        continue
                    if back is not None and on_ is not None:
                        quarter = 1 << back
                        t = K[cur].rearrange("p (s four d) -> p s four d", four=4, d=quarter)[:, :, 1:3, :]
                    else:
                        t = blocks(K[cur], 1 << (on_ if back is None else back), 1)
                    need(k_ok)
                    k_ok = do(dve.tensor_scalar(t, t, -1.0, None, ALU.mult))
                elif op[0] == "switch":
                    n += 1
                    need(max(k_ok, v_ok))
                    dve.sem_inc(switch_ready, 1)
                    cur ^= 1
                    dve.wait_ge(switched, 2 * n - 1)
                    k_ok = do(dve.tensor_copy(K[cur], PS[0][:, 0:512]))
                    dve.wait_ge(v_back, n)
                    v_ok = k_ok
                else:
                    d = op[1]
                    ka, kb, va, vb = (blocks(t, d, part) for t in (K[cur], V[cur]) for part in (0, 1))
                    new = cur ^ 1
                    nka, nkb, nva, nvb = (blocks(t, d, part) for t in (K[new], V[new]) for part in (0, 1))
                    mask = MASK[cur][:, 0:256].rearrange("p (s d) -> p s d", d=d)
                    dif = DIF[:, 0:256].rearrange("p (s d) -> p s d", d=d)
                    need(k_ok)
                    do(dve.tensor_tensor(nka, ka, kb, ALU.min))
                    m = do(dve.tensor_tensor(mask, ka, kb, ALU.is_gt))
                    need(v_ok)
                    f = do(dve.tensor_tensor(dif, vb, va, ALU.subtract))
                    k_ok = do(dve.tensor_tensor(nkb, ka, kb, ALU.max))
                    need(m, f)
                    f = do(dve.tensor_tensor(dif, dif, mask, ALU.mult))
                    need(f)
                    do(dve.tensor_tensor(nva, va, dif, ALU.add))
                    v_ok = do(dve.tensor_tensor(nvb, vb, dif, ALU.subtract))
                    cur = new
            assert cur == SORTED
            KS = K[cur]
            need(v_ok, k_ok)
            dve.sem_inc(keys_out, 1)

            dve.wait_ge(keys_in, 16 * 6)
            a = do(dve.tensor_tensor(CONT, KS, KPREV, ALU.is_equal))
            f = do(dve.tensor_tensor(KNEXT, KS, KNEXT, ALU.is_equal))
            need(f)
            dve.sem_inc(keys_out, 1)
            do(dve.scalar_tensor_tensor(SIDX, KNEXT, FAR, KS, ALU.mult, ALU.add))
            for q in range(4):
                part = slice(q * P, (q + 1) * P)
                do(dve.tensor_tensor_scan(LOCAL[:, part], CONT[:, part], ones[:], 0.0, ALU.mult, ALU.add))
                a = do(dve.tensor_tensor_scan(CPROD[:, part], CONT[:, part], ones[:], 1.0, ALU.mult, ALU.mult))
            need(a)
            dve.sem_inc(post_v, 1)
            dve.wait_ge(post_pe, 1)
            a = do(dve.tensor_copy(cnt_in[:], PS[2][0:1, :]))
            need(a)
            for side in range(2):
                row = slice(side * SORT_COLS, (side + 1) * SORT_COLS)
                goes_on = slice((side + 2) * SORT_COLS, (side + 3) * SORT_COLS)
                a = do(dve.tensor_tensor_scan(cnt_row[0:1, side, 1:SORT_COLS + 1], cnt_in[:, goes_on], cnt_in[:, row],
                                              0.0, ALU.mult, ALU.add))
            need(a)
            dve.sem_inc(post_v, 1)
            dve.wait_ge(post_pe, 2)
            a = do(dve.tensor_copy(cnt_col[:], PS[3][:, 0:4]))
            need(a)
            for q in range(4):
                part = slice(q * P, (q + 1) * P)
                a = do(dve.scalar_tensor_tensor(CNT[:, part], CPROD[:, part], cnt_col[:, q:q + 1], LOCAL[:, part],
                                                ALU.mult, ALU.add))
            need(a)
            dve.sem_inc(post_v, 1)
            dve.wait_ge(post_pe, 3)
            flat = lambda t: t[:].rearrange("p s c -> p (s c)")
            do(dve.tensor_copy(flat(scat_i), PS[0][:, 0:512]))
            do(dve.tensor_copy(flat(pay_i), PS[0][:, 512:1024]))
            do(dve.tensor_scalar(flat(key_i), PS[1][:, 0:512], float(N - 1), None, ALU.min))
            for side in range(2):
                do(dve.tensor_copy(mapv[:, side, :, 0], pos_i[:]))
            b_ = do(dve.reciprocal(nrc[:], PS[1][:, 512:768]))
            do(dve.tensor_scalar(rcb[:], PS[1][:, 768:1024], 1.0, None, ALU.max))
            need(count[0])
            dve.sem_inc(post_v, 1)
            dve.wait_ge(roots, 1)
            a = do(dve.reciprocal(mapv[:, :, :, 1], MX[1][:, 0:512].rearrange("p (s c) -> p s c", s=2)))
            need(a)
            do(dve.tensor_scalar(ndinv[:], mapv[:, 0, :, 1], -1.0, None, ALU.mult))
            do(dve.tensor_scalar(nrc[:], nrc[:], -1.0, None, ALU.mult))
            a = do(dve.reciprocal(rcb[:], rcb[:]))
            a = do(dve.memset(SC[1][:, GE - 1:GE], 0.0))
            for t in MX:
                a = do(dve.memset(t[:, GE:GE + 1], 0.0))
            need(a)
            dve.sem_inc(idx_ready, 1)

            def means(out, sq):
                return dve.tensor_reduce(out, sq, AX.X, ALU.add)

            def inverse(m):
                return dve.reciprocal(m[:, 1, :], m[:, 3, :])

            def scale_by(out, rows, m, p, tiles):
                return dve.tensor_tensor(out, rows, spread(m[:, 1, :], p, tiles), ALU.mult)

            def about_mean(v, i, rows, six, m, tiles):
                for t in range(tiles):
                    ins = dve.bn_stats(six[:, t, :], rows[:, t, :])
                v.done(ins, "bn")
                on(dve, v, i, "bn")
                v.done(dve.tensor_tensor(m[:, 0, :], six[:, :, 1], six[:, :, 4], ALU.subtract), "dm")
                v.done(dve.tensor_tensor(m[:, 2, :], six[:, :, 2], six[:, :, 5], ALU.add), "m2")
                on(dve, v, i, "dm")
                v.done(dve.scalar_tensor_tensor(m[:, 1, :], m[:, 0, :], D / 4.0, m[:, 0, :], ALU.mult, ALU.mult), "dm2")
                on(dve, v, i, "dm2")
                v.done(dve.tensor_tensor(m[:, 2, :], m[:, 1, :], m[:, 2, :], ALU.add), "m2s")

            def dense(j, s):
                v, a_, m, ps = d_v[s], d_act[s], dsm[s], PS[(s + 1) % DS]
                rows = rows_of(ps, DP, DT)
                A, B, C = (by_tile(t[s]) for t in (dA, dB, dC))

                def summed(step, sq, name):
                    on(dve, a_, j, step)
                    v.done(means(m[:, 0, :], sq), name)

                def scaled(step, r, out, rows, name, free=None):
                    on(dve, a_, j, step)
                    if free:
                        free()
                    v.done(inverse(m), r)
                    on(dve, v, j, r)
                    v.done(scale_by(out, rows, m, DP, DT), name)

                def spread_about_mean():
                    on(dve, d_pe[s], j, "mm0")
                    about_mean(v, j, rows, dst6[s], m, DT)

                def residual():
                    scaled("sd2", "r2", B, rows, "h2")
                    on(dve, v, j, "h2")
                    v.done(dve.tensor_tensor(B, B, A, ALU.add), "z")

                return [(4, lambda: summed("sq", B, "sum")),
                        (6, lambda: scaled("sd", "r", A, rows, "x1", lambda: on(dve, d_so[s], j, "out", back=1))),
                        (10, spread_about_mean), (12, lambda: scaled("sd1", "r1", C, rows, "h1")),
                        (17, lambda: summed("sq2", B, "sum2")), (19, residual),
                        (21, lambda: summed("sqz", C, "sumz")), (23, lambda: scaled("sdz", "rz", C, B, "x3")),
                        (28, lambda: summed("sqo", B, "sumo")),
                        (30, lambda: scaled("sdo", "ro", A, rows, "out", lambda: on(dve, d_sx[s], j, "x1")))]

            dense_rounds(dve, dense, 0, ROUNDS4, START4)

            dve.wait_ge(map_out, 2 * GROUPS)
            a = do(dve.tensor_copy(found_i[:], found[:, :, :, 0]))
            need(a)
            dve.sem_inc(found_ready, 1)

            def cols(t, g):
                return t[:, bass.ds(g * W, W)]

            def scan(out, flags_, values, before, op1=ALU.add):
                return dve.tensor_tensor_scan(out, flags_, values, before, ALU.mult, op1)

            def sums(r, stage, g, b, i, rows, source):
                on(dve, r.fl[b], i, "all")
                on(dve, r.v[stage], g, "scan", back=1)
                r.v[stage].done(scan(SC[b][0:rows, :], FL[b][0:rows, :], source[0:rows, 0:GE],
                                     SC[b ^ 1][0:rows, GE - 1:GE]), "scan")

            for k, r in enumerate(cheb[:2]):
                def scaled(g, b, i, r=r):
                    on(dve, r.ga[b], i, "all")
                    r.v[2].done(dve.tensor_tensor(GB[b][:], GB[b][:], spread(found[:, 0, bass.ds(g * W, W), 1], P, W),
                                                  ALU.mult), "scaled")

                def summed(g, b, i, k=k, r=r):
                    on(dve, r.pe[0], g, "zT")
                    on(dve, r.pe[1], g, "back", back=2)
                    on(dve, r.st[b], i, "all", back=1)
                    sums(r, 0, g, b, i, D, PS[b if k else 0])

                def table(g, b, i, k=k, r=r):
                    on(dve, r.pe[1], g, "back")
                    on(dve, r.st[b], i, "all", back=1)
                    r.v[1].done(dve.tensor_tensor(OR[b][:], rows_of(PS[b if k else 0], P, W), spread(cols(nrc, g), P, W),
                                                  ALU.mult), "u")

                if k:
                    staged(dve, (summed, 0), (table, 1))
                else:
                    first_round(dve, dense, (0, scaled, 0), (4, summed, 0), (8, table, 0),
                                (15, scaled, 1), (19, summed, 1), (23, table, 1))
                finished(dve, r)
            r = cheb[2]

            def summed(g, b, i, r=r):
                on(dve, r.pe[0], g, "zT")
                on(dve, r.pe[0], g, "mix", back=2)
                sums(r, 0, g, b, i, D, PS[0])
                yield
                on(dve, r.pe[0], g, "mix")
                on(dve, r.v[1], g, "pre", back=2)
                r.v[0].done(dve.tensor_tensor(TH[b][:], rows_of(PS[0], P, W), spread(cols(ndinv, g), P, W), ALU.mult), "y")
                yield

            def own(g, b, i, r=r):
                v = r.v[1]
                yield 1
                on(dve, r.pe[1], g, "self")
                on(dve, r.v[0], g, "y")
                on(dve, v, g, "x1", back=1)
                v.done(dve.tensor_tensor(eH[0][:], TH[b][:], rows_of(PS[1], P, W), ALU.add), "pre")
                yield
                on(dve, r.act[1], g, "sq")
                v.done(means(esm[1][:, 0, :], eSQ[0]), "sum")
                yield
                on(dve, r.act[1], g, "sd")
                v.done(inverse(esm[1]), "r")
                on(dve, v, g, "r")
                on(dve, r.sc[b], i, "all", back=1)
                on(dve, r.v[2], g, "z", back=2)
                on(dve, r.pe[2], g, "x1T", back=2)
                v.done(scale_by(OR[b][:], eH[0][:], esm[1], P, W), "x1")
                yield

            def depths(g, b, i, r=r):
                v, a_, m, rows = r.v[2], r.act[2], esm[2], rows_of(PS[2], P, W)
                yield 1
                on(dve, r.pe[2], g, "self")
                about_mean(v, g, rows, est6[2], m, W)
                yield
                on(dve, a_, g, "sd1")
                v.done(inverse(m), "r")
                on(dve, v, g, "r")
                on(dve, r.pe[2], g, "h1T", back=1)
                v.done(scale_by(eH[1][:], rows, m, P, W), "h1")
                yield 4
                on(dve, a_, g, "sq")
                v.done(means(m[:, 0, :], eSQ[1]), "sum")
                yield
                on(dve, a_, g, "sd")
                v.done(inverse(m), "r2")
                on(dve, v, g, "r2")
                on(dve, r.v[3], g, "x3", back=2)
                v.done(scale_by(eZ[b][:], rows, m, P, W), "h2")
                on(dve, v, g, "h2")
                on(dve, r.v[1], g, "x1")
                v.done(dve.tensor_tensor(eZ[b][:], eZ[b][:], OR[b][:], ALU.add), "z")
                yield

            def last(g, b, i, r=r):
                v, a_, m = r.v[3], r.act[3], esm[3]
                on(dve, a_, g, "sqz")
                v.done(means(m[:, 0, :], eSQ[2]), "sumz")
                yield
                on(dve, a_, g, "sdz")
                v.done(inverse(m), "rz")
                on(dve, v, g, "rz")
                on(dve, r.pe[3], g, "x3T", back=1)
                v.done(scale_by(eQ, eZ[b][:], m, P, W), "x3")
                yield 3
                on(dve, a_, g, "sqo")
                v.done(means(m[:, 0, :], eSQ[2]), "sumo")
                yield
                on(dve, a_, g, "sdo")
                v.done(inverse(m), "ro")
                on(dve, v, g, "ro")
                on(dve, r.so[b], i, "all", back=1)
                v.done(scale_by(AR[b][:], rows_of(PS[3], P, W), m, P, W), "out")
                yield
            staged(dve, (summed, 0), (own, 1), (depths, 2), (last, 3))
            finished(dve, r)

            r = sage1

            def src_rows(g, b, i, r=r):
                on(dve, r.pe[0], g, "rT")
                on(dve, r.pe[0], g, "agg", back=2)
                sums(r, 0, g, b, i, D1, PS[b])
                yield

            def dst_h(g, b, i, r=r):
                yield 1
                on(dve, r.pe[1], g, "self")
                on(dve, r.act[0], g, "agg")
                on(dve, r.v[2], g, "h1", back=2)
                r.v[1].done(dve.tensor_tensor(eH[b][:], rows_of(PS[2 + b], P, W), AR[b][:], ALU.add), "h")
                yield

            def deviated(r, stage, source, g, b, i, out, before):
                v, m = r.v[stage], esm[stage]
                on(dve, r.v[stage - 1], g, "h")
                about_mean(v, g, source, est6[stage], m, W)
                yield
                on(dve, r.act[stage], g, "sd")
                v.done(inverse(m), "r")
                on(dve, v, g, "r")
                before()
                v.done(scale_by(out, source, m, P, W), "h1")
                yield

            def dst_h1(g, b, i, r=r):
                yield from deviated(r, 2, eH[b][:], g, b, i, TH[b][:], lambda: on(dve, r.su[b], i, "all", back=1))
            staged(dve, (src_rows, 0), (dst_h1, 1), (dst_h, 0))
            finished(dve, r)

            r = sage2

            def src_h(g, b, i, r=r, read="h1"):
                yield 1
                on(dve, r.pe[0], g, "self")
                on(dve, r.ga[b], i, "all")
                on(dve, r.v[1], g, read, back=2)
                r.v[0].done(dve.tensor_tensor(eH[b][:], rows_of(PS[0], P, W), GB[b][:], ALU.add), "h")
                yield

            def src_agg(g, b, i, r=r):
                def free():
                    on(dve, r.st[b], i, "all", back=1)
                    on(dve, r.pe[1], g, "h1T", back=2)
                yield from deviated(r, 1, eH[b][:], g, b, i, RH[b][:, :, 0:D], free)
                on(dve, r.pe[1], g, "h1T")
                on(dve, r.pe[1], g, "agg", back=2)
                sums(r, 1, g, b, i, D1, PS[1])
                yield

            def residual(v, acts, g, H, X, Z, m, sq, before):
                on(dve, acts, g, "sq")
                v.done(means(m[:, 0, :], sq), "sum")
                yield
                on(dve, acts, g, "sd")
                v.done(inverse(m), "r")
                on(dve, v, g, "r")
                before()
                v.done(scale_by(Z, H, m, P, W), "h2")
                on(dve, v, g, "h2")
                v.done(dve.tensor_tensor(Z, Z, X, ALU.add), "z")
                yield

            def normed(v, acts, g, out, name, Z, m, sq, before):
                on(dve, acts, g, "sqz")
                v.done(means(m[:, 0, :], sq), "sumz")
                yield
                on(dve, acts, g, "sdz")
                v.done(inverse(m), "rz")
                on(dve, v, g, "rz")
                before()
                v.done(scale_by(out, Z, m, P, W), name)
                yield

            def dst_z(g, b, i, r=r):
                yield 1
                on(dve, r.pe[2], g, "self")
                on(dve, r.act[1], g, "agg")
                on(dve, r.v[2], g, "h2", back=1)
                r.v[2].done(dve.tensor_tensor(eQ, rows_of(PS[2], P, W), AR[b][:], ALU.add), "h")
                yield
                yield from residual(r.v[2], r.act[2], g, eQ, TB[b][:], eZ[b][:], esm[2], eSQ[0],
                                    lambda: on(dve, r.v[3], g, "x2", back=2))

            def dst_x2(g, b, i, r=r):
                yield from normed(r.v[3], r.act[3], g, OR[b][:], "x2", eZ[b][:], esm[3], eSQ[1],
                                  lambda: on(dve, r.su[b], i, "all", back=1))
            staged(dve, (src_h, 0), (src_agg, 1), (dst_z, 2), (dst_x2, 3))
            finished(dve, r)

            r = meanr

            def src_z(g, b, i, r=r):
                on(dve, r.lr[b], i, "all")
                yield from residual(r.v[1], r.act[1], g, eH[b][:], RB[b][:, :, 0:D], eZ[b][:], esm[1], eSQ[0],
                                    lambda: on(dve, r.v[2], g, "x2", back=2))

            def src_agg(g, b, i, r=r):
                def free():
                    on(dve, r.st[b], i, "all", back=1)
                    on(dve, r.pe[2], g, "x2T", back=2)
                yield from normed(r.v[2], r.act[2], g, RH[b][:, :, 0:D], "x2", eZ[b][:], esm[2], eSQ[1], free)
                on(dve, r.pe[2], g, "x2T")
                on(dve, r.pe[2], g, "agg", back=2)
                sums(r, 2, g, b, i, D1, PS[1])
                yield
                on(dve, r.pe[2], g, "agg")
                on(dve, r.st[b], i, "all", back=1)
                on(dve, r.v[3], g, "z", back=2)
                r.v[2].done(dve.tensor_tensor(AR[b][:], rows_of(PS[1], P, W), spread(cols(rcb, g), P, W), ALU.mult), "agg")
                yield

            def dst_x3(g, b, i, r=r):
                on(dve, r.lt[b], i, "all")
                on(dve, r.v[2], g, "agg")
                on(dve, r.v[3], g, "x3", back=1)
                r.v[3].done(dve.tensor_tensor(eQ, TB[b][:], AR[b][:], ALU.add), "z")
                yield
                yield from normed(r.v[3], r.act[3], g, OR[b][:], "x3", eQ, esm[3], eSQ[2],
                                  lambda: on(dve, r.su[b], i, "all", back=1))
            staged(dve, (dst_x3, 3), (src_agg, 2), (src_z, 1), (lambda g, b, i: src_h(g, b, i, r=meanr, read="h2"), 0))
            finished(dve, r)

            for t in (DEN[1], NUM[1]):
                a = do(dve.memset(t[0:D, GE - 1:GE], 0.0))
            need(a)
            r = softr

            def src_x3(g, b, i, r=r):
                on(dve, r.ga[b], i, "all")
                on(dve, r.ld[b], i, "all")
                on(dve, r.v[0], g, "x3", back=2)
                r.v[0].done(dve.tensor_tensor(eZ[b][:], RB[b][:, :, 0:D], GB[b][:], ALU.add), "z")
                yield
                yield from normed(r.v[0], r.act[0], g, eH[b][:], "x3", eZ[b][:], esm[0], eSQ[0],
                                  lambda: on(dve, r.pe[0], g, "x3T", back=2))

            def messages(g, b, i, r=r):
                f = lambda t: t[0:D, 0:GE]
                v = r.v[1]
                on(dve, r.pe[0], g, "x3T")
                on(dve, v, g, "msg", back=1)
                v.done(dve.tensor_scalar(f(MB), PS[b][0:D, 0:GE], 0.0, MSG_EPS, ALU.max, ALU.add), "m")
                v.done(dve.tensor_copy(MX[b][0:D, 0:1], MX[b ^ 1][0:D, GE:GE + 1]), "carry")
                on(dve, r.fl[b], i, "all")
                on(dve, v, g, "carry")
                v.done(scan(MX[b][0:D, 1:GE + 1], FL[b][0:D, :], f(MB), MX[b][0:D, 0:1], ALU.max), "max")
                on(dve, v, g, "max")
                v.done(dve.tensor_tensor(f(DEC), FL[b][0:D, :], MX[b][0:D, 0:GE], ALU.mult), "kept")
                on(dve, v, g, "kept")
                v.done(dve.tensor_tensor(f(DEC), f(DEC), MX[b][0:D, 1:GE + 1], ALU.subtract), "less")
                v.done(dve.tensor_tensor(f(EX), f(MB), MX[b][0:D, 1:GE + 1], ALU.subtract), "off")
                yield
                on(dve, r.act[1], g, "dec")
                v.done(dve.tensor_tensor(f(DEC), f(DEC), FL[b][0:D, :], ALU.mult), "dec")
                on(dve, r.act[1], g, "ex")
                v.done(dve.tensor_tensor(f(QQ), f(EX), f(MB), ALU.mult), "q")
                on(dve, v, g, "dec")
                v.done(scan(f(DEN[b]), f(DEC), f(EX), DEN[b ^ 1][0:D, GE - 1:GE]), "den")
                on(dve, v, g, "q")
                v.done(scan(f(NUM[b]), f(DEC), f(QQ), NUM[b ^ 1][0:D, GE - 1:GE]), "num")
                yield
                on(dve, v, g, "den")
                on(dve, r.pe[2], g, "out", back=2)
                v.done(dve.reciprocal(f(MS[b]), f(DEN[b])), "rec")
                on(dve, v, g, "rec")
                v.done(dve.tensor_tensor(f(MS[b]), f(MS[b]), f(NUM[b]), ALU.mult), "msg")
                yield

            def dst_out(g, b, i, r=r):
                v, m = r.v[2], esm[2]
                yield 1
                on(dve, r.act[2], g, "sqo")
                v.done(means(m[:, 0, :], eSQ[1]), "sumo")
                yield
                on(dve, r.act[2], g, "sdo")
                v.done(inverse(m), "ro")
                on(dve, v, g, "ro")
                on(dve, r.sc[b], i, "all", back=1)
                v.done(scale_by(OR[b][:], rows_of(PS[2], P, W), m, P, W), "out")
                yield
            staged(dve, (src_x3, 0), (messages, 1), (dst_out, 2))




_INS = ["x", "src", "dst", "L0_gnn_weight", "L0_gnn_bias", "L1_gnn_W0", "L1_gnn_b0", "L1_gnn_W1", "L1_gnn_b1",
        "L1_gnn_W2", "L1_gnn_b2", "L2_gnn_W", "L2_gnn_b", "L3_gnn_W", "L3_gnn_b"]


def kernel(**inputs):
    import concourse.bacc as _bacc
    from concourse.bass_utils import run_bass_kernel_spmd as _run

    nc = _bacc.Bacc("TRN2", target_bir_lowering=False, num_devices=1)
    arrays, args = {}, []
    for name in _INS:
        a = np.ascontiguousarray(inputs[name])
        arrays[f"in_{name}"] = a
        args.append(nc.dram_tensor(f"in_{name}", a.shape, mybir.dt.from_np(a.dtype), kind="ExternalInput").ap())
    args.append(nc.dram_tensor("out_x", (N, D), F32, kind="ExternalOutput").ap())
    gnn_program(nc, *args)
    r = _run(nc, [arrays], core_ids=[0])
    return r.results[0]["out_x"]
```

```python
import numpy as np
import concourse.bass as bass
from concourse import mybir
from contextlib import ExitStack

F32 = mybir.dt.float32
I32 = mybir.dt.int32
ALU = mybir.AluOpType
ACT = mybir.ActivationFunctionType
AX = mybir.AxisListType

P = 128
N, D, E = 100000, 96, 25000
D1 = D + 1
SORT = 32768
SORT_BITS = 15
SORT_COLS = SORT // P
TILES = -(-E // P)
EP = TILES * P
W = 7
GROUPS = TILES // W
PAIRS = GROUPS // 2
GE = W * P
NONE_ROW = EP
FAR = float(1 << 20)
DP, DT = P, 8
DROWS = DP * DT
DENSE = -(-N // DROWS)
CREDIT = 16
LN_EPS = 1e-5
MSG_EPS = 1e-7


class Steps:

    def __init__(self, sem, start, names, unit=1):
        self.sem, self.start, self.names, self.unit = sem, start, names, unit
        self.n = 0

    def at(self, i, name, back=0):
        k = self.start + (self.names.index(name) + 1 - back * len(self.names)) * self.unit
        assert k > 0 or k == self.start
        return i * (len(self.names) * self.unit) + k

    def done(self, instruction, name):
        assert self.names[self.n % len(self.names)] == name, (name, self.names[self.n % len(self.names)])
        self.n += 1
        return instruction.then_inc(self.sem, self.unit)

    def end(self, rounds):
        return self.start + rounds * len(self.names) * self.unit


def weave(*programs):
    due = [(p, 0) for p in programs if p]
    slot = 0
    while due:
        later = []
        for p, at in due:
            while at is not None and at <= slot:
                try:
                    at = next(p)
                    at = slot + 1 if at is None else at
                except StopIteration:
                    at = None
            if at is not None:
                later.append((p, at))
        due = later
        slot += 1




def gnn_program(nc, x, src, dst, cheb_w, cheb_b, sage_w0, sage_b0, sage_w1, sage_b1, sage_w2, sage_b2,
                mean_w, mean_b, soft_w, soft_b, out):
    ctx = ExitStack()
    with ctx:
        def sb(name, shape, dt=F32):
            return ctx.enter_context(nc.sbuf_tensor(name, shape, dt))

        def sem(name):
            return ctx.enter_context(nc.semaphore(name))

        def dram(name, shape):
            return nc.dram_tensor(name, shape, F32, kind="Internal").ap()

        x1_d = dram("x1_table", [N, D])
        sorted_d = dram("sorted_keys", [2, SORT + 2])
        cont_d = dram("segment_goes_on", [2, SORT])
        map_d = [dram(f"node_map{s}", [N, 2]) for s in range(2)]
        u_d = [dram(f"u_table{k}", [EP + 1, D]) for k in range(2)]
        sT_d = [dram(f"cheb_sums{k}", [D, EP]) for k in range(2)]
        agg_d = [dram(f"agg_table{k}", [EP + 1, D]) for k in range(3)]
        r_d = [dram(f"src_rows{k}", [GROUPS, P, W * D]) for k in range(3)]
        t_d = [dram(f"dst_rows{k}", [GROUPS, P, W * D]) for k in range(4)]

        ident = sb("ident", [P, P])
        zrow = sb("zrow", [1, D])
        neg = sb("neg", [1, 1])
        one = sb("one", [1, 1])
        eps = sb("eps", [P, 1])
        eps2 = sb("eps2", [P, 1])
        msg_eps = sb("msg_eps", [P, 1])
        ones = sb("ones", [P, P])
        pos_i = sb("pos_i", [P, SORT_COLS], I32)
        chebw = sb("chebw", [D, 4, D])
        w1b1 = sb("w1b1", [D1, 2, D])
        w0b0 = sb("w0b0", [D1, 2, D])
        w2top = sb("w2top", [D, 2, D])
        w2bot = sb("w2bot", [D, 2, D])
        b2row = sb("b2row", [D1, 2, D])
        wT = sb("wT", [D, 4, D1])
        wt = sb("wt", [D1, 11, D])
        wmean = sb("wmean", [D1, 9])
        A0, B1, B2, B3, SELF1, NB1, MEANW, SOFTI, SOFTW, SELF0, NB0 = range(11)

        scat_i = sb("scat_i", [P, 2, SORT_COLS], I32)
        pay_i = sb("pay_i", [P, 2, SORT_COLS], I32)
        key_i = sb("key_i", [P, 2, SORT_COLS], I32)
        mapv = sb("mapv", [P, 2, SORT_COLS, 2])
        found = sb("found", [P, 2, TILES, 2])
        found_i = sb("found_i", [P, 2, TILES], I32)
        ndinv = sb("ndinv", [P, SORT_COLS])
        nrc = sb("nrc", [P, SORT_COLS])
        rcb = sb("rcb", [P, SORT_COLS])
        cnt_row = sb("cnt_row", [1, 2, SORT_COLS + 1])
        cnt_in = sb("cnt_in", [1, 4 * SORT_COLS])
        cnt_col = sb("cnt_col", [P, 4])

        DS = 4
        dX = [sb(f"dX{s}", [DP, DT * D]) for s in range(DS)]
        dXT = [sb(f"dXT{s}", [D1, DROWS]) for s in range(DS)]
        d_six = [sb(f"d_six{s}", [DP, DT, 6]) for s in range(DS)]
        dsm = [sb(f"dsm{s}", [DP, 4, DT]) for s in range(DS)]

        def pair(name, shape, dt=F32):
            return [sb(f"{name}{b}", shape, dt) for b in range(2)]

        idx_a = pair("idx_a", [P, W], I32)
        idx_b = pair("idx_b", [P, W], I32)
        idx_s = pair("idx_s", [P, W], I32)
        idx_o = pair("idx_o", [P, W], I32)
        mrow = pair("mrow", [P, W, 2])
        GB = pair("GB", [P, W, D])
        RB = pair("RB", [P, W, D])
        TB = pair("TB", [P, W, D])
        TH = pair("TH", [P, W, D])
        RH = pair("RH", [P, W, D])
        AR = pair("AR", [P, W, D])
        OR = pair("OR", [P, W, D])
        eH = pair("eH", [P, W, D])
        eZ = pair("eZ", [P, W, D])
        e_six = [sb(f"e_six{k}", [P, W, 6]) for k in range(4)]
        esm = [sb(f"esm{k}", [P, 4, W]) for k in range(4)]
        FL_ROWS = 112
        FL = pair("FL", [FL_ROWS, GE])
        SC = pair("SC", [D1, GE])
        XT = [sb(f"XT{k}", [D1, GE]) for k in range(3)]
        MX = pair("MX", [P, GE + 1])
        DEN = pair("DEN", [P, GE])
        NUM = pair("NUM", [P, GE])
        MB = sb("MB", [P, GE])
        DEC = sb("DEC", [P, GE])
        EX = sb("EX", [P, GE])
        QQ = sb("QQ", [P, GE])
        MS = pair("MS", [P, GE])

        K = [DEN[0][:, 0:512], NUM[0][:, 0:512]]
        V = [DEN[1][:, 0:512], NUM[1][:, 0:512]]
        MASK = [MB[:, 0:512], DEC[:, 0:512]]
        DIF = EX[:, 0:512]
        KPREV, KNEXT, LOCAL, CPROD, CONT = QQ[:, 0:512], MS[0][:, 0:512], MX[0][:, 0:512], MX[1][:, 0:512], EX[:, 0:512]
        SIDX, CNT = MB[:, 0:512], DEC[:, 0:512]
        dA, dB, dC = ([*(sb(f"{name}{s}", [DP, DT * D]) for s in range(2)), *(t[0:DP, 0:DT * D] for t in held_)]
                      for name, held_ in (("dA", (MB, DEC)), ("dB", (EX, QQ)), ("dC", MX)))
        as_rows = lambda t: t[:, 0:W * D].rearrange("p (w d) -> p w d", d=D)
        eSQ = [sb("eSQ0", [P, W, D])[:], sb("eSQ1", [P, W, D])[:], as_rows(EX)]
        eQ = as_rows(QQ)
        FILL_P, MAP_Q = 80, 250
        fill = TH[0][0:FILL_P, :, :].rearrange("p w d -> p (w d)")[:, 0:2 * MAP_Q]

        PS = [ctx.enter_context(nc.psum_tensor(f"PS{k}", [P, 1024], F32)) for k in range(4)]

        def rows_of(ps, p, tiles):
            return ps[0:p, 0:tiles * P].rearrange("p (t c) -> p t c", c=P)[:, :, 0:D]

        loaded_w = sem("loaded_w")
        loaded_e = sem("loaded_e")
        pool_init = sem("pool_init")
        filled = sem("filled")
        prep_v = sem("prep_v")
        prep_pe = sem("prep_pe")
        sort_step = sem("sort_step")
        switch_ready = sem("switch_ready")
        switched = sem("switched")
        v_back = sem("v_back")
        keys_out = sem("keys_out")
        keys_in = sem("keys_in")
        post_v = sem("post_v")
        post_pe = sem("post_pe")
        roots = sem("roots")
        idx_ready = sem("idx_ready")
        map_out = sem("map_out")
        found_ready = sem("found_ready")
        held = sem("held")

        d_ld = [Steps(sem(f"dense_loaded{s}"), 0, ["x"], 16) for s in range(DS)]
        d_sx = [Steps(sem(f"dense_x1_stored{s}"), CREDIT, ["x1"], 16) for s in range(DS)]
        d_so = [Steps(sem(f"dense_out_stored{s}"), CREDIT, ["out"], 16) for s in range(DS)]
        d_pe = [Steps(sem(f"dense_pe{s}"), CREDIT, ["xT", "mm", "x1T", "mm0", "h1T", "mm1", "x3T", "mm3"])
                for s in range(DS)]
        d_act = [Steps(sem(f"dense_act{s}"), CREDIT,
                       ["xT", "sq", "sd", "x1T", "sd1", "h1T", "sq2", "sd2", "sqz", "sdz", "x3T", "sqo", "sdo"])
                 for s in range(DS)]
        d_v = [Steps(sem(f"dense_v{s}"), CREDIT,
                     ["sum", "r", "x1", "bn", "dm", "m2", "dm2", "m2s", "r1", "h1", "sum2", "r2", "h2", "z",
                      "sumz", "rz", "x3", "sumo", "ro", "out"]) for s in range(DS)]
        BESIDE = 10
        ROUNDS4 = (DENSE - 3 * BESIDE) // DS
        assert ROUNDS4 * DS + BESIDE * 3 == DENSE
        ROUNDS_OF = [ROUNDS4 + (BESIDE if s < 3 else 0) for s in range(DS)]
        SLOTS = 31
        START4, START3 = (0, 19, 15, 3), (0, 5, 2)

        def dense_group(j, s, beside):
            return j * 3 + (s + ROUNDS4 * DS) if beside else j * DS + s

        def part(steps, low, high, shift):
            for at, action in steps:
                if low <= at < high:
                    yield at + shift
                    action()

        def dense_round(program, j, start, others=(), old=True, new=True):
            def stream(s, first):
                if old:
                    yield from part(program(j - 1, s), SLOTS - first, SLOTS, first - SLOTS)
                if new:
                    yield from part(program(j, s), 0, SLOTS - first, first)
            weave(*(stream(s, first) for s, first in enumerate(start)), *others)

        def dense_rounds(eng, program, begin, count, start, others=lambda i: ()):
            dense_round(program, begin, start, others(0), old=False)
            with eng.Fori(1, count) as i:
                dense_round(program, i + begin, start, others(i))
            dense_round(program, begin + count, start, new=False)

        dma_sems = {k: [sem(f"{k}_dma{b}") for b in range(2)]
                    for k in ("ga", "gb", "sc", "so", "fl", "ld", "lr", "lt", "st", "su")}
        step_sems = {k: sem(f"{k}_steps")
                     for k in ("idx", "sidx", "oidx", *(f"{e}{n}" for e in ("pe", "act", "v") for n in range(4)))}
        pool_dmas = ("ga", "gb", "sc", "so")
        reached = {k: 0 if k in pool_dmas else CREDIT for k in (*dma_sems, *step_sems)}

        class Round:
            def __init__(self, order=(), **lists):
                self.at = {name: n for line in order for n, name in enumerate(line.split(", "))}
                self.steps, self.dmas = {}, {}
                for k in step_sems:
                    self.steps[k] = Steps(step_sems[k], reached[k], lists.get(k, []))
                    reached[k] = self.steps[k].end(GROUPS)
                for k in dma_sems:
                    unit = 16 * (lists.get(k, 0))
                    self.dmas[k] = [Steps(q, reached[k], ["all"] if unit else [], unit) for q in dma_sems[k]]
                    reached[k] = self.dmas[k][0].end(PAIRS)
                self.idx, self.sidx, self.oidx = (self.steps[k] for k in ("idx", "sidx", "oidx"))
                self.pe, self.act, self.v = ([self.steps[f"{e}{n}"] for n in range(4)] for e in ("pe", "act", "v"))
                self.ga, self.gb, self.sc, self.so = (self.dmas[k] for k in pool_dmas)
                self.fl, self.ld, self.lr, self.lt, self.st, self.su = (
                    self.dmas[k] for k in ("fl", "ld", "lr", "lt", "st", "su"))

        map_put = [Round(idx=["a", "row"], sc=W), Round(idx=["a", "row"], so=W)]
        map_get = [Round(idx=["a"], ga=W), Round(idx=["a"], gb=W)]
        BN = ["bn", "dm", "m2", "dm2", "m2s", "r"]
        cheb = [
            Round(idx=["a", "b"], ga=W, gb=W, fl=1, st=3, pe0=["zT"], v2=["scaled"], v0=["scan"], pe1=["back"], v1=["u"]),
            Round(idx=["a"], ga=W, fl=1, st=2, pe0=["zT"], v0=["scan"], pe1=["back"], v1=["u"]),
            Round(idx=["a"], sidx=["s"], oidx=["s"], ga=W, fl=1, ld=2, lr=1, sc=W, so=W,
                  pe0=["zT", "mix"], v0=["scan", "y"],
                  pe1=["xT", "self"], act1=["xT", "sq", "sd"], v1=["pre", "sum", "r", "x1"],
                  pe2=["x1T", "self", "h1T", "self1"], act2=["x1T", "sd1", "h1T", "sq", "sd"],
                  v2=[*BN, "h1", "sum", "r2", "h2", "z"],
                  pe3=["x3T", "out"], act3=["sqz", "sdz", "x3T", "sqo", "sdo"],
                  v3=["sumz", "rz", "x3", "sumo", "ro", "out"],
                  order=("pe1 xT, pe0 zT, pe2 x1T, pe1 self, pe2 self, pe0 mix, pe3 x3T, pe2 h1T, pe3 out, pe2 self1",
                         "act1 xT, act3 sqz, act2 x1T, act3 sdz, act1 sq, act2 sd1, act3 x3T, act1 sd, act2 h1T, "
                         "act3 sqo, act2 sq, act2 sd, act3 sdo",
                         "v3 sumz, v0 scan, v3 x3, v1 pre, v2 bn, v1 sum, v2 h1, v0 y, v1 x1, v3 sumo, v2 sum, v2 z, "
                         "v3 out")),
        ]
        sage1 = Round(idx=["a", "b"], ga=W, gb=W, fl=1, st=3, su=1,
                      pe0=["rT", "agg"], act0=["agg"], v0=["scan"],
                      pe1=["tT", "self"], act1=["tT"], v1=["h"],
                      act2=["sd"], v2=[*BN, "h1"],
                      order=("", "", "v2 bn, v2 h1"))
        sage2 = Round(idx=["a"], ga=W, fl=1, ld=1, lt=2, st=2, su=1,
                      pe0=["rT", "self"], act0=["rT"], v0=["h"],
                      pe1=["h1T", "agg"], act1=["sd", "agg"], v1=[*BN, "h1", "scan"],
                      pe2=["tT", "self"], act2=["tT", "sq", "sd"], v2=["h", "sum", "r", "h2", "z"],
                      act3=["sqz", "sdz"], v3=["sumz", "rz", "x2"],
                      order=("pe2 tT, pe0 rT, pe2 self, pe1 h1T, pe0 self, pe1 agg",
                             "act2 tT, act3 sqz, act1 sd, act0 rT, act3 sdz, act2 sq, act2 sd, act1 agg",
                             "v1 bn, v3 sumz, v1 h1, v2 h, v3 x2, v1 scan, v2 sum, v0 h, v2 z"))
        meanr = Round(idx=["a"], ga=W, fl=1, ld=1, lr=1, lt=1, st=2, su=1,
                      pe0=["rT", "self"], act0=["rT"], v0=["h"],
                      act1=["sq", "sd"], v1=["sum", "r", "h2", "z"],
                      pe2=["x2T", "agg"], act2=["sqz", "sdz"], v2=["sumz", "rz", "x2", "scan", "agg"],
                      act3=["sqz", "sdz"], v3=["z", "sumz", "rz", "x3"],
                      order=("pe0 rT, pe2 x2T, pe0 self, pe2 agg",
                             "act2 sqz, act2 sdz, act1 sq, act3 sqz, act0 rT, act1 sd, act3 sdz",
                             "v2 sumz, v3 z, v2 x2, v1 sum, v3 sumz, v2 scan, v1 z, v3 x3, v2 agg, v0 h"))
        softr = Round(idx=["a"], sidx=["s"], ga=W, fl=1, ld=1, lt=1, sc=W,
                      pe0=["x3T"], act0=["sqz", "sdz"], v0=["z", "sumz", "rz", "x3"],
                      act1=["relu", "m", "down", "dec", "ex"],
                      v1=["carry", "max", "less", "off", "dec", "q", "den", "num"], act3=["ln", "inverse"], v3=["msg"],
                      pe2=["tT", "out"], act2=["tT", "sqo", "sdo"], v2=["sumo", "ro", "out"],
                      order=("pe2 tT, pe2 out, pe0 x3T",
                             "act2 tT, act1 relu, act1 m, act0 sqz, act0 sdz, act2 sqo, act1 down, act2 sdo, "
                             "act1 dec, act1 ex, act3 ln, act3 inverse",
                             "v3 msg, v0 z, v1 max, v0 sumz, v1 less, v2 sumo, v0 x3, v2 out, v1 off, v1 dec, v1 q, "
                             "v1 den, v1 num"))

        def staged(eng, *stages):
            most = max(lag for _, lag in stages)
            lead = (most + 1) // 2

            def step(i, t, live):
                weave(*(program(i * 2 + (t - lag), (t - lag) % 2, i + (t - lag) // 2)
                        for program, lag in stages if live(lag)))

            for t in range(2 * lead):
                step(0, t, lambda lag: lag <= t)
            with eng.Fori(lead, PAIRS) as i:
                for t in range(2):
                    step(i, t, lambda lag: True)
            for t in range(most):
                step(PAIRS, t, lambda lag: lag > t)

        def nodes(table, g):
            at = 0 if isinstance(g, int) and g == 0 else g * DROWS + (N - DENSE * DROWS)
            return table[bass.ds(at, DROWS), :].rearrange("(p i) d -> p (i d)", p=DP)

        def group(view, g):
            return view[bass.ds(g, 1)].rearrange("g p f -> (g p) f")

        def table_group(table, g):
            v = table[0:EP].rearrange("(g p i) d -> g p i d", p=P, i=W)
            return v[bass.ds(g, 1)].rearrange("g p i d -> (g p) i d")

        def by_tile(t):
            return t[:, :].rearrange("p (t d) -> p t d", d=D)

        def spread(scale, p, tiles):
            return scale.unsqueeze(2).to_broadcast([p, tiles, D])

        def on(eng, steps, i, name, back=0):
            eng.wait_ge(steps.sem, steps.at(i, name, back))

        def credit(eng, kind, streams):
            for n in range(4):
                eng.sem_inc(step_sems[f"{kind}{n}"], CREDIT)
            for steps in streams:
                eng.sem_inc(steps.sem, CREDIT)

        def beside(i, *steps):
            for at, stage, b in steps:
                yield at
                stage(i * 2 + b, b, i)

        def first_round(eng, program, *steps):
            dense_rounds(eng, program, ROUNDS4, BESIDE, START3, lambda i: [beside(i, *steps)])
            with eng.Fori(BESIDE, PAIRS) as i:
                weave(beside(i, *steps))

        def stored(eng, r):
            for q in r.st:
                eng.wait_ge(q.sem, q.end(PAIRS))

        def finished(eng, r):
            for steps in r.steps.values():
                if steps.names:
                    eng.wait_ge(steps.sem, steps.end(GROUPS))
            for made in r.dmas.values():
                for q in made:
                    if q.names:
                        eng.wait_ge(q.sem, q.end(PAIRS))

        FILLS = 5 + 2 * (N // FILL_P // MAP_Q) + 4
        SORTED = SORT_BITS * (SORT_BITS + 1) // 2 % 2
        POOL_INITS = 9
        WEIGHT_LOADS = 8 + 6

        block = ctx.enter_context(nc.Block())

        @block.sync
        def _(sp):
            for q in (*(q for k in ("fl", "ld", "lr", "lt", "st", "su") for q in dma_sems[k]),
                      *(steps.sem for steps in (*d_sx, *d_so))):
                sp.sem_inc(q, CREDIT)
            sp.wait_ge(pool_init, 2)
            full, rest = E // P, E % P
            for side, (k, v) in enumerate(((src, dst), (dst, src))):
                for t, a in ((key_i, k), (pay_i, v)):
                    rows = a[0:full * P].rearrange("(r p) -> r p", p=P)
                    sp.dma_start(t[:, side, 0:P], rows[0:P, :]).then_inc(loaded_e, 16)
                    sp.dma_start(t[0:full - P, side, P:2 * P], rows[P:full, :]).then_inc(loaded_e, 16)
                    sp.dma_start(t[full - P:full - P + 1, side, P:P + rest],
                                 a[full * P:E].rearrange("(o p) -> o p", o=1)).then_inc(loaded_e, 16)
            for t, a in ((chebw, cheb_w.rearrange("k i o -> i k o")),
                         (w1b1[0:D], sage_w1.rearrange("k i o -> i k o")),
                         (w0b0[0:D], sage_w0.rearrange("k i o -> i k o")),
                         (w2top, sage_w2[:, 0:D, :].rearrange("k i o -> i k o")),
                         (w2bot, sage_w2[:, D:2 * D, :].rearrange("k i o -> i k o"))):
                sp.dma_start(t[:], a).then_inc(loaded_w, 16)
            for t, a in ((w1b1, sage_b1), (w0b0, sage_b0), (b2row, sage_b2)):
                sp.dma_start(t[D:D1], a.rearrange("(o k) f -> o k f", o=1)).then_inc(loaded_w, 16)
            sp.wait_ge(pool_init, 3)
            for n, w, b in ((MEANW, mean_w, mean_b), (SOFTI, soft_w, soft_b), (SOFTW, soft_w, None), (A0, None, cheb_b)):
                if w is not None:
                    sp.dma_start(wt[0:D, n, :], w).then_inc(loaded_w, 16)
                if b is not None:
                    sp.dma_start(wt[D:D1, n, :], b.rearrange("(o f) -> o f", o=1)).then_inc(loaded_w, 16)
            sp.wait_ge(pool_init, 6)
            for table in (*u_d, *agg_d):
                sp.dma_start(table[NONE_ROW:NONE_ROW + 1, :], zrow[:]).then_inc(filled, 16)
            for m in map_d:
                mv = m.rearrange("(c p q) t -> c p (q t)", p=FILL_P, q=MAP_Q)
                for c in range(mv.shape[0]):
                    sp.dma_start(mv[c], fill).then_inc(filled, 16)
            for side in range(2):
                for at in (0, SORT + 1):
                    sp.dma_start(sorted_d[side:side + 1, at:at + 1], neg[:]).then_inc(filled, 16)
            shifted = lambda side, o: sorted_d[side, o:o + SORT].rearrange("(h q p) -> q h p", h=2, p=P)
            sp.wait_ge(keys_out, 1)
            sp.wait_ge(filled, 16 * FILLS)
            for side in range(2):
                sp.dma_start(shifted(side, 1), K[SORTED][:, side * 256:side * 256 + 256]
                             .rearrange("q (h p) -> q h p", h=2)).then_inc(keys_in, 16)
            sp.wait_ge(keys_in, 32)
            for side in range(2):
                for o, t in ((0, KPREV), (2, KNEXT)):
                    sp.dma_start(t[:, side * 256:side * 256 + 256].rearrange("q (h p) -> q h p", h=2),
                                 shifted(side, o)).then_inc(keys_in, 16)
            sp.wait_ge(keys_out, 2)
            for side in range(2):
                sp.dma_start(cont_d[side].rearrange("(h q p) -> q h p", h=2, p=P),
                             CONT[:, side * 256:side * 256 + 256].rearrange("q (h p) -> q h p", h=2)).then_inc(keys_in, 16)
            sp.wait_ge(keys_in, 16 * 8)

            def load_rows(j, g, s):
                on(sp, d_pe[s], j, "xT", back=1)
                sp.dma_start(dX[s][:], nodes(x, g)).then_inc(d_ld[s].sem, 16)

            def dense_io(base, beside, more):
                def program(j, s):
                    g = dense_group(j - base, s, beside)

                    def store(step, steps, table):
                        on(sp, d_v[s], j, step)
                        if s == 1:
                            on(sp, steps[0], j, step)
                        sp.dma_start(nodes(table, g), dA[s][:, :]).then_inc(steps[s].sem, 16)

                    load = lambda: load_rows(j + 1, dense_group(j + (1 - base), s, beside), s)
                    return [*([(1, load)] if more else []), (7, lambda: store("x1", d_sx, x1_d)),
                            (30, lambda: store("out", d_so, out))]
                return program

            for s in range(DS):
                load_rows(0, dense_group(0, s, False), s)
            def flags(r, side, stage, name):
                def load(g, b, i):
                    on(sp, r.v[stage], g, name, back=2)
                    sp.dma_start(FL[b][:], cont_d[side:side + 1, bass.ds(g * GE, GE)].to_broadcast([FL_ROWS, GE])
                                 ).then_inc(r.fl[b].sem, 16)
                    yield
                return load

            def dense_rounds_io(begin, count, start, beside, others=lambda i: ()):
                program, last = dense_io(begin, beside, True), dense_io(begin, beside, False)
                dense_round(program, begin, start, others(0), old=False)
                with sp.Fori(1, count - 1) as i:
                    dense_round(program, i + begin, start, others(i))
                dense_round(last, begin + count - 1, start, others(count - 1))
                dense_round(last, begin + count, start, new=False)

            dense_rounds_io(0, ROUNDS4, START4, False)
            for s in range(3):
                load_rows(ROUNDS4, dense_group(0, s, True), s)

            for k, r in enumerate(cheb[:2]):
                def store_sums(g, b, i, r=r, k=k):
                    on(sp, r.v[0], g, "scan")
                    sp.dma_start(sT_d[k][:, bass.ds(g * GE, GE)], SC[b][0:D, :]).then_inc(r.st[b].sem, 16)

                def store_table(g, b, i, r=r, k=k):
                    on(sp, r.v[1], g, "u")
                    sp.dma_start(table_group(u_d[k], g), OR[b][:]).then_inc(r.st[b].sem, 16)

                def store_rows(g, b, i, r=r):
                    on(sp, r.gb[b], i, "all")
                    sp.dma_start(group(r_d[0], g), RB[b][:]).then_inc(r.st[b].sem, 16)

                def next_flags(g, b, i, r=r):
                    weave(flags(r, 0, 0, "scan")(g + 2, b, i))

                if k:
                    staged(sp, (flags(r, 0, 0, "scan"), 0), (store_sums, 2), (store_table, 2))
                else:
                    for b in range(2):
                        next_flags(b - 2, b, 0)
                    steps = [(5, store_sums, 0), (5, store_rows, 0), (6, next_flags, 0), (9, store_table, 0),
                             (20, store_sums, 1), (20, store_rows, 1), (21, next_flags, 1), (24, store_table, 1)]
                    dense_rounds_io(ROUNDS4, BESIDE, START3, True, lambda i: [beside(i, *steps)])
                    with sp.Fori(BESIDE, PAIRS - 1) as i:
                        weave(beside(i, *steps))
                    weave(beside(PAIRS - 1, *(step for step in steps if step[1] is not next_flags)))
                finished(sp, r)
            r = cheb[2]

            def load(g, b, i, r=r):
                on(sp, r.pe[0], g, "mix", back=2)
                for k, t in enumerate((DEN, NUM)):
                    sp.dma_start(t[b][0:D, :], sT_d[k][:, bass.ds(g * GE, GE)]).then_inc(r.ld[b].sem, 16)
                yield

            def load_rows_of_x(g, b, i, r=r):
                on(sp, r.pe[1], g, "xT", back=2)
                sp.dma_start(RB[b][:], group(r_d[0], g)).then_inc(r.lr[b].sem, 16)
                yield
            staged(sp, (flags(r, 0, 0, "scan"), 0), (load, 0), (load_rows_of_x, 1))
            finished(sp, r)

            r = sage1

            def store_r(g, b, i, r=r):
                on(sp, r.ga[b], i, "all")
                sp.dma_start(group(r_d[0], g), RB[b][:]).then_inc(r.st[b].sem, 16)
                yield
                on(sp, r.gb[b], i, "all")
                sp.dma_start(group(t_d[0], g), TB[b][:]).then_inc(r.st[b].sem, 16)
                yield
                on(sp, r.act[0], g, "agg")
                sp.dma_start(table_group(agg_d[0], g), AR[b][:]).then_inc(r.st[b].sem, 16)
                yield
                on(sp, r.v[2], g, "h1")
                sp.dma_start(group(t_d[1], g), TH[b][:]).then_inc(r.su[b].sem, 16)
            staged(sp, (flags(r, 1, 0, "scan"), 0), (store_r, 2))

            finished(sp, sage1)
            r = sage2

            def load(g, b, i, r=r):
                on(sp, r.pe[0], g, "rT", back=2)
                sp.dma_start(RB[b][:], group(r_d[0], g)).then_inc(r.ld[b].sem, 16)
                yield

            def load_t(g, b, i, r=r):
                on(sp, r.v[2], g, "z", back=2)
                sp.dma_start(TB[b][:], group(t_d[0], g)).then_inc(r.lt[b].sem, 16)
                sp.dma_start(TH[b][:], group(t_d[1], g)).then_inc(r.lt[b].sem, 16)
                yield

            def store(g, b, i, r=r):
                on(sp, r.v[1], g, "h1")
                sp.dma_start(group(r_d[1], g), RH[b][:]).then_inc(r.st[b].sem, 16)
                on(sp, r.act[1], g, "agg")
                sp.dma_start(table_group(agg_d[1], g), AR[b][:]).then_inc(r.st[b].sem, 16)
                yield

            def store_t(g, b, i, r=r):
                on(sp, r.v[3], g, "x2")
                sp.dma_start(group(t_d[2], g), OR[b][:]).then_inc(r.su[b].sem, 16)
                yield
            staged(sp, (load, 0), (flags(r, 1, 1, "scan"), 1), (load_t, 2), (store, 3), (store_t, 5))

            finished(sp, sage2)
            r = meanr

            def load(g, b, i, r=r):
                on(sp, r.pe[0], g, "rT", back=2)
                sp.dma_start(TH[b][:], group(r_d[1], g)).then_inc(r.ld[b].sem, 16)
                yield

            def load_r(g, b, i, r=r):
                on(sp, r.v[1], g, "z", back=2)
                sp.dma_start(RB[b][:], group(r_d[0], g)).then_inc(r.lr[b].sem, 16)
                yield

            def load_t(g, b, i, r=r):
                on(sp, r.v[3], g, "z", back=2)
                sp.dma_start(TB[b][:], group(t_d[2], g)).then_inc(r.lt[b].sem, 16)
                yield

            def store(g, b, i, r=r):
                on(sp, r.v[2], g, "x2")
                sp.dma_start(group(r_d[2], g), RH[b][:]).then_inc(r.st[b].sem, 16)
                on(sp, r.v[2], g, "agg")
                sp.dma_start(table_group(agg_d[2], g), AR[b][:]).then_inc(r.st[b].sem, 16)
                yield

            def store_t(g, b, i, r=r):
                on(sp, r.v[3], g, "x3")
                sp.dma_start(group(t_d[3], g), OR[b][:]).then_inc(r.su[b].sem, 16)
                yield
            staged(sp, (load, 0), (load_r, 1), (flags(r, 1, 2, "scan"), 2), (load_t, 3), (store, 4), (store_t, 5))

            finished(sp, meanr)
            r = softr

            def load(g, b, i, r=r):
                on(sp, r.v[0], g, "z", back=2)
                sp.dma_start(RB[b][:], group(r_d[2], g)).then_inc(r.ld[b].sem, 16)
                yield

            def load_t(g, b, i, r=r):
                on(sp, r.pe[2], g, "tT", back=2)
                sp.dma_start(TB[b][:], group(t_d[3], g)).then_inc(r.lt[b].sem, 16)
                yield
            staged(sp, (load, 0), (flags(r, 1, 1, "dec"), 1), (load_t, 3))
            for b in range(2):
                sp.wait_ge(r.sc[b].sem, r.sc[b].end(PAIRS))

        @block.gpsimd
        def _(gp):
            gp.sem_inc(step_sems["idx"], CREDIT)
            gp.sem_inc(step_sems["sidx"], CREDIT)
            gp.sem_inc(step_sems["oidx"], CREDIT)
            gp.memset(key_i[:], N).then_inc(pool_init, 1)
            gp.memset(pay_i[:], 0).then_inc(pool_init, 1)
            gp.memset(wt[:], 0.0).then_inc(pool_init, 1)
            gp.memset(zrow[:], 0.0)
            gp.memset(neg[:], -1.0).then_inc(pool_init, 1)
            fv = fill.rearrange("p (q t) -> p q t", t=2)
            gp.memset(fv[:, :, 0], float(NONE_ROW)).then_inc(pool_init, 1)
            gp.memset(fv[:, :, 1], 0.0).then_inc(pool_init, 1)
            gp.memset(ident[:], 0.0).then_inc(pool_init, 1)
            gp.iota(pos_i[:, 0:TILES].rearrange("p (g i) -> p g i", i=W), pattern=[[GE, GROUPS], [1, W]], base=0,
                    channel_multiplier=W).then_inc(pool_init, 1)
            gp.wait_ge(pool_init, 8)
            gp.affine_select(out=ident[:], in_=ident[:], compare_op=ALU.not_equal, fill=1.0, base=0,
                             pattern=[[-1, P]], channel_multiplier=1).then_inc(pool_init, 1)

            last_node = gp.to_reg(N - 1)

            def hold(*conditions):
                for steps, i, name, back in conditions:
                    on(gp, steps, i, name, back)
                gp.sem_inc(held, 1)

            def cols(t, side, g):
                return t[:, side, bass.ds(g * W, W)]

            def copy_idx(steps, name, to, columns, dmas, i, b, first=False):
                if not first:
                    on(gp, dmas[b], i, "all", back=1)
                steps.done(gp.tensor_copy(to[b][:], columns), name)

            gp.wait_ge(idx_ready, 1)
            gp.wait_ge(filled, 16 * FILLS)

            def put_map(side, i, first=False):
                r = map_put[side]
                dmas = (r.sc, r.so)[side]
                for b in range(2):
                    g = i * 2 + b
                    copy_idx(r.idx, "a", idx_a, cols(scat_i, side, g), dmas, i, b, first)
                    r.idx.done(gp.tensor_copy(mrow[b][:], mapv[:, side, bass.ds(g * W, W), :]), "row")
                    hold((r.idx, g, "row", 0))
                    for w in range(W):
                        gp.indirect_dma_start(
                            out=map_d[side], out_offset=bass.IndirectOffsetOnAxis(ap=idx_a[b][:, w:w + 1], axis=0),
                            in_=mrow[b][:, w, :], in_offset=None, bounds_check=last_node, oob_is_err=False,
                        ).then_inc(dmas[b].sem, 16)

            for side in range(2):
                if side:
                    finished(gp, map_put[0])
                put_map(side, 0, first=True)
                with gp.Fori(1, PAIRS) as i:
                    put_map(side, i)
            finished(gp, map_put[1])
            for side, r in enumerate(map_get):
                dmas = (r.ga, r.gb)[side]

                def fetch(i, b, side=side, r=r, dmas=dmas):
                    g = i * 2 + b
                    r.idx.done(gp.tensor_copy(idx_a[b][:], cols(pay_i, side, g)), "a")
                    hold((r.idx, g, "a", 0))
                    for w in range(W):
                        gp.indirect_dma_start(
                            out=mrow[b][:, w, :], out_offset=None, in_=map_d[side],
                            in_offset=bass.IndirectOffsetOnAxis(ap=idx_a[b][:, w:w + 1], axis=0),
                        ).then_inc(dmas[b].sem, 16)

                def keep(i, b, side=side, dmas=dmas):
                    on(gp, dmas[b], i, "all")
                    gp.tensor_copy(found[:, side, bass.ds((i * 2 + b) * W, W), :], mrow[b][:]).then_inc(map_out, 1)

                for b in range(2):
                    if side:
                        gp.wait_ge(map_out, GROUPS)
                    fetch(0, b)
                with gp.Fori(0, PAIRS - 1) as i:
                    for b in range(2):
                        keep(i, b)
                        gp.wait_ge(map_out, i * 2 + (b + 1 + side * GROUPS))
                        fetch(i + 1, b)
                for b in range(2):
                    keep(PAIRS - 1, b)

            def gather(r, key, b, to, table, idx):
                for w in range(W):
                    gp.indirect_dma_start(out=to[b][:, w, 0:D], out_offset=None, in_=table,
                                          in_offset=bass.IndirectOffsetOnAxis(ap=idx[b][:, w:w + 1], axis=0),
                                          ).then_inc(r.dmas[key][b].sem, 16)

            def scatter(dmas, b, table, rows, idx):
                for w in range(W):
                    gp.indirect_dma_start(out=table, out_offset=bass.IndirectOffsetOnAxis(ap=idx[b][:, w:w + 1], axis=0),
                                          in_=rows[b][:, w, :], in_offset=None, bounds_check=last_node, oob_is_err=False,
                                          ).then_inc(dmas[b].sem, 16)

            found_rows = lambda side, g: found_i[:, side, bass.ds(g * W, W)]

            for k, r in enumerate(cheb[:2]):
                if k:
                    gp.wait_ge(found_ready, 1)
                with gp.Fori(0, PAIRS) as i:
                    for b in range(2):
                        g = i * 2 + b
                        copy_idx(r.idx, "a", idx_a, found_rows(0, g) if k else cols(pay_i, 0, g), r.ga, i, b)
                        hold((r.pe[0], g, "zT", 2), (r.idx, g, "a", 0))
                        gather(r, "ga", b, GB, u_d[k - 1] if k else x, idx_a)
                        if k == 0:
                            copy_idx(r.idx, "b", idx_b, cols(key_i, 0, g), r.gb, i, b)
                            hold((r.st[b], i, "all", 1), (r.idx, g, "b", 0))
                            gather(r, "gb", b, RB, x, idx_b)
                finished(gp, r)
            for s in range(DS):
                gp.wait_ge(d_sx[s].sem, d_sx[s].end(ROUNDS_OF[s]))
                gp.wait_ge(d_so[s].sem, d_so[s].end(ROUNDS_OF[s]))
            r = cheb[2]

            def fetch(g, b, i, r=r):
                copy_idx(r.idx, "a", idx_a, found_rows(0, g), r.ga, i, b)
                hold((r.pe[0], g, "zT", 2), (r.idx, g, "a", 0))
                gather(r, "ga", b, GB, u_d[1], idx_a)
                yield

            def put_x1(g, b, i, r=r):
                copy_idx(r.sidx, "s", idx_s, cols(scat_i, 0, g), r.sc, i, b)
                hold((r.v[1], g, "x1", 0), (r.sidx, g, "s", 0))
                scatter(r.sc, b, x1_d, OR, idx_s)
                yield

            def put_out(g, b, i, r=r, first=False):
                copy_idx(r.oidx, "s", idx_o, cols(scat_i, 0, g), r.so, i, b, first)
                hold((r.v[3], g, "out", 0), (r.oidx, g, "s", 0))
                scatter(r.so, b, out, AR, idx_o)
                yield
            staged(gp, (fetch, 0), (put_x1, 3), (put_out, 5))
            finished(gp, r)

            r = sage1
            with gp.Fori(0, PAIRS) as i:
                for b in range(2):
                    g = i * 2 + b
                    copy_idx(r.idx, "a", idx_a, cols(pay_i, 1, g), r.ga, i, b)
                    copy_idx(r.idx, "b", idx_b, cols(key_i, 1, g), r.gb, i, b)
                    hold((r.pe[0], g, "rT", 2), (r.st[b], i, "all", 1), (r.idx, g, "b", 0))
                    gather(r, "ga", b, RB, x1_d, idx_a)
                    hold((r.pe[1], g, "tT", 2))
                    gather(r, "gb", b, TB, x1_d, idx_b)
            stored(gp, r)
            for r, table in ((sage2, agg_d[0]), (meanr, agg_d[1])):
                with gp.Fori(0, PAIRS) as i:
                    for b in range(2):
                        g = i * 2 + b
                        copy_idx(r.idx, "a", idx_a, found_rows(1, g), r.ga, i, b)
                        hold((r.v[0], g, "h", 2), (r.idx, g, "a", 0))
                        gather(r, "ga", b, GB, table, idx_a)
                stored(gp, r)
            r = softr

            def fetch(g, b, i, r=r):
                copy_idx(r.idx, "a", idx_a, found_rows(1, g), r.ga, i, b)
                hold((r.v[0], g, "z", 2), (r.idx, g, "a", 0))
                gather(r, "ga", b, GB, agg_d[2], idx_a)
                yield

            def put_out(g, b, i, r=r):
                copy_idx(r.sidx, "s", idx_s, cols(scat_i, 1, g), r.sc, i, b)
                hold((r.v[2], g, "out", 0), (r.sidx, g, "s", 0))
                scatter(r.sc, b, out, OR, idx_s)
                yield
            staged(gp, (fetch, 0), (put_out, 5))

        def sort_plan():
            for k in range(1, SORT_BITS + 1):
                if k <= 6:
                    yield ("flip", k - 1 if k > 1 else None, k)
                else:
                    if k == 7:
                        yield ("flip", 6, None)
                    yield ("switch",)
                    yield ("flip", k - 8 if k > 7 else None, k - 7 if k < SORT_BITS else None)
                    for j in range(k - 8, -1, -1):
                        yield ("step", 1 << j)
                    yield ("switch",)
                for j in range(min(k, 7) - 1, -1, -1):
                    yield ("step", 1 << j)

        @block.tensor
        def _(pe):
            credit(pe, "pe", d_pe)
            pe.wait_ge(pool_init, POOL_INITS)
            pe.wait_ge(loaded_w, 16 * WEIGHT_LOADS)
            for q, t in enumerate((w1b1[:, 0], w1b1[:, 1], w0b0[:, 0], w0b0[:, 1])):
                last = pe.transpose(PS[0][0:D, q * P:q * P + D1], t, ident[0:D1, 0:D1])
            last.then_inc(prep_pe, 1)
            pe.wait_ge(prep_v, 1)
            for q, t in enumerate((w2top[:, 0], w2top[:, 1], w2bot[:, 0], w2bot[:, 1])):
                last = pe.matmul(PS[1][0:D1, q * P:q * P + D], wT[:, q, :], t, start=True, stop=True)
            last.then_inc(prep_pe, 1)
            pe.wait_ge(prep_v, 2)
            cur = n = 0
            for op in sort_plan():
                if op[0] == "step":
                    cur ^= 1
                if op[0] != "switch":
                    continue
                n += 1
                pe.wait_ge(switch_ready, n)
                for ps, t in ((PS[0], K[cur]), (PS[1], V[cur])):
                    for q in range(4):
                        last = pe.transpose(ps[:, q * P:(q + 1) * P], t[:, q * P:(q + 1) * P], ident[:])
                    last.then_inc(switched, 1)
                cur ^= 1
            pe.wait_ge(post_v, 1)
            for k, t in enumerate((LOCAL, CPROD)):
                for q in range(4):
                    last = pe.matmul(PS[2][0:1, (4 * k + q) * P:(4 * k + q + 1) * P], t[:, q * P + P - 1:q * P + P],
                                     ident[:], start=True, stop=True)
            last.then_inc(post_pe, 1)
            pe.wait_ge(post_v, 2)
            for q in range(4):
                last = pe.matmul(PS[3][:, q:q + 1], cnt_row[0:1, q // 2, (q % 2) * P:(q % 2 + 1) * P], one[:],
                                 start=True, stop=True)
            last.then_inc(post_pe, 1)
            pe.wait_ge(post_v, 3)
            for k, t in enumerate((SIDX, V[SORTED], K[SORTED], CNT)):
                for q in range(4):
                    last = pe.transpose(PS[k // 2][:, (k % 2) * 512 + q * P:(k % 2) * 512 + (q + 1) * P],
                                        t[:, q * P:(q + 1) * P], ident[:])
            last.then_inc(post_pe, 1)
            pe.wait_ge(idx_ready, 1)

            def transposed(ps, t, tiles=W, p=P, width=D):
                for i in range(tiles):
                    last = pe.transpose(ps[0:width, i * P:i * P + p], t(i), ident[0:p, 0:p])
                return last

            def times(ps, parts, tiles=W, p=P):
                for i in range(tiles):
                    for k, (t, w) in enumerate(parts):
                        last = pe.matmul(ps[0:p, i * P:i * P + D], t(i), w, start=k == 0, stop=k == len(parts) - 1)
                return last

            columns = lambda t: lambda i: t[:, i * D:(i + 1) * D]
            columns_T = lambda t: lambda i: t[:, i * DP:(i + 1) * DP]
            tile = lambda t: lambda i: t[:, i, :]
            tile_T = lambda t, rows=D1: lambda i: t[0:rows, i * P:(i + 1) * P]
            w97 = lambda n: wt[:, n, :]
            w96 = lambda n: wt[0:D, n, :]

            def dense(j, s):
                ps, v, a = PS[(s + 1) % DS], d_v[s], d_act[s]

                def turned(rows, name):
                    d_pe[s].done(transposed(ps, columns(rows[s]), DT, DP), name)

                def x_turned():
                    on(pe, d_ld[s], j, "x")
                    on(pe, v, j, "out", back=1)
                    turned(dX, "xT")

                def made(step, rows, name):
                    on(pe, v, j, step)
                    turned(rows, name)

                def product(turned_name, w, name):
                    on(pe, a, j, turned_name)
                    d_pe[s].done(times(ps, [(columns_T(dXT[s]), w97(w))], DT, DP), name)

                return [(0, x_turned), (2, lambda: product("xT", A0, "mm")),
                        (7, lambda: made("x1", dA, "x1T")), (9, lambda: product("x1T", SELF0, "mm0")),
                        (13, lambda: made("h1", dC, "h1T")), (15, lambda: product("h1T", SELF1, "mm1")),
                        (24, lambda: made("x3", dC, "x3T")), (26, lambda: product("x3T", SOFTI, "mm3"))]

            dense_rounds(pe, dense, 0, ROUNDS4, START4)

            for k, r in enumerate(cheb[:2]):
                def sums(g, b, i, k=k, r=r):
                    if k == 0:
                        on(pe, r.v[2], g, "scaled")
                    else:
                        on(pe, r.ga[b], i, "all")
                    on(pe, r.v[1], g, "u", back=2 if k else 1)
                    r.pe[0].done(transposed(PS[b if k else 0], tile(GB[b])), "zT")

                def back(g, b, i, k=k, r=r):
                    on(pe, r.v[0], g, "scan")
                    ps = PS[b if k else 0]
                    for t in range(W):
                        last = pe.transpose(ps[:, t * P:t * P + D], SC[b][0:D, t * P:(t + 1) * P], ident[0:D, 0:D])
                    r.pe[1].done(last, "back")

                if k:
                    staged(pe, (sums, 0), (back, 1))
                else:
                    first_round(pe, dense, (2, sums, 0), (6, back, 0), (17, sums, 1), (21, back, 1))
                finished(pe, r)
            r = cheb[2]

            def mix(g, b, i, r=r):
                yield r.at["pe0 zT"]
                on(pe, r.ga[b], i, "all")
                on(pe, r.v[0], g, "y", back=1)
                r.pe[0].done(transposed(PS[0], tile(GB[b])), "zT")
                yield r.at["pe0 mix"]
                on(pe, r.v[0], g, "scan")
                on(pe, r.ld[b], i, "all")
                r.pe[0].done(times(PS[0], [(tile_T(DEN[b], D), w96(B1)), (tile_T(NUM[b], D), w96(B2)),
                                           (tile_T(SC[b], D), w96(B3))]), "mix")

            def own(g, b, i, r=r):
                yield r.at["pe1 xT"]
                on(pe, r.lr[b], i, "all")
                on(pe, r.v[1], g, "pre", back=1)
                r.pe[1].done(transposed(PS[1], tile(RB[b])), "xT")
                yield r.at["pe1 self"]
                on(pe, r.act[1], g, "xT")
                r.pe[1].done(times(PS[1], [(tile_T(XT[0]), w97(A0))]), "self")

            def depths(g, b, i, r=r):
                yield r.at["pe2 x1T"]
                on(pe, r.v[1], g, "x1")
                on(pe, r.v[2], g, "h2", back=1)
                r.pe[2].done(transposed(PS[2], tile(OR[b])), "x1T")
                yield r.at["pe2 self"]
                on(pe, r.act[2], g, "x1T")
                r.pe[2].done(times(PS[2], [(tile_T(XT[1]), w97(SELF0))]), "self")
                yield r.at["pe2 h1T"]
                on(pe, r.v[2], g, "h1")
                r.pe[2].done(transposed(PS[2], tile(eH[1])), "h1T")
                yield r.at["pe2 self1"]
                on(pe, r.act[2], g, "h1T")
                r.pe[2].done(times(PS[2], [(tile_T(XT[1]), w97(SELF1))]), "self1")

            def last(g, b, i, r=r):
                yield r.at["pe3 x3T"]
                on(pe, r.v[3], g, "x3")
                on(pe, r.v[3], g, "out", back=1)
                r.pe[3].done(transposed(PS[3], tile(eQ)), "x3T")
                yield r.at["pe3 out"]
                on(pe, r.act[3], g, "x3T")
                r.pe[3].done(times(PS[3], [(tile_T(XT[2]), w97(SOFTI))]), "out")
            staged(pe, (mix, 0), (own, 1), (depths, 2), (last, 3))
            finished(pe, r)

            r = sage1

            def src_rows(g, b, i, r=r):
                on(pe, r.ga[b], i, "all")
                on(pe, r.v[0], g, "scan", back=1)
                r.pe[0].done(transposed(PS[3], tile(RB[b])), "rT")
                yield
                on(pe, r.v[0], g, "scan")
                on(pe, r.act[0], g, "agg", back=1)
                r.pe[0].done(times(PS[0], [(tile_T(SC[b]), w97(NB0))]), "agg")
                yield

            def dst_rows(g, b, i, r=r):
                on(pe, r.gb[b], i, "all")
                on(pe, r.v[1], g, "h", back=2)
                r.pe[1].done(transposed(PS[1 + b], tile(TB[b])), "tT")
                yield
                on(pe, r.act[1], g, "tT")
                r.pe[1].done(times(PS[1 + b], [(tile_T(XT[1]), w97(SELF0))]), "self")
                yield
            staged(pe, (src_rows, 0), (dst_rows, 0))
            finished(pe, r)

            r = sage2

            def src_self(g, b, i, r=r):
                yield r.at["pe0 rT"]
                on(pe, r.ld[b], i, "all")
                on(pe, r.v[0], g, "h", back=1)
                r.pe[0].done(transposed(PS[0], tile(RB[b])), "rT")
                yield r.at["pe0 self"]
                on(pe, r.act[0], g, "rT")
                r.pe[0].done(times(PS[0], [(tile_T(XT[0]), w97(SELF0))]), "self")

            def src_agg(g, b, i, r=r):
                yield r.at["pe1 h1T"]
                on(pe, r.v[1], g, "h1")
                on(pe, r.v[1], g, "scan", back=1)
                r.pe[1].done(transposed(PS[3], tile(RH[b])), "h1T")
                yield r.at["pe1 agg"]
                on(pe, r.v[1], g, "scan")
                on(pe, r.act[1], g, "agg", back=1)
                r.pe[1].done(times(PS[1], [(tile_T(SC[b]), w97(NB1))]), "agg")

            def dst_self(g, b, i, r=r):
                yield r.at["pe2 tT"]
                on(pe, r.lt[b], i, "all")
                on(pe, r.v[2], g, "h", back=1)
                r.pe[2].done(transposed(PS[2], tile(TH[b])), "tT")
                yield r.at["pe2 self"]
                on(pe, r.act[2], g, "tT")
                r.pe[2].done(times(PS[2], [(tile_T(XT[1]), w97(SELF1))]), "self")
            staged(pe, (src_self, 0), (src_agg, 1), (dst_self, 2))
            finished(pe, r)

            r = meanr

            def src_self(g, b, i, r=r):
                yield r.at["pe0 rT"]
                on(pe, r.ld[b], i, "all")
                on(pe, r.v[0], g, "h", back=1)
                r.pe[0].done(transposed(PS[0], tile(TH[b])), "rT")
                yield r.at["pe0 self"]
                on(pe, r.act[0], g, "rT")
                r.pe[0].done(times(PS[0], [(tile_T(XT[0]), w97(SELF1))]), "self")

            def src_agg(g, b, i, r=r):
                yield r.at["pe2 x2T"]
                on(pe, r.v[2], g, "x2")
                on(pe, r.v[2], g, "scan", back=1)
                r.pe[2].done(transposed(PS[3], tile(RH[b])), "x2T")
                yield r.at["pe2 agg"]
                on(pe, r.v[2], g, "scan")
                on(pe, r.v[2], g, "agg", back=1)
                r.pe[2].done(times(PS[1], [(tile_T(SC[b]), w97(MEANW))]), "agg")
            staged(pe, (src_self, 0), (src_agg, 2))
            finished(pe, r)

            r = softr

            def src_T(g, b, i, r=r):
                yield r.at["pe0 x3T"]
                on(pe, r.v[0], g, "x3")
                on(pe, r.act[1], g, "relu", back=2)
                r.pe[0].done(transposed(PS[b], tile(eH[b])), "x3T")

            def dst_out(g, b, i, r=r):
                yield r.at["pe2 tT"]
                on(pe, r.lt[b], i, "all")
                on(pe, r.v[2], g, "out", back=1)
                r.pe[2].done(transposed(PS[2], tile(TB[b])), "tT")
                yield r.at["pe2 out"]
                on(pe, r.act[2], g, "tT")
                on(pe, r.v[3], g, "msg")
                r.pe[2].done(times(PS[2], [(tile_T(XT[1]), w97(SOFTI)), (tile_T(MS[b], D), w96(SOFTW))]), "out")
            staged(pe, (src_T, 0), (dst_out, 3))

        @block.scalar
        def _(act):
            credit(act, "act", d_act)
            cur = n = 0
            for op in sort_plan():
                if op[0] == "step":
                    cur ^= 1
                if op[0] != "switch":
                    continue
                n += 1
                cur ^= 1
                act.wait_ge(switched, 2 * n)
                act.copy(V[cur], PS[1][:, 0:512]).then_inc(v_back, 1)

            act.wait_ge(post_v, 4)
            act.activation(MX[1][:, 0:512], PS[1][:, 512:1024], ACT.Sqrt).then_inc(roots, 1)

            LN = float(D) ** -0.5
            STD = float(D - 1) ** -0.5

            def from_T(out, ps):
                return act.copy(out[0:D, :], ps[0:D, :])

            def square(out, in_, scale):
                return act.activation(out, in_, ACT.Square, scale=scale)

            def deviation(m, p, scale=1.0, bias=0.0):
                return act.activation(m[:, 3, :], m[:, 0, :], ACT.Sqrt, scale=scale, bias=bias)

            eps_ = eps[:, :]
            act.wait_ge(idx_ready, 1)

            def plain_std(m):
                return act.activation(m[:, 3, :], m[:, 2, :], ACT.Sqrt, scale=1.0 / (D - 1))

            def dense(j, s):
                ps, pe_, v, m, a = PS[(s + 1) % DS], d_pe[s], d_v[s], dsm[s], d_act[s]
                rows = rows_of(ps, DP, DT)

                def turned(name):
                    on(act, pe_, j, name)
                    a.done(from_T(dXT[s], ps), name)

                def squares(after, step, out, rows, scale, name):
                    on(act, after, j, step)
                    a.done(square(out, rows, scale), name)

                def root(step, name, make):
                    on(act, v, j, step)
                    a.done(make(), name)

                B, e = by_tile(dB[s]), eps[0:DP, :]
                return [(1, lambda: turned("xT")), (3, lambda: squares(pe_, "mm", B, rows, LN, "sq")),
                        (5, lambda: root("sum", "sd", lambda: deviation(m, DP, 1.0, e))),
                        (8, lambda: turned("x1T")), (11, lambda: root("m2s", "sd1", lambda: plain_std(m))),
                        (14, lambda: turned("h1T")), (16, lambda: squares(pe_, "mm1", B, rows, STD, "sq2")),
                        (18, lambda: root("sum2", "sd2", lambda: deviation(m, DP))),
                        (20, lambda: squares(v, "z", dC[s][:, :], dB[s][:, :], LN, "sqz")),
                        (22, lambda: root("sumz", "sdz", lambda: deviation(m, DP, 1.0 + LN_EPS, eps2[0:DP, :]))),
                        (25, lambda: turned("x3T")), (27, lambda: squares(pe_, "mm3", B, rows, LN, "sqo")),
                        (29, lambda: root("sumo", "sdo", lambda: deviation(m, DP, 1.0, e)))]

            dense_rounds(act, dense, 0, ROUNDS4, START4)
            dense_rounds(act, dense, ROUNDS4, BESIDE, START3)
            finished(act, cheb[1])

            r = cheb[2]

            def own(g, b, i, r=r):
                yield r.at["act1 xT"]
                on(act, r.pe[1], g, "xT")
                on(act, r.pe[1], g, "self", back=1)
                r.act[1].done(act.copy(XT[0][0:D, :], PS[1][0:D, 0:GE]), "xT")
                yield r.at["act1 sq"]
                on(act, r.v[1], g, "pre")
                on(act, r.v[1], g, "sum", back=1)
                r.act[1].done(square(eSQ[0], eH[0][:], LN), "sq")
                yield r.at["act1 sd"]
                on(act, r.v[1], g, "sum")
                r.act[1].done(deviation(esm[1], P, 1.0, eps_), "sd")

            def depths(g, b, i, r=r):
                yield r.at["act2 x1T"]
                on(act, r.pe[2], g, "x1T")
                on(act, r.pe[2], g, "self1", back=1)
                r.act[2].done(act.copy(XT[1][0:D, :], PS[2][0:D, 0:GE]), "x1T")
                yield r.at["act2 sd1"]
                on(act, r.v[2], g, "m2s")
                r.act[2].done(plain_std(esm[2]), "sd1")
                yield r.at["act2 h1T"]
                on(act, r.pe[2], g, "h1T")
                r.act[2].done(act.copy(XT[1][0:D, :], PS[2][0:D, 0:GE]), "h1T")
                yield r.at["act2 sq"]
                on(act, r.pe[2], g, "self1")
                on(act, r.v[2], g, "sum", back=1)
                r.act[2].done(square(eSQ[1], rows_of(PS[2], P, W), STD), "sq")
                yield r.at["act2 sd"]
                on(act, r.v[2], g, "sum")
                r.act[2].done(deviation(esm[2], P), "sd")

            def last(g, b, i, r=r):
                yield r.at["act3 sqz"]
                on(act, r.v[2], g, "z")
                on(act, r.v[3], g, "sumo", back=1)
                r.act[3].done(square(eSQ[2], eZ[b][:], LN), "sqz")
                yield r.at["act3 sdz"]
                on(act, r.v[3], g, "sumz")
                r.act[3].done(deviation(esm[3], P, 1.0 + LN_EPS, eps2[:, :]), "sdz")
                yield r.at["act3 x3T"]
                on(act, r.pe[3], g, "x3T")
                on(act, r.pe[3], g, "out", back=1)
                r.act[3].done(act.copy(XT[2][0:D, :], PS[3][0:D, 0:GE]), "x3T")
                yield r.at["act3 sqo"]
                on(act, r.pe[3], g, "out")
                r.act[3].done(square(eSQ[2], rows_of(PS[3], P, W), LN), "sqo")
                yield r.at["act3 sdo"]
                on(act, r.v[3], g, "sumo")
                r.act[3].done(deviation(esm[3], P, 1.0, eps_), "sdo")
            staged(act, (own, 1), (depths, 2), (last, 3))
            finished(act, r)

            r = sage1

            def src_rows(g, b, i, r=r):
                yield 1
                on(act, r.pe[0], g, "agg")
                on(act, r.st[b], i, "all", back=1)
                on(act, r.v[1], g, "h", back=2)
                r.act[0].done(act.copy(AR[b][:], rows_of(PS[0], P, W)), "agg")
                yield

            def dst_rows(g, b, i, r=r):
                on(act, r.pe[1], g, "tT")
                on(act, r.pe[1], g, "self", back=1)
                r.act[1].done(act.copy(XT[1][0:D, :], PS[1 + b][0:D, 0:GE]), "tT")
                yield

            def dst_h1(g, b, i, r=r):
                yield 1
                on(act, r.v[2], g, "m2s")
                r.act[2].done(plain_std(esm[2]), "sd")
                yield
            staged(act, (dst_rows, 0), (dst_h1, 1), (src_rows, 0))
            finished(act, r)

            r = sage2

            def src_self(g, b, i, r=r):
                yield r.at["act0 rT"]
                on(act, r.pe[0], g, "rT")
                on(act, r.pe[0], g, "self", back=1)
                r.act[0].done(act.copy(XT[0][0:D, :], PS[0][0:D, 0:GE]), "rT")

            def src_agg(g, b, i, r=r):
                yield r.at["act1 sd"]
                on(act, r.v[1], g, "m2s")
                r.act[1].done(plain_std(esm[1]), "sd")
                yield r.at["act1 agg"]
                on(act, r.pe[1], g, "agg")
                on(act, r.st[b], i, "all", back=1)
                on(act, r.v[2], g, "h", back=2)
                r.act[1].done(act.copy(AR[b][:], rows_of(PS[1], P, W)), "agg")

            def dst_self(g, b, i, r=r):
                yield r.at["act2 tT"]
                on(act, r.pe[2], g, "tT")
                on(act, r.pe[2], g, "self", back=1)
                r.act[2].done(act.copy(XT[1][0:D, :], PS[2][0:D, 0:GE]), "tT")
                yield r.at["act2 sq"]
                on(act, r.v[2], g, "h")
                on(act, r.v[2], g, "sum", back=1)
                r.act[2].done(square(eSQ[0], eQ, STD), "sq")
                yield r.at["act2 sd"]
                on(act, r.v[2], g, "sum")
                r.act[2].done(deviation(esm[2], P), "sd")

            def normed(r, stage, Z, sq):
                def program(g, b, i):
                    yield r.at[f"act{stage} sqz"]
                    made = r.v[stage] if "z" in r.v[stage].names else r.v[stage - 1]
                    on(act, made, g, "z")
                    on(act, r.v[stage], g, "sumz", back=1)
                    r.act[stage].done(square(sq, Z(b), LN), "sqz")
                    yield r.at[f"act{stage} sdz"]
                    on(act, r.v[stage], g, "sumz")
                    r.act[stage].done(deviation(esm[stage], P, 1.0, eps_), "sdz")
                return program

            staged(act, (src_self, 0), (src_agg, 1), (dst_self, 2), (normed(r, 3, lambda b: eZ[b][:], eSQ[1]), 3))
            finished(act, r)

            r = meanr

            def src_z(g, b, i, r=r):
                yield r.at["act1 sq"]
                on(act, r.v[0], g, "h")
                on(act, r.v[1], g, "sum", back=1)
                r.act[1].done(square(eSQ[0], eH[b][:], STD), "sq")
                yield r.at["act1 sd"]
                on(act, r.v[1], g, "sum")
                r.act[1].done(deviation(esm[1], P), "sd")
            staged(act, (lambda g, b, i: src_self(g, b, i, r=meanr), 0), (src_z, 1),
                   (normed(r, 2, lambda b: eZ[b][:], eSQ[1]), 2), (normed(r, 3, lambda b: eQ, eSQ[2]), 3))
            finished(act, r)

            r = softr

            def weights(g, b, i, r=r):
                yield r.at["act1 relu"]
                f = lambda t: t[0:D, 0:GE]
                on(act, r.pe[0], g, "x3T")
                on(act, r.v[1], g, "num", back=1)
                r.act[1].done(act.activation(f(MB), PS[b][0:D, 0:GE], ACT.Relu), "relu")
                yield r.at["act1 m"]
                on(act, r.act[1], g, "relu")
                r.act[1].done(act.activation(f(MB), f(MB), ACT.Identity, bias=msg_eps[0:D, :]), "m")
                yield r.at["act1 down"]
                on(act, r.v[1], g, "less")
                r.act[1].done(act.activation(f(DEC), f(DEC), ACT.Relu, scale=-1.0), "down")
                yield r.at["act1 dec"]
                on(act, r.act[1], g, "down")
                r.act[1].done(act.activation(f(DEC), f(DEC), ACT.Exp, scale=-1.0), "dec")
                yield r.at["act1 ex"]
                on(act, r.v[1], g, "off")
                r.act[1].done(act.activation(f(EX), f(EX), ACT.Exp), "ex")

            def quotients(g, b, i, r=r):
                f = lambda t: t[0:D, 0:GE]
                yield r.at["act3 ln"]
                on(act, r.v[1], g, "den")
                on(act, r.pe[2], g, "out", back=2)
                r.act[3].done(act.activation(f(MS[b]), f(DEN[b]), ACT.Ln), "ln")
                yield r.at["act3 inverse"]
                on(act, r.act[3], g, "ln")
                r.act[3].done(act.activation(f(MS[b]), f(MS[b]), ACT.Exp, scale=-1.0), "inverse")

            def dst_out(g, b, i, r=r):
                yield r.at["act2 tT"]
                on(act, r.pe[2], g, "tT")
                on(act, r.pe[2], g, "out", back=1)
                r.act[2].done(act.copy(XT[1][0:D, :], PS[2][0:D, 0:GE]), "tT")
                yield r.at["act2 sqo"]
                on(act, r.pe[2], g, "out")
                on(act, r.v[2], g, "sumo", back=1)
                r.act[2].done(square(eSQ[1], rows_of(PS[2], P, W), LN), "sqo")
                yield r.at["act2 sdo"]
                on(act, r.v[2], g, "sumo")
                r.act[2].done(deviation(esm[2], P, 1.0, eps_), "sdo")
            staged(act, (normed(r, 0, lambda b: eZ[b][:], eSQ[0]), 0), (weights, 1), (dst_out, 3), (quotients, 2))

        @block.vector
        def _(dve):
            credit(dve, "v", d_v)
            count = [0]

            def do(instruction):
                count[0] += 1
                instruction.then_inc(sort_step, 1)
                return count[0]

            def need(*numbers):
                dve.wait_ge(sort_step, max(numbers))

            for t, value in ((ones[:], 1.0), (one[:], 1.0), (cnt_row[:], 0.0),
                             (eps[:], LN_EPS), (msg_eps[:], MSG_EPS), (eps2[:], LN_EPS * LN_EPS),
                             *((t[D:D1, :], 1.0) for t in (*dXT, *XT))):
                do(dve.memset(t, value))
            dve.wait_ge(pool_init, POOL_INITS)
            dve.wait_ge(loaded_w, 16 * WEIGHT_LOADS)
            dve.wait_ge(prep_pe, 1)
            a = do(dve.tensor_copy(wT[:], PS[0][0:D, 0:512].rearrange("p (q c) -> p q c", c=P)[:, :, 0:D1]))
            need(a)
            dve.sem_inc(prep_v, 1)
            dve.wait_ge(prep_pe, 2)
            q4 = lambda q: PS[1][0:D1, q * P:q * P + D]
            for q, w in ((0, SELF0), (1, SELF1), (2, NB0), (3, NB1)):
                a = do(dve.tensor_copy(wt[:, w, :], q4(q)))
            need(a)
            for q, w in ((0, SELF0), (1, SELF1)):
                a = do(dve.tensor_tensor(wt[D:D1, w, :], wt[D:D1, w, :], b2row[D:D1, q, :], ALU.add))
            dve.sem_inc(prep_v, 1)
            idn = ident[0:D, 0:D]
            c = lambda k: chebw[:, k, :]
            a = do(dve.tensor_tensor(wt[0:D, A0, :], c(0), c(2), ALU.subtract))
            do(dve.scalar_tensor_tensor(wt[0:D, B1, :], c(3), -3.0, c(1), ALU.mult, ALU.add))
            do(dve.tensor_scalar(wt[0:D, B2, :], c(2), 2.0, None, ALU.mult))
            do(dve.tensor_scalar(wt[0:D, B3, :], c(3), 4.0, None, ALU.mult))
            do(dve.tensor_copy(wt[0:D, SOFTI, :], wt[0:D, SOFTW, :]))
            need(count[0])
            do(dve.tensor_tensor(wt[0:D, A0, :], wt[0:D, A0, :], idn, ALU.add))
            a = do(dve.tensor_tensor(wt[0:D, SOFTI, :], wt[0:D, SOFTI, :], idn, ALU.add))
            need(a)
            a = do(dve.tensor_reduce(wmean[:], wt[:, 0:9, :], AX.X, ALU.add))
            need(a)
            a = do(dve.tensor_scalar(wmean[:], wmean[:], -1.0 / D, None, ALU.mult))
            need(a)
            a = do(dve.tensor_tensor(wt[:, 0:9, :], wt[:, 0:9, :], spread(wmean[:], D1, 9), ALU.add))
            need(a)
            dve.wait_ge(loaded_e, 16 * 12)
            k_in = do(dve.tensor_copy(K[0], key_i[:].rearrange("p s c -> p (s c)")))
            v_in = do(dve.tensor_copy(V[0], pay_i[:].rearrange("p s c -> p (s c)")))

            cur = n = 0
            k_ok, v_ok = k_in, v_in

            def blocks(t, half, part):
                return t.rearrange("p (s two d) -> p s two d", two=2, d=half)[:, :, part, :]

            for op in sort_plan():
                if op[0] == "flip":
                    back, on_ = op[1], op[2]
                    if back is None and on_ is None:
                        continue
                    if back is not None and on_ is not None:
                        quarter = 1 << back
                        t = K[cur].rearrange("p (s four d) -> p s four d", four=4, d=quarter)[:, :, 1:3, :]
                    else:
                        t = blocks(K[cur], 1 << (on_ if back is None else back), 1)
                    need(k_ok)
                    k_ok = do(dve.tensor_scalar(t, t, -1.0, None, ALU.mult))
                elif op[0] == "switch":
                    n += 1
                    need(max(k_ok, v_ok))
                    dve.sem_inc(switch_ready, 1)
                    cur ^= 1
                    dve.wait_ge(switched, 2 * n - 1)
                    k_ok = do(dve.tensor_copy(K[cur], PS[0][:, 0:512]))
                    dve.wait_ge(v_back, n)
                    v_ok = k_ok
                else:
                    d = op[1]
                    ka, kb, va, vb = (blocks(t, d, part) for t in (K[cur], V[cur]) for part in (0, 1))
                    new = cur ^ 1
                    nka, nkb, nva, nvb = (blocks(t, d, part) for t in (K[new], V[new]) for part in (0, 1))
                    mask = MASK[cur][:, 0:256].rearrange("p (s d) -> p s d", d=d)
                    dif = DIF[:, 0:256].rearrange("p (s d) -> p s d", d=d)
                    need(k_ok)
                    do(dve.tensor_tensor(nka, ka, kb, ALU.min))
                    m = do(dve.tensor_tensor(mask, ka, kb, ALU.is_gt))
                    need(v_ok)
                    f = do(dve.tensor_tensor(dif, vb, va, ALU.subtract))
                    k_ok = do(dve.tensor_tensor(nkb, ka, kb, ALU.max))
                    need(m, f)
                    f = do(dve.tensor_tensor(dif, dif, mask, ALU.mult))
                    need(f)
                    do(dve.tensor_tensor(nva, va, dif, ALU.add))
                    v_ok = do(dve.tensor_tensor(nvb, vb, dif, ALU.subtract))
                    cur = new
            assert cur == SORTED
            KS = K[cur]
            need(v_ok, k_ok)
            dve.sem_inc(keys_out, 1)

            dve.wait_ge(keys_in, 16 * 6)
            a = do(dve.tensor_tensor(CONT, KS, KPREV, ALU.is_equal))
            f = do(dve.tensor_tensor(KNEXT, KS, KNEXT, ALU.is_equal))
            need(f)
            dve.sem_inc(keys_out, 1)
            do(dve.scalar_tensor_tensor(SIDX, KNEXT, FAR, KS, ALU.mult, ALU.add))
            for q in range(4):
                part = slice(q * P, (q + 1) * P)
                do(dve.tensor_tensor_scan(LOCAL[:, part], CONT[:, part], ones[:], 0.0, ALU.mult, ALU.add))
                a = do(dve.tensor_tensor_scan(CPROD[:, part], CONT[:, part], ones[:], 1.0, ALU.mult, ALU.mult))
            need(a)
            dve.sem_inc(post_v, 1)
            dve.wait_ge(post_pe, 1)
            a = do(dve.tensor_copy(cnt_in[:], PS[2][0:1, :]))
            need(a)
            for side in range(2):
                row = slice(side * SORT_COLS, (side + 1) * SORT_COLS)
                goes_on = slice((side + 2) * SORT_COLS, (side + 3) * SORT_COLS)
                a = do(dve.tensor_tensor_scan(cnt_row[0:1, side, 1:SORT_COLS + 1], cnt_in[:, goes_on], cnt_in[:, row],
                                              0.0, ALU.mult, ALU.add))
            need(a)
            dve.sem_inc(post_v, 1)
            dve.wait_ge(post_pe, 2)
            a = do(dve.tensor_copy(cnt_col[:], PS[3][:, 0:4]))
            need(a)
            for q in range(4):
                part = slice(q * P, (q + 1) * P)
                a = do(dve.scalar_tensor_tensor(CNT[:, part], CPROD[:, part], cnt_col[:, q:q + 1], LOCAL[:, part],
                                                ALU.mult, ALU.add))
            need(a)
            dve.sem_inc(post_v, 1)
            dve.wait_ge(post_pe, 3)
            flat = lambda t: t[:].rearrange("p s c -> p (s c)")
            do(dve.tensor_copy(flat(scat_i), PS[0][:, 0:512]))
            do(dve.tensor_copy(flat(pay_i), PS[0][:, 512:1024]))
            do(dve.tensor_scalar(flat(key_i), PS[1][:, 0:512], float(N - 1), None, ALU.min))
            for side in range(2):
                do(dve.tensor_copy(mapv[:, side, 0:TILES, 0], pos_i[:, 0:TILES]))
            b_ = do(dve.reciprocal(nrc[:], PS[1][:, 512:768]))
            do(dve.tensor_scalar(rcb[:], PS[1][:, 768:1024], 1.0, None, ALU.max))
            need(count[0])
            dve.sem_inc(post_v, 1)
            dve.wait_ge(roots, 1)
            a = do(dve.reciprocal(mapv[:, :, :, 1], MX[1][:, 0:512].rearrange("p (s c) -> p s c", s=2)))
            need(a)
            do(dve.tensor_scalar(ndinv[:], mapv[:, 0, :, 1], -1.0, None, ALU.mult))
            do(dve.tensor_scalar(nrc[:], nrc[:], -1.0, None, ALU.mult))
            a = do(dve.reciprocal(rcb[:], rcb[:]))
            a = do(dve.memset(SC[1][:, GE - 1:GE], 0.0))
            for t in MX:
                a = do(dve.memset(t[:, GE:GE + 1], 0.0))
            need(a)
            dve.sem_inc(idx_ready, 1)

            def means(out, sq):
                return dve.tensor_reduce(out, sq, AX.X, ALU.add)

            def inverse(m):
                return dve.reciprocal(m[:, 1, :], m[:, 3, :])

            def scale_by(out, rows, m, p, tiles):
                return dve.tensor_tensor(out, rows, spread(m[:, 1, :], p, tiles), ALU.mult)

            def about_mean(v, i, rows, six, m, tiles):
                for t in range(tiles):
                    ins = dve.bn_stats(six[:, t, :], rows[:, t, :])
                v.done(ins, "bn")
                on(dve, v, i, "bn")
                v.done(dve.tensor_tensor(m[:, 0, :], six[:, :, 1], six[:, :, 4], ALU.subtract), "dm")
                v.done(dve.tensor_tensor(m[:, 2, :], six[:, :, 2], six[:, :, 5], ALU.add), "m2")
                on(dve, v, i, "dm")
                v.done(dve.scalar_tensor_tensor(m[:, 1, :], m[:, 0, :], D / 4.0, m[:, 0, :], ALU.mult, ALU.mult), "dm2")
                on(dve, v, i, "dm2")
                v.done(dve.tensor_tensor(m[:, 2, :], m[:, 1, :], m[:, 2, :], ALU.add), "m2s")

            def dense(j, s):
                v, a_, m, ps = d_v[s], d_act[s], dsm[s], PS[(s + 1) % DS]
                rows = rows_of(ps, DP, DT)
                A, B, C = (by_tile(t[s]) for t in (dA, dB, dC))

                def summed(step, sq, name):
                    on(dve, a_, j, step)
                    v.done(means(m[:, 0, :], sq), name)

                def scaled(step, r, out, rows, name, free=None):
                    on(dve, a_, j, step)
                    if free:
                        free()
                    v.done(inverse(m), r)
                    on(dve, v, j, r)
                    v.done(scale_by(out, rows, m, DP, DT), name)

                def spread_about_mean():
                    on(dve, d_pe[s], j, "mm0")
                    about_mean(v, j, rows, d_six[s], m, DT)

                def residual():
                    scaled("sd2", "r2", B, rows, "h2")
                    on(dve, v, j, "h2")
                    v.done(dve.tensor_tensor(B, B, A, ALU.add), "z")

                return [(4, lambda: summed("sq", B, "sum")),
                        (6, lambda: scaled("sd", "r", A, rows, "x1", lambda: on(dve, d_so[s], j, "out", back=1))),
                        (10, spread_about_mean), (12, lambda: scaled("sd1", "r1", C, rows, "h1")),
                        (17, lambda: summed("sq2", B, "sum2")), (19, residual),
                        (21, lambda: summed("sqz", C, "sumz")), (23, lambda: scaled("sdz", "rz", C, B, "x3")),
                        (28, lambda: summed("sqo", B, "sumo")),
                        (30, lambda: scaled("sdo", "ro", A, rows, "out", lambda: on(dve, d_sx[s], j, "x1")))]

            dense_rounds(dve, dense, 0, ROUNDS4, START4)

            dve.wait_ge(map_out, 2 * GROUPS)
            a = do(dve.tensor_copy(found_i[:], found[:, :, :, 0]))
            need(a)
            dve.sem_inc(found_ready, 1)

            def cols(t, g):
                return t[:, bass.ds(g * W, W)]

            def scan(out, flags_, values, before, op1=ALU.add):
                return dve.tensor_tensor_scan(out, flags_, values, before, ALU.mult, op1)

            def sums(r, stage, g, b, i, rows, source):
                on(dve, r.fl[b], i, "all")
                on(dve, r.v[stage], g, "scan", back=1)
                r.v[stage].done(scan(SC[b][0:rows, :], FL[b][0:rows, :], source[0:rows, 0:GE],
                                     SC[b ^ 1][0:rows, GE - 1:GE]), "scan")

            for k, r in enumerate(cheb[:2]):
                def scaled(g, b, i, r=r):
                    on(dve, r.ga[b], i, "all")
                    r.v[2].done(dve.tensor_tensor(GB[b][:], GB[b][:], spread(found[:, 0, bass.ds(g * W, W), 1], P, W),
                                                  ALU.mult), "scaled")

                def summed(g, b, i, k=k, r=r):
                    on(dve, r.pe[0], g, "zT")
                    on(dve, r.pe[1], g, "back", back=2)
                    on(dve, r.st[b], i, "all", back=1)
                    sums(r, 0, g, b, i, D, PS[b if k else 0])

                def table(g, b, i, k=k, r=r):
                    on(dve, r.pe[1], g, "back")
                    on(dve, r.st[b], i, "all", back=1)
                    r.v[1].done(dve.tensor_tensor(OR[b][:], rows_of(PS[b if k else 0], P, W), spread(cols(nrc, g), P, W),
                                                  ALU.mult), "u")

                if k:
                    staged(dve, (summed, 0), (table, 1))
                else:
                    first_round(dve, dense, (0, scaled, 0), (4, summed, 0), (8, table, 0),
                                (15, scaled, 1), (19, summed, 1), (23, table, 1))
                finished(dve, r)
            r = cheb[2]

            def summed(g, b, i, r=r):
                yield r.at["v0 scan"]
                on(dve, r.pe[0], g, "zT")
                on(dve, r.pe[0], g, "mix", back=2)
                sums(r, 0, g, b, i, D, PS[0])
                yield r.at["v0 y"]
                on(dve, r.pe[0], g, "mix")
                on(dve, r.v[1], g, "pre", back=2)
                r.v[0].done(dve.tensor_tensor(TH[b][:], rows_of(PS[0], P, W), spread(cols(ndinv, g), P, W), ALU.mult), "y")

            def own(g, b, i, r=r):
                v = r.v[1]
                yield r.at["v1 pre"]
                on(dve, r.pe[1], g, "self")
                on(dve, r.v[0], g, "y")
                on(dve, v, g, "x1", back=1)
                v.done(dve.tensor_tensor(eH[0][:], TH[b][:], rows_of(PS[1], P, W), ALU.add), "pre")
                yield r.at["v1 sum"]
                on(dve, r.act[1], g, "sq")
                v.done(means(esm[1][:, 0, :], eSQ[0]), "sum")
                yield r.at["v1 x1"]
                on(dve, r.act[1], g, "sd")
                v.done(inverse(esm[1]), "r")
                on(dve, v, g, "r")
                on(dve, r.sc[b], i, "all", back=1)
                on(dve, r.v[2], g, "z", back=2)
                on(dve, r.pe[2], g, "x1T", back=2)
                v.done(scale_by(OR[b][:], eH[0][:], esm[1], P, W), "x1")

            def depths(g, b, i, r=r):
                v, a_, m, rows = r.v[2], r.act[2], esm[2], rows_of(PS[2], P, W)
                yield r.at["v2 bn"]
                on(dve, r.pe[2], g, "self")
                about_mean(v, g, rows, e_six[2], m, W)
                yield r.at["v2 h1"]
                on(dve, a_, g, "sd1")
                v.done(inverse(m), "r")
                on(dve, v, g, "r")
                on(dve, r.pe[2], g, "h1T", back=1)
                v.done(scale_by(eH[1][:], rows, m, P, W), "h1")
                yield r.at["v2 sum"]
                on(dve, a_, g, "sq")
                v.done(means(m[:, 0, :], eSQ[1]), "sum")
                yield r.at["v2 z"]
                on(dve, a_, g, "sd")
                v.done(inverse(m), "r2")
                on(dve, v, g, "r2")
                on(dve, r.v[3], g, "x3", back=2)
                v.done(scale_by(eZ[b][:], rows, m, P, W), "h2")
                on(dve, v, g, "h2")
                on(dve, r.v[1], g, "x1")
                v.done(dve.tensor_tensor(eZ[b][:], eZ[b][:], OR[b][:], ALU.add), "z")

            def last(g, b, i, r=r):
                v, a_, m = r.v[3], r.act[3], esm[3]
                yield r.at["v3 sumz"]
                on(dve, a_, g, "sqz")
                v.done(means(m[:, 0, :], eSQ[2]), "sumz")
                yield r.at["v3 x3"]
                on(dve, a_, g, "sdz")
                v.done(inverse(m), "rz")
                on(dve, v, g, "rz")
                on(dve, r.pe[3], g, "x3T", back=1)
                v.done(scale_by(eQ, eZ[b][:], m, P, W), "x3")
                yield r.at["v3 sumo"]
                on(dve, a_, g, "sqo")
                v.done(means(m[:, 0, :], eSQ[2]), "sumo")
                yield r.at["v3 out"]
                on(dve, a_, g, "sdo")
                v.done(inverse(m), "ro")
                on(dve, v, g, "ro")
                on(dve, r.so[b], i, "all", back=1)
                v.done(scale_by(AR[b][:], rows_of(PS[3], P, W), m, P, W), "out")
            staged(dve, (summed, 0), (own, 1), (depths, 2), (last, 3))
            finished(dve, r)

            need(do(dve.memset(PS[3][D:D1, 0:GE], 1.0)))
            r = sage1

            def src_rows(g, b, i, r=r):
                on(dve, r.pe[0], g, "rT")
                on(dve, r.pe[0], g, "agg", back=2)
                sums(r, 0, g, b, i, D1, PS[3])
                yield

            def dst_h(g, b, i, r=r):
                yield 1
                on(dve, r.pe[1], g, "self")
                on(dve, r.act[0], g, "agg")
                on(dve, r.v[2], g, "h1", back=2)
                r.v[1].done(dve.tensor_tensor(eH[b][:], rows_of(PS[1 + b], P, W), AR[b][:], ALU.add), "h")
                yield

            def deviated(r, stage, source, g, b, i, out, before):
                yield r.at[f"v{stage} bn"]
                v, m = r.v[stage], esm[stage]
                on(dve, r.v[stage - 1], g, "h")
                about_mean(v, g, source, e_six[stage], m, W)
                yield r.at[f"v{stage} h1"]
                on(dve, r.act[stage], g, "sd")
                v.done(inverse(m), "r")
                on(dve, v, g, "r")
                before()
                v.done(scale_by(out, source, m, P, W), "h1")

            def dst_h1(g, b, i, r=r):
                yield from deviated(r, 2, eH[b][:], g, b, i, TH[b][:], lambda: on(dve, r.su[b], i, "all", back=1))
            staged(dve, (src_rows, 0), (dst_h1, 1), (dst_h, 0))
            finished(dve, r)

            r = sage2

            def src_h(g, b, i, r=r, read="h1"):
                yield r.at["v0 h"]
                on(dve, r.pe[0], g, "self")
                on(dve, r.ga[b], i, "all")
                on(dve, r.v[1], g, read, back=2)
                r.v[0].done(dve.tensor_tensor(eH[b][:], rows_of(PS[0], P, W), GB[b][:], ALU.add), "h")

            def src_agg(g, b, i, r=r):
                def free():
                    on(dve, r.st[b], i, "all", back=1)
                    on(dve, r.pe[1], g, "h1T", back=2)
                yield from deviated(r, 1, eH[b][:], g, b, i, RH[b][:], free)
                yield r.at["v1 scan"]
                on(dve, r.pe[1], g, "h1T")
                on(dve, r.pe[1], g, "agg", back=2)
                sums(r, 1, g, b, i, D1, PS[3])

            def residual(r, stage, g, H, X, Z, sq, before):
                v, m = r.v[stage], esm[stage]
                yield r.at[f"v{stage} sum"]
                on(dve, r.act[stage], g, "sq")
                v.done(means(m[:, 0, :], sq), "sum")
                yield r.at[f"v{stage} z"]
                on(dve, r.act[stage], g, "sd")
                v.done(inverse(m), "r")
                on(dve, v, g, "r")
                before()
                v.done(scale_by(Z, H, m, P, W), "h2")
                on(dve, v, g, "h2")
                v.done(dve.tensor_tensor(Z, Z, X, ALU.add), "z")

            def normed(r, stage, g, out, name, Z, sq, before):
                v, m = r.v[stage], esm[stage]
                yield r.at[f"v{stage} sumz"]
                on(dve, r.act[stage], g, "sqz")
                v.done(means(m[:, 0, :], sq), "sumz")
                yield r.at[f"v{stage} {name}"]
                on(dve, r.act[stage], g, "sdz")
                v.done(inverse(m), "rz")
                on(dve, v, g, "rz")
                before()
                v.done(scale_by(out, Z, m, P, W), name)

            def dst_z(g, b, i, r=r):
                yield r.at["v2 h"]
                on(dve, r.pe[2], g, "self")
                on(dve, r.act[1], g, "agg")
                on(dve, r.v[2], g, "h2", back=1)
                r.v[2].done(dve.tensor_tensor(eQ, rows_of(PS[2], P, W), AR[b][:], ALU.add), "h")
                yield from residual(r, 2, g, eQ, TB[b][:], eZ[b][:], eSQ[0], lambda: on(dve, r.v[3], g, "x2", back=2))

            def dst_x2(g, b, i, r=r):
                yield from normed(r, 3, g, OR[b][:], "x2", eZ[b][:], eSQ[1], lambda: on(dve, r.su[b], i, "all", back=1))
            staged(dve, (src_h, 0), (src_agg, 1), (dst_z, 2), (dst_x2, 3))
            finished(dve, r)

            r = meanr

            def src_z(g, b, i, r=r):
                def free():
                    on(dve, r.lr[b], i, "all")
                    on(dve, r.v[2], g, "x2", back=2)
                yield from residual(r, 1, g, eH[b][:], RB[b][:], eZ[b][:], eSQ[0], free)

            def src_agg(g, b, i, r=r):
                def free():
                    on(dve, r.st[b], i, "all", back=1)
                    on(dve, r.pe[2], g, "x2T", back=2)
                yield from normed(r, 2, g, RH[b][:], "x2", eZ[b][:], eSQ[1], free)
                yield r.at["v2 scan"]
                on(dve, r.pe[2], g, "x2T")
                on(dve, r.pe[2], g, "agg", back=2)
                sums(r, 2, g, b, i, D1, PS[3])
                yield r.at["v2 agg"]
                on(dve, r.pe[2], g, "agg")
                on(dve, r.st[b], i, "all", back=1)
                on(dve, r.v[3], g, "z", back=2)
                r.v[2].done(dve.tensor_tensor(AR[b][:], rows_of(PS[1], P, W), spread(cols(rcb, g), P, W), ALU.mult), "agg")

            def dst_x3(g, b, i, r=r):
                yield r.at["v3 z"]
                on(dve, r.lt[b], i, "all")
                on(dve, r.v[2], g, "agg")
                on(dve, r.v[3], g, "x3", back=1)
                r.v[3].done(dve.tensor_tensor(eQ, TB[b][:], AR[b][:], ALU.add), "z")
                yield from normed(r, 3, g, OR[b][:], "x3", eQ, eSQ[2], lambda: on(dve, r.su[b], i, "all", back=1))
            staged(dve, (lambda g, b, i: src_h(g, b, i, r=meanr, read="h2"), 0), (src_z, 1), (src_agg, 2), (dst_x3, 3))
            finished(dve, r)

            for t in (DEN[1], NUM[1]):
                a = do(dve.memset(t[0:D, GE - 1:GE], 0.0))
            need(a)
            r = softr

            def src_x3(g, b, i, r=r):
                yield r.at["v0 z"]
                on(dve, r.ga[b], i, "all")
                on(dve, r.ld[b], i, "all")
                on(dve, r.v[0], g, "x3", back=2)
                r.v[0].done(dve.tensor_tensor(eZ[b][:], RB[b][:], GB[b][:], ALU.add), "z")
                yield from normed(r, 0, g, eH[b][:], "x3", eZ[b][:], eSQ[0], lambda: on(dve, r.pe[0], g, "x3T", back=2))

            def messages(g, b, i, r=r):
                f = lambda t: t[0:D, 0:GE]
                v = r.v[1]
                yield r.at["v1 max"]
                on(dve, v, g, "num", back=1)
                v.done(dve.tensor_copy(MX[b][0:D, 0:1], MX[b ^ 1][0:D, GE:GE + 1]), "carry")
                on(dve, r.fl[b], i, "all")
                on(dve, r.act[1], g, "m")
                on(dve, v, g, "carry")
                v.done(scan(MX[b][0:D, 1:GE + 1], FL[b][0:D, :], f(MB), MX[b][0:D, 0:1], ALU.max), "max")
                yield r.at["v1 less"]
                on(dve, v, g, "max")
                v.done(dve.tensor_tensor(f(DEC), MX[b][0:D, 0:GE], MX[b][0:D, 1:GE + 1], ALU.subtract), "less")
                yield r.at["v1 off"]
                v.done(dve.tensor_tensor(f(EX), f(MB), MX[b][0:D, 1:GE + 1], ALU.subtract), "off")
                yield r.at["v1 dec"]
                on(dve, r.act[1], g, "dec")
                v.done(dve.tensor_tensor(f(DEC), f(DEC), FL[b][0:D, :], ALU.mult), "dec")
                yield r.at["v1 q"]
                on(dve, r.act[1], g, "ex")
                v.done(dve.tensor_tensor(f(QQ), f(EX), f(MB), ALU.mult), "q")
                yield r.at["v1 den"]
                on(dve, v, g, "dec")
                on(dve, r.act[3], g, "ln", back=2)
                v.done(scan(f(DEN[b]), f(DEC), f(EX), DEN[b ^ 1][0:D, GE - 1:GE]), "den")
                yield r.at["v1 num"]
                on(dve, v, g, "q")
                on(dve, r.v[3], g, "msg", back=2)
                v.done(scan(f(NUM[b]), f(DEC), f(QQ), NUM[b ^ 1][0:D, GE - 1:GE]), "num")

            def quotients(g, b, i, r=r):
                f = lambda t: t[0:D, 0:GE]
                yield r.at["v3 msg"]
                on(dve, r.act[3], g, "inverse")
                on(dve, r.v[1], g, "num")
                r.v[3].done(dve.tensor_tensor(f(MS[b]), f(MS[b]), f(NUM[b]), ALU.mult), "msg")

            def dst_out(g, b, i, r=r):
                v, m = r.v[2], esm[2]
                yield r.at["v2 sumo"]
                on(dve, r.act[2], g, "sqo")
                v.done(means(m[:, 0, :], eSQ[1]), "sumo")
                yield r.at["v2 out"]
                on(dve, r.act[2], g, "sdo")
                v.done(inverse(m), "ro")
                on(dve, v, g, "ro")
                on(dve, r.sc[b], i, "all", back=1)
                v.done(scale_by(OR[b][:], rows_of(PS[2], P, W), m, P, W), "out")
            staged(dve, (src_x3, 0), (messages, 1), (dst_out, 3), (quotients, 3))




_INS = ["x", "src", "dst", "L0_gnn_weight", "L0_gnn_bias", "L1_gnn_W0", "L1_gnn_b0", "L1_gnn_W1", "L1_gnn_b1",
        "L1_gnn_W2", "L1_gnn_b2", "L2_gnn_W", "L2_gnn_b", "L3_gnn_W", "L3_gnn_b"]


def kernel(**inputs):
    import concourse.bacc as _bacc
    from concourse.bass_utils import run_bass_kernel_spmd as _run

    nc = _bacc.Bacc("TRN2", target_bir_lowering=False, num_devices=1)
    arrays, args = {}, []
    for name in _INS:
        a = np.ascontiguousarray(inputs[name])
        arrays[f"in_{name}"] = a
        args.append(nc.dram_tensor(f"in_{name}", a.shape, mybir.dt.from_np(a.dtype), kind="ExternalInput").ap())
    args.append(nc.dram_tensor("out_x", (N, D), F32, kind="ExternalOutput").ap())
    gnn_program(nc, *args)
    r = _run(nc, [arrays], core_ids=[0])
    return r.results[0]["out_x"]
```
